# Optimizing a Trainium2 kernel written in Bass

```python
import numpy as np
import jax
import jax.numpy as jnp

def _softmax(x, axis=-1):
    return jax.nn.softmax(x, axis=axis)

def _gelu(x):
    return jax.nn.gelu(x, approximate=True)

def _silu(x):
    return jax.nn.silu(x)

def _sigmoid(x):
    return jax.nn.sigmoid(x)

def _layernorm(x, axis=-1, eps=1e-05):
    m = jnp.mean(x, axis=axis, keepdims=True)
    v = jnp.var(x, axis=axis, keepdims=True)
    return (x - m) / jnp.sqrt(v + eps)

def _scatter_add(tgt, idx, src, axis=0):
    return tgt.at[idx].add(src)

def _segment_sum(src, seg, n):
    return jax.ops.segment_sum(src, seg, n)
kernel_name = 'mk_xattn_seq_d4_seqx_r4_e7bea6'

def setup_inputs(seed: int=0):
    np.random.seed(seed)
    _w = jnp.asarray

    def _rec_inputs():
        import jax
        import jax.numpy as jnp
        _rk = jax.random.key(seed)
        x = -0.0002928 + 1 * jax.random.normal(jax.random.fold_in(_rk, 1), (8, 112, 256), jnp.float32)
        _lenS = 112 - jax.random.randint(jax.random.fold_in(_rk, 7), (8,), 0, max(1, 112 // 4) + 1, jnp.int32)
        _lenS2 = 375 - jax.random.randint(jax.random.fold_in(_rk, 8), (8,), 0, max(1, 375 // 4) + 1, jnp.int32)
        _ctx_1024P = jax.random.normal(jax.random.fold_in(_rk, 11), (8, 16, 256), jnp.float32)
        _ctx_1024c = jax.random.dirichlet(jax.random.fold_in(_rk, 511), 0.3 * jnp.ones((16,), jnp.float32), (8, 375))
        _ctx_1024t = jnp.einsum('bsk,bkd->bsd', _ctx_1024c, _ctx_1024P)
        _ctx_1024t = _ctx_1024t * jax.lax.rsqrt(jnp.mean(jnp.square(_ctx_1024t)) + 1e-12) * 0.953939
        ctx_1024 = -1.39393e-06 + 0.999914 * (_ctx_1024t + 0.3 * jax.random.normal(jax.random.fold_in(_rk, 611), (8, 375, 256), jnp.float32))
        return (x, ctx_1024)
    x, ctx_1024 = _rec_inputs()

    def _L0_xattn_setup():
        import jax, jax.numpy as jnp
        import numpy as np
        B, S, SE, D, H, FF, E, K = (2, 512, 512, 256, 16, 1024, 8, 2)
        HD = D // H

        def _layernorm(x, g, b):
            m = x.mean(-1, keepdims=True)
            v = ((x - m) ** 2).mean(-1, keepdims=True)
            return (x - m) / jnp.sqrt(v + 1e-05) * g + b

        def _attn(q_in, k_in, v_in, wq, bq, wk, bk, wv, bv, wo, bo, causal):
            Bq, Sq, Dm = q_in.shape
            Sk = k_in.shape[1]
            Q = (q_in @ wq + bq).reshape(Bq, Sq, H, HD)
            Kp = (k_in @ wk + bk).reshape(Bq, Sk, H, HD)
            V = (v_in @ wv + bv).reshape(Bq, Sk, H, HD)
            scores = jnp.einsum('bqhd,bkhd->bhqk', Q, Kp) / jnp.sqrt(jnp.float32(HD))
            if causal:
                mask = jnp.tril(jnp.ones((Sq, Sk), bool))
                scores = jnp.where(mask, scores, -jnp.inf)
            a = jax.nn.softmax(scores, axis=-1)
            o = jnp.einsum('bhqk,bkhd->bqhd', a, V).reshape(Bq, Sq, Dm)
            return o @ wo + bo

        def _moe(x, rw, rb, w1, b1, w2, b2):
            T = x.shape[0] * x.shape[1]
            xf = x.reshape(T, D)
            router_weights = jax.nn.softmax(xf @ rw + rb, axis=-1)
            topw, topi = jax.lax.top_k(router_weights, K)
            topw = jax.nn.softmax(topw, axis=-1)
            combine = jnp.zeros((T, E), xf.dtype).at[jnp.arange(T)[:, None], topi].add(topw)
            h = jax.nn.gelu(jnp.einsum('td,edf->etf', xf, w1) + b1[:, None, :], approximate=False)
            eo = jnp.einsum('etf,efd->etd', h, w2) + b2[:, None, :]
            out = jnp.einsum('etd,te->td', eo, combine)
            return out.reshape(x.shape)
        key = jax.random.key(seed)
        ks = jax.random.split(key, 32)
        w = lambda k, shape: jax.random.normal(k, shape, jnp.float32) * 0.02
        inp = {'x': jax.random.normal(ks[0], (B, S, D), jnp.float32), 'encoder_output': jax.random.normal(ks[1], (B, SE, D), jnp.float32), 'sa_wq': w(ks[2], (D, D)), 'sa_bq': jnp.zeros((D,), jnp.float32), 'sa_wk': w(ks[3], (D, D)), 'sa_bk': jnp.zeros((D,), jnp.float32), 'sa_wv': w(ks[4], (D, D)), 'sa_bv': jnp.zeros((D,), jnp.float32), 'sa_wo': w(ks[5], (D, D)), 'sa_bo': jnp.zeros((D,), jnp.float32), 'ca_wq': w(ks[6], (D, D)), 'ca_bq': jnp.zeros((D,), jnp.float32), 'ca_wk': w(ks[7], (D, D)), 'ca_bk': jnp.zeros((D,), jnp.float32), 'ca_wv': w(ks[8], (D, D)), 'ca_bv': jnp.zeros((D,), jnp.float32), 'ca_wo': w(ks[9], (D, D)), 'ca_bo': jnp.zeros((D,), jnp.float32), 'ln1_g': jnp.ones((D,), jnp.float32), 'ln1_b': jnp.zeros((D,), jnp.float32), 'ln2_g': jnp.ones((D,), jnp.float32), 'ln2_b': jnp.zeros((D,), jnp.float32), 'ln3_g': jnp.ones((D,), jnp.float32), 'ln3_b': jnp.zeros((D,), jnp.float32), 'router_w': w(ks[10], (D, E)), 'router_b': jnp.zeros((E,), jnp.float32), 'e_w1': w(ks[11], (E, D, FF)), 'e_b1': jnp.zeros((E, FF), jnp.float32), 'e_w2': w(ks[12], (E, FF, D)), 'e_b2': jnp.zeros((E, D), jnp.float32)}
        return inp
    _L0_xattn_all = _L0_xattn_setup()
    _L0_xattn_in = {k: v for k, v in _L0_xattn_all.items() if k in ('sa_wq', 'sa_bq', 'sa_wk', 'sa_bk', 'sa_wv', 'sa_bv', 'sa_wo', 'sa_bo', 'ca_wq', 'ca_bq', 'ca_wk', 'ca_bk', 'ca_wv', 'ca_bv', 'ca_wo', 'ca_bo', 'ln1_g', 'ln1_b', 'ln2_g', 'ln2_b', 'ln3_g', 'ln3_b', 'router_w', 'router_b', 'e_w1', 'e_b1', 'e_w2', 'e_b2')}
    del _L0_xattn_all

    def _L1_xattn_setup():
        import jax, jax.numpy as jnp
        import numpy as np
        B, N, M, D, H = (2, 512, 77, 256, 16)
        DH = D // H
        SCALE = DH ** (-0.5)
        EPS = 1e-05

        def _round_ste(x):
            return x + jax.lax.stop_gradient(jnp.round(x) - x)

        def _fq(x, delta, zp, n_bits):
            xi = _round_ste(x / delta) + zp
            xq = jnp.clip(xi, 0.0, 2.0 ** n_bits - 1.0)
            return (xq - zp) * delta

        def _ln(x, g, b):
            mu = jnp.mean(x, -1, keepdims=True)
            var = jnp.var(x, -1, keepdims=True)
            return (x - mu) * jax.lax.rsqrt(var + EPS) * g + b

        def _attn(x, ctx, wq, wk, wv, wo, bo, dq, dk, dv, dw):
            b, n, _ = x.shape
            m = ctx.shape[1]
            q = (x @ wq).reshape(b, n, H, DH).transpose(0, 2, 1, 3)
            k = (ctx @ wk).reshape(b, m, H, DH).transpose(0, 2, 1, 3)
            v = (ctx @ wv).reshape(b, m, H, DH).transpose(0, 2, 1, 3)
            sim = jnp.einsum('bhid,bhjd->bhij', _fq(q, dq, 128.0, 8), _fq(k, dk, 128.0, 8)) * SCALE
            attn = jax.nn.softmax(sim, axis=-1)
            out = jnp.einsum('bhij,bhjd->bhid', _fq(attn, dw, 0.0, 8), _fq(v, dv, 128.0, 8))
            out = out.transpose(0, 2, 1, 3).reshape(b, n, D)
            return out @ wo + bo
        key = jax.random.key(seed)
        ks = jax.random.split(key, 16)
        w = lambda k, s: jax.random.normal(k, s, jnp.float32) * 0.02
        d = lambda v: jnp.full((1,), v, jnp.float32)
        return {'x': jax.random.normal(ks[0], (B, N, D), jnp.float32), 'context': jax.random.normal(ks[1], (B, M, D), jnp.float32), 'ln1_g': jnp.ones((D,), jnp.float32), 'ln1_b': jnp.zeros((D,), jnp.float32), 'ln2_g': jnp.ones((D,), jnp.float32), 'ln2_b': jnp.zeros((D,), jnp.float32), 'ln3_g': jnp.ones((D,), jnp.float32), 'ln3_b': jnp.zeros((D,), jnp.float32), 'a1_wq': w(ks[2], (D, D)), 'a1_wk': w(ks[3], (D, D)), 'a1_wv': w(ks[4], (D, D)), 'a1_wo': w(ks[5], (D, D)), 'a1_bo': jnp.zeros((D,), jnp.float32), 'a2_wq': w(ks[6], (D, D)), 'a2_wk': w(ks[7], (D, D)), 'a2_wv': w(ks[8], (D, D)), 'a2_wo': w(ks[9], (D, D)), 'a2_bo': jnp.zeros((D,), jnp.float32), 'ff_w1': w(ks[10], (D, 8 * D)), 'ff_b1': jnp.zeros((8 * D,), jnp.float32), 'ff_w2': w(ks[11], (4 * D, D)), 'ff_b2': jnp.zeros((D,), jnp.float32), 'd_q1': d(0.02), 'd_k1': d(0.02), 'd_v1': d(0.02), 'd_w1': d(1.0 / 255.0), 'd_q2': d(0.02), 'd_k2': d(0.02), 'd_v2': d(0.02), 'd_w2': d(1.0 / 255.0)}
    _L1_xattn_all = _L1_xattn_setup()
    _L1_xattn_in = {k: v for k, v in _L1_xattn_all.items() if k in ('ln1_g', 'ln1_b', 'ln2_g', 'ln2_b', 'ln3_g', 'ln3_b', 'a1_wq', 'a1_wk', 'a1_wv', 'a1_wo', 'a1_bo', 'a2_wq', 'a2_wk', 'a2_wv', 'a2_wo', 'a2_bo', 'ff_w1', 'ff_b1', 'ff_w2', 'ff_b2', 'd_q1', 'd_k1', 'd_v1', 'd_w1', 'd_q2', 'd_k2', 'd_v2', 'd_w2')}
    del _L1_xattn_all

    def _L2_xattn_setup():
        import jax, jax.numpy as jnp
        import numpy as np
        B, T, E = (4, 512, 256)
        H, HS = (16, 64)
        EPS = 1e-05

        def _layernorm(x, g, b):
            mu = jnp.mean(x, axis=-1, keepdims=True)
            var = jnp.mean(jnp.square(x - mu), axis=-1, keepdims=True)
            return (x - mu) * jax.lax.rsqrt(var + EPS) * g + b
        key = jax.random.key(seed)
        ks = jax.random.split(key, 8)
        q = jax.random.normal(ks[0], (B, T, E), dtype=jnp.float32)
        s_in = 1.0 / np.sqrt(E)
        s_o = 1.0 / np.sqrt(H * HS)
        return {'q': q, 'kv': q, 'ln_g': jnp.ones((E,), jnp.float32), 'ln_b': jnp.zeros((E,), jnp.float32), 'wq': jax.random.uniform(ks[1], (E, H * HS), jnp.float32, -s_in, s_in), 'bq': jax.random.uniform(ks[2], (H * HS,), jnp.float32, -s_in, s_in), 'wkv': jax.random.uniform(ks[3], (E, 2 * H * HS), jnp.float32, -s_in, s_in), 'bkv': jax.random.uniform(ks[4], (2 * H * HS,), jnp.float32, -s_in, s_in), 'wo': jax.random.uniform(ks[5], (H * HS, E), jnp.float32, -s_o, s_o), 'bo': jax.random.uniform(ks[6], (E,), jnp.float32, -s_o, s_o)}
    _L2_xattn_all = _L2_xattn_setup()
    _L2_xattn_in = {k: v for k, v in _L2_xattn_all.items() if k in ('ln_g', 'ln_b', 'wq', 'bq', 'wkv', 'bkv', 'wo', 'bo')}
    del _L2_xattn_all

    def _L3_xattn_setup():
        import jax, jax.numpy as jnp
        import numpy as np
        B, S, E, H, T, R = (8, 256, 256, 16, 196, 4)
        HD = E // H
        EPS = 1e-05

        def _ln(x, g, b):
            mu = jnp.mean(x, axis=-1, keepdims=True)
            var = jnp.mean(jnp.square(x - mu), axis=-1, keepdims=True)
            return (x - mu) * jax.lax.rsqrt(var + EPS) * g + b

        def _lin(x, w, b):
            return jnp.einsum('bse,oe->bso', x, w) + b

        def _heads(t):
            b, s, _ = t.shape
            return t.reshape(b, s, H, HD).transpose(0, 2, 1, 3)

        def _attend(q, k, v, causal):
            scale = HD ** (-0.5)
            scores = jnp.einsum('bhqd,bhkd->bhqk', q, k) * scale
            if causal:
                sq, sk = (scores.shape[-2], scores.shape[-1])
                mask = jnp.tril(jnp.ones((sq, sk), bool))
                scores = jnp.where(mask, scores, -jnp.inf)
            w = jax.nn.softmax(scores, axis=-1)
            out = jnp.einsum('bhqk,bhkd->bhqd', w, v)
            b, h, s, d = out.shape
            return out.transpose(0, 2, 1, 3).reshape(b, s, h * d)
        key = jax.random.key(seed)
        ks = jax.random.split(key, 12)
        w = lambda k, shape: jax.random.normal(k, shape, jnp.float32) * 0.02
        return {'x': jax.random.normal(ks[0], (B, S, E), jnp.float32), 'enc_out': jax.random.normal(ks[1], (B, T, E), jnp.float32), 'ln1_g': jnp.ones(E), 'ln1_b': jnp.zeros(E), 'attn_qkv_w': w(ks[2], (3 * E, E)), 'attn_qkv_b': jnp.zeros(3 * E), 'attn_proj_w': w(ks[3], (E, E)), 'attn_proj_b': jnp.zeros(E), 'ln2_g': jnp.ones(E), 'ln2_b': jnp.zeros(E), 'q_w': w(ks[4], (E, E)), 'q_b': jnp.zeros(E), 'k_w': w(ks[5], (E, E)), 'k_b': jnp.zeros(E), 'v_w': w(ks[6], (E, E)), 'v_b': jnp.zeros(E), 'ca_proj_w': w(ks[7], (E, E)), 'ca_proj_b': jnp.zeros(E), 'ln3_g': jnp.ones(E), 'ln3_b': jnp.zeros(E), 'fc_w': w(ks[8], (R * E, E)), 'fc_b': jnp.zeros(R * E), 'proj_w': w(ks[9], (E, R * E)), 'proj_b': jnp.zeros(E)}
    _L3_xattn_all = _L3_xattn_setup()
    _L3_xattn_in = {k: v for k, v in _L3_xattn_all.items() if k in ('ln1_g', 'ln1_b', 'attn_qkv_w', 'attn_qkv_b', 'attn_proj_w', 'attn_proj_b', 'ln2_g', 'ln2_b', 'q_w', 'q_b', 'k_w', 'k_b', 'v_w', 'v_b', 'ca_proj_w', 'ca_proj_b', 'ln3_g', 'ln3_b', 'fc_w', 'fc_b', 'proj_w', 'proj_b')}
    del _L3_xattn_all
    return {'x': x, 'ctx_1024': ctx_1024, 'L0_xattn_sa_wq': _L0_xattn_in['sa_wq'], 'L0_xattn_sa_bq': _L0_xattn_in['sa_bq'], 'L0_xattn_sa_wk': _L0_xattn_in['sa_wk'], 'L0_xattn_sa_bk': _L0_xattn_in['sa_bk'], 'L0_xattn_sa_wv': _L0_xattn_in['sa_wv'], 'L0_xattn_sa_bv': _L0_xattn_in['sa_bv'], 'L0_xattn_sa_wo': _L0_xattn_in['sa_wo'], 'L0_xattn_sa_bo': _L0_xattn_in['sa_bo'], 'L0_xattn_ca_wq': _L0_xattn_in['ca_wq'], 'L0_xattn_ca_bq': _L0_xattn_in['ca_bq'], 'L0_xattn_ca_wk': _L0_xattn_in['ca_wk'], 'L0_xattn_ca_bk': _L0_xattn_in['ca_bk'], 'L0_xattn_ca_wv': _L0_xattn_in['ca_wv'], 'L0_xattn_ca_bv': _L0_xattn_in['ca_bv'], 'L0_xattn_ca_wo': _L0_xattn_in['ca_wo'], 'L0_xattn_ca_bo': _L0_xattn_in['ca_bo'], 'L0_xattn_ln1_g': _L0_xattn_in['ln1_g'], 'L0_xattn_ln1_b': _L0_xattn_in['ln1_b'], 'L0_xattn_ln2_g': _L0_xattn_in['ln2_g'], 'L0_xattn_ln2_b': _L0_xattn_in['ln2_b'], 'L0_xattn_ln3_g': _L0_xattn_in['ln3_g'], 'L0_xattn_ln3_b': _L0_xattn_in['ln3_b'], 'L0_xattn_router_w': _L0_xattn_in['router_w'], 'L0_xattn_router_b': _L0_xattn_in['router_b'], 'L0_xattn_e_w1': _L0_xattn_in['e_w1'], 'L0_xattn_e_b1': _L0_xattn_in['e_b1'], 'L0_xattn_e_w2': _L0_xattn_in['e_w2'], 'L0_xattn_e_b2': _L0_xattn_in['e_b2'], 'L1_xattn_ln1_g': _L1_xattn_in['ln1_g'], 'L1_xattn_ln1_b': _L1_xattn_in['ln1_b'], 'L1_xattn_ln2_g': _L1_xattn_in['ln2_g'], 'L1_xattn_ln2_b': _L1_xattn_in['ln2_b'], 'L1_xattn_ln3_g': _L1_xattn_in['ln3_g'], 'L1_xattn_ln3_b': _L1_xattn_in['ln3_b'], 'L1_xattn_a1_wq': _L1_xattn_in['a1_wq'], 'L1_xattn_a1_wk': _L1_xattn_in['a1_wk'], 'L1_xattn_a1_wv': _L1_xattn_in['a1_wv'], 'L1_xattn_a1_wo': _L1_xattn_in['a1_wo'], 'L1_xattn_a1_bo': _L1_xattn_in['a1_bo'], 'L1_xattn_a2_wq': _L1_xattn_in['a2_wq'], 'L1_xattn_a2_wk': _L1_xattn_in['a2_wk'], 'L1_xattn_a2_wv': _L1_xattn_in['a2_wv'], 'L1_xattn_a2_wo': _L1_xattn_in['a2_wo'], 'L1_xattn_a2_bo': _L1_xattn_in['a2_bo'], 'L1_xattn_ff_w1': _L1_xattn_in['ff_w1'], 'L1_xattn_ff_b1': _L1_xattn_in['ff_b1'], 'L1_xattn_ff_w2': _L1_xattn_in['ff_w2'], 'L1_xattn_ff_b2': _L1_xattn_in['ff_b2'], 'L1_xattn_d_q1': _L1_xattn_in['d_q1'], 'L1_xattn_d_k1': _L1_xattn_in['d_k1'], 'L1_xattn_d_v1': _L1_xattn_in['d_v1'], 'L1_xattn_d_w1': _L1_xattn_in['d_w1'], 'L1_xattn_d_q2': _L1_xattn_in['d_q2'], 'L1_xattn_d_k2': _L1_xattn_in['d_k2'], 'L1_xattn_d_v2': _L1_xattn_in['d_v2'], 'L1_xattn_d_w2': _L1_xattn_in['d_w2'], 'L2_xattn_ln_g': _L2_xattn_in['ln_g'], 'L2_xattn_ln_b': _L2_xattn_in['ln_b'], 'L2_xattn_wq': _L2_xattn_in['wq'], 'L2_xattn_bq': _L2_xattn_in['bq'], 'L2_xattn_wkv': _L2_xattn_in['wkv'], 'L2_xattn_bkv': _L2_xattn_in['bkv'], 'L2_xattn_wo': _L2_xattn_in['wo'], 'L2_xattn_bo': _L2_xattn_in['bo'], 'L3_xattn_ln1_g': _L3_xattn_in['ln1_g'], 'L3_xattn_ln1_b': _L3_xattn_in['ln1_b'], 'L3_xattn_attn_qkv_w': _L3_xattn_in['attn_qkv_w'], 'L3_xattn_attn_qkv_b': _L3_xattn_in['attn_qkv_b'], 'L3_xattn_attn_proj_w': _L3_xattn_in['attn_proj_w'], 'L3_xattn_attn_proj_b': _L3_xattn_in['attn_proj_b'], 'L3_xattn_ln2_g': _L3_xattn_in['ln2_g'], 'L3_xattn_ln2_b': _L3_xattn_in['ln2_b'], 'L3_xattn_q_w': _L3_xattn_in['q_w'], 'L3_xattn_q_b': _L3_xattn_in['q_b'], 'L3_xattn_k_w': _L3_xattn_in['k_w'], 'L3_xattn_k_b': _L3_xattn_in['k_b'], 'L3_xattn_v_w': _L3_xattn_in['v_w'], 'L3_xattn_v_b': _L3_xattn_in['v_b'], 'L3_xattn_ca_proj_w': _L3_xattn_in['ca_proj_w'], 'L3_xattn_ca_proj_b': _L3_xattn_in['ca_proj_b'], 'L3_xattn_ln3_g': _L3_xattn_in['ln3_g'], 'L3_xattn_ln3_b': _L3_xattn_in['ln3_b'], 'L3_xattn_fc_w': _L3_xattn_in['fc_w'], 'L3_xattn_fc_b': _L3_xattn_in['fc_b'], 'L3_xattn_proj_w': _L3_xattn_in['proj_w'], 'L3_xattn_proj_b': _L3_xattn_in['proj_b']}

def reference(x, ctx_1024, L0_xattn_sa_wq, L0_xattn_sa_bq, L0_xattn_sa_wk, L0_xattn_sa_bk, L0_xattn_sa_wv, L0_xattn_sa_bv, L0_xattn_sa_wo, L0_xattn_sa_bo, L0_xattn_ca_wq, L0_xattn_ca_bq, L0_xattn_ca_wk, L0_xattn_ca_bk, L0_xattn_ca_wv, L0_xattn_ca_bv, L0_xattn_ca_wo, L0_xattn_ca_bo, L0_xattn_ln1_g, L0_xattn_ln1_b, L0_xattn_ln2_g, L0_xattn_ln2_b, L0_xattn_ln3_g, L0_xattn_ln3_b, L0_xattn_router_w, L0_xattn_router_b, L0_xattn_e_w1, L0_xattn_e_b1, L0_xattn_e_w2, L0_xattn_e_b2, L1_xattn_ln1_g, L1_xattn_ln1_b, L1_xattn_ln2_g, L1_xattn_ln2_b, L1_xattn_ln3_g, L1_xattn_ln3_b, L1_xattn_a1_wq, L1_xattn_a1_wk, L1_xattn_a1_wv, L1_xattn_a1_wo, L1_xattn_a1_bo, L1_xattn_a2_wq, L1_xattn_a2_wk, L1_xattn_a2_wv, L1_xattn_a2_wo, L1_xattn_a2_bo, L1_xattn_ff_w1, L1_xattn_ff_b1, L1_xattn_ff_w2, L1_xattn_ff_b2, L1_xattn_d_q1, L1_xattn_d_k1, L1_xattn_d_v1, L1_xattn_d_w1, L1_xattn_d_q2, L1_xattn_d_k2, L1_xattn_d_v2, L1_xattn_d_w2, L2_xattn_ln_g, L2_xattn_ln_b, L2_xattn_wq, L2_xattn_bq, L2_xattn_wkv, L2_xattn_bkv, L2_xattn_wo, L2_xattn_bo, L3_xattn_ln1_g, L3_xattn_ln1_b, L3_xattn_attn_qkv_w, L3_xattn_attn_qkv_b, L3_xattn_attn_proj_w, L3_xattn_attn_proj_b, L3_xattn_ln2_g, L3_xattn_ln2_b, L3_xattn_q_w, L3_xattn_q_b, L3_xattn_k_w, L3_xattn_k_b, L3_xattn_v_w, L3_xattn_v_b, L3_xattn_ca_proj_w, L3_xattn_ca_proj_b, L3_xattn_ln3_g, L3_xattn_ln3_b, L3_xattn_fc_w, L3_xattn_fc_b, L3_xattn_proj_w, L3_xattn_proj_b):
    import jax
    import jax.numpy as jnp

    def _L0_xattn_ref(x, encoder_output, sa_wq, sa_bq, sa_wk, sa_bk, sa_wv, sa_bv, sa_wo, sa_bo, ca_wq, ca_bq, ca_wk, ca_bk, ca_wv, ca_bv, ca_wo, ca_bo, ln1_g, ln1_b, ln2_g, ln2_b, ln3_g, ln3_b, router_w, router_b, e_w1, e_b1, e_w2, e_b2):
        import jax, jax.numpy as jnp
        import numpy as np
        B, S, SE, D, H, FF, E, K = (2, 512, 512, 256, 16, 1024, 8, 2)
        HD = D // H

        def _layernorm(x, g, b):
            m = x.mean(-1, keepdims=True)
            v = ((x - m) ** 2).mean(-1, keepdims=True)
            return (x - m) / jnp.sqrt(v + 1e-05) * g + b

        def _attn(q_in, k_in, v_in, wq, bq, wk, bk, wv, bv, wo, bo, causal):
            Bq, Sq, Dm = q_in.shape
            Sk = k_in.shape[1]
            Q = (q_in @ wq + bq).reshape(Bq, Sq, H, HD)
            Kp = (k_in @ wk + bk).reshape(Bq, Sk, H, HD)
            V = (v_in @ wv + bv).reshape(Bq, Sk, H, HD)
            scores = jnp.einsum('bqhd,bkhd->bhqk', Q, Kp) / jnp.sqrt(jnp.float32(HD))
            if causal:
                mask = jnp.tril(jnp.ones((Sq, Sk), bool))
                scores = jnp.where(mask, scores, -jnp.inf)
            a = jax.nn.softmax(scores, axis=-1)
            o = jnp.einsum('bhqk,bkhd->bqhd', a, V).reshape(Bq, Sq, Dm)
            return o @ wo + bo

        def _moe(x, rw, rb, w1, b1, w2, b2):
            T = x.shape[0] * x.shape[1]
            xf = x.reshape(T, D)
            router_weights = jax.nn.softmax(xf @ rw + rb, axis=-1)
            topw, topi = jax.lax.top_k(router_weights, K)
            topw = jax.nn.softmax(topw, axis=-1)
            combine = jnp.zeros((T, E), xf.dtype).at[jnp.arange(T)[:, None], topi].add(topw)
            h = jax.nn.gelu(jnp.einsum('td,edf->etf', xf, w1) + b1[:, None, :], approximate=False)
            eo = jnp.einsum('etf,efd->etd', h, w2) + b2[:, None, :]
            out = jnp.einsum('etd,te->td', eo, combine)
            return out.reshape(x.shape)
        x = _layernorm(x + _attn(x, x, x, sa_wq, sa_bq, sa_wk, sa_bk, sa_wv, sa_bv, sa_wo, sa_bo, True), ln1_g, ln1_b)
        x = _layernorm(x + _attn(x, encoder_output, encoder_output, ca_wq, ca_bq, ca_wk, ca_bk, ca_wv, ca_bv, ca_wo, ca_bo, False), ln2_g, ln2_b)
        x = _layernorm(x + _moe(x, router_w, router_b, e_w1, e_b1, e_w2, e_b2), ln3_g, ln3_b)
        return x

    def _L1_xattn_ref(x, context, ln1_g, ln1_b, ln2_g, ln2_b, ln3_g, ln3_b, a1_wq, a1_wk, a1_wv, a1_wo, a1_bo, a2_wq, a2_wk, a2_wv, a2_wo, a2_bo, ff_w1, ff_b1, ff_w2, ff_b2, d_q1, d_k1, d_v1, d_w1, d_q2, d_k2, d_v2, d_w2):
        import jax, jax.numpy as jnp
        import numpy as np
        B, N, M, D, H = (2, 512, 77, 256, 16)
        DH = D // H
        SCALE = DH ** (-0.5)
        EPS = 1e-05

        def _round_ste(x):
            return x + jax.lax.stop_gradient(jnp.round(x) - x)

        def _fq(x, delta, zp, n_bits):
            xi = _round_ste(x / delta) + zp
            xq = jnp.clip(xi, 0.0, 2.0 ** n_bits - 1.0)
            return (xq - zp) * delta

        def _ln(x, g, b):
            mu = jnp.mean(x, -1, keepdims=True)
            var = jnp.var(x, -1, keepdims=True)
            return (x - mu) * jax.lax.rsqrt(var + EPS) * g + b

        def _attn(x, ctx, wq, wk, wv, wo, bo, dq, dk, dv, dw):
            b, n, _ = x.shape
            m = ctx.shape[1]
            q = (x @ wq).reshape(b, n, H, DH).transpose(0, 2, 1, 3)
            k = (ctx @ wk).reshape(b, m, H, DH).transpose(0, 2, 1, 3)
            v = (ctx @ wv).reshape(b, m, H, DH).transpose(0, 2, 1, 3)
            sim = jnp.einsum('bhid,bhjd->bhij', _fq(q, dq, 128.0, 8), _fq(k, dk, 128.0, 8)) * SCALE
            attn = jax.nn.softmax(sim, axis=-1)
            out = jnp.einsum('bhij,bhjd->bhid', _fq(attn, dw, 0.0, 8), _fq(v, dv, 128.0, 8))
            out = out.transpose(0, 2, 1, 3).reshape(b, n, D)
            return out @ wo + bo
        h1 = _ln(x, ln1_g, ln1_b)
        x = _attn(h1, h1, a1_wq, a1_wk, a1_wv, a1_wo, a1_bo, d_q1, d_k1, d_v1, d_w1) + x
        h2 = _ln(x, ln2_g, ln2_b)
        x = _attn(h2, context, a2_wq, a2_wk, a2_wv, a2_wo, a2_bo, d_q2, d_k2, d_v2, d_w2) + x
        h3 = _ln(x, ln3_g, ln3_b)
        hg = h3 @ ff_w1 + ff_b1
        a, g = jnp.split(hg, 2, axis=-1)
        x = a * jax.nn.gelu(g, approximate=False) @ ff_w2 + ff_b2 + x
        return x

    def _L2_xattn_ref(q, kv, ln_g, ln_b, wq, bq, wkv, bkv, wo, bo):
        import jax, jax.numpy as jnp
        import numpy as np
        B, T, E = (4, 512, 256)
        H, HS = (16, 64)
        EPS = 1e-05

        def _layernorm(x, g, b):
            mu = jnp.mean(x, axis=-1, keepdims=True)
            var = jnp.mean(jnp.square(x - mu), axis=-1, keepdims=True)
            return (x - mu) * jax.lax.rsqrt(var + EPS) * g + b
        oq = q
        qn = _layernorm(q, ln_g, ln_b)
        kvn = _layernorm(kv, ln_g, ln_b)
        b, qT, _ = q.shape
        kvT = kv.shape[1]
        qp = (qn @ wq + bq).reshape(b, qT, H, HS).transpose(0, 2, 1, 3)
        kvp = kvn @ wkv + bkv
        kp, vp = jnp.split(kvp, 2, axis=-1)
        kp = kp.reshape(b, kvT, H, HS).transpose(0, 2, 1, 3)
        vp = vp.reshape(b, kvT, H, HS).transpose(0, 2, 1, 3)
        attn = jnp.einsum('bhqd,bhkd->bhqk', qp, kp) / jnp.sqrt(jnp.float32(HS))
        causal = jnp.tril(jnp.ones((qT, kvT), dtype=bool))
        attn = jnp.where(causal, attn, -jnp.inf)
        attn = jax.nn.softmax(attn, axis=-1)
        ctx = jnp.einsum('bhqk,bhkd->bhqd', attn, vp)
        ctx = ctx.transpose(0, 2, 1, 3).reshape(b, qT, H * HS)
        out = ctx @ wo + bo + oq
        return out

    def _L3_xattn_ref(x, enc_out, ln1_g, ln1_b, attn_qkv_w, attn_qkv_b, attn_proj_w, attn_proj_b, ln2_g, ln2_b, q_w, q_b, k_w, k_b, v_w, v_b, ca_proj_w, ca_proj_b, ln3_g, ln3_b, fc_w, fc_b, proj_w, proj_b):
        import jax, jax.numpy as jnp
        import numpy as np
        B, S, E, H, T, R = (8, 256, 256, 16, 196, 4)
        HD = E // H
        EPS = 1e-05

        def _ln(x, g, b):
            mu = jnp.mean(x, axis=-1, keepdims=True)
            var = jnp.mean(jnp.square(x - mu), axis=-1, keepdims=True)
            return (x - mu) * jax.lax.rsqrt(var + EPS) * g + b

        def _lin(x, w, b):
            return jnp.einsum('bse,oe->bso', x, w) + b

        def _heads(t):
            b, s, _ = t.shape
            return t.reshape(b, s, H, HD).transpose(0, 2, 1, 3)

        def _attend(q, k, v, causal):
            scale = HD ** (-0.5)
            scores = jnp.einsum('bhqd,bhkd->bhqk', q, k) * scale
            if causal:
                sq, sk = (scores.shape[-2], scores.shape[-1])
                mask = jnp.tril(jnp.ones((sq, sk), bool))
                scores = jnp.where(mask, scores, -jnp.inf)
            w = jax.nn.softmax(scores, axis=-1)
            out = jnp.einsum('bhqk,bhkd->bhqd', w, v)
            b, h, s, d = out.shape
            return out.transpose(0, 2, 1, 3).reshape(b, s, h * d)
        h = _ln(x, ln1_g, ln1_b)
        qkv = _lin(h, attn_qkv_w, attn_qkv_b)
        q, k, v = jnp.split(qkv, 3, axis=-1)
        a = _attend(_heads(q), _heads(k), _heads(v), causal=True)
        x = x + _lin(a, attn_proj_w, attn_proj_b)
        h = _ln(x, ln2_g, ln2_b)
        q = _heads(_lin(h, q_w, q_b))
        k = _heads(_lin(enc_out, k_w, k_b))
        v = _heads(_lin(enc_out, v_w, v_b))
        a = _attend(q, k, v, causal=False)
        x = x + _lin(a, ca_proj_w, ca_proj_b)
        h = _ln(x, ln3_g, ln3_b)
        h = jax.nn.gelu(_lin(h, fc_w, fc_b), approximate=False)
        x = x + _lin(h, proj_w, proj_b)
        return x
    x = _L0_xattn_ref(x, ctx_1024, L0_xattn_sa_wq, L0_xattn_sa_bq, L0_xattn_sa_wk, L0_xattn_sa_bk, L0_xattn_sa_wv, L0_xattn_sa_bv, L0_xattn_sa_wo, L0_xattn_sa_bo, L0_xattn_ca_wq, L0_xattn_ca_bq, L0_xattn_ca_wk, L0_xattn_ca_bk, L0_xattn_ca_wv, L0_xattn_ca_bv, L0_xattn_ca_wo, L0_xattn_ca_bo, L0_xattn_ln1_g, L0_xattn_ln1_b, L0_xattn_ln2_g, L0_xattn_ln2_b, L0_xattn_ln3_g, L0_xattn_ln3_b, L0_xattn_router_w, L0_xattn_router_b, L0_xattn_e_w1, L0_xattn_e_b1, L0_xattn_e_w2, L0_xattn_e_b2)
    x = _L1_xattn_ref(x, ctx_1024, L1_xattn_ln1_g, L1_xattn_ln1_b, L1_xattn_ln2_g, L1_xattn_ln2_b, L1_xattn_ln3_g, L1_xattn_ln3_b, L1_xattn_a1_wq, L1_xattn_a1_wk, L1_xattn_a1_wv, L1_xattn_a1_wo, L1_xattn_a1_bo, L1_xattn_a2_wq, L1_xattn_a2_wk, L1_xattn_a2_wv, L1_xattn_a2_wo, L1_xattn_a2_bo, L1_xattn_ff_w1, L1_xattn_ff_b1, L1_xattn_ff_w2, L1_xattn_ff_b2, L1_xattn_d_q1, L1_xattn_d_k1, L1_xattn_d_v1, L1_xattn_d_w1, L1_xattn_d_q2, L1_xattn_d_k2, L1_xattn_d_v2, L1_xattn_d_w2)
    x = _L2_xattn_ref(x, ctx_1024, L2_xattn_ln_g, L2_xattn_ln_b, L2_xattn_wq, L2_xattn_bq, L2_xattn_wkv, L2_xattn_bkv, L2_xattn_wo, L2_xattn_bo)
    x = _L3_xattn_ref(x, ctx_1024, L3_xattn_ln1_g, L3_xattn_ln1_b, L3_xattn_attn_qkv_w, L3_xattn_attn_qkv_b, L3_xattn_attn_proj_w, L3_xattn_attn_proj_b, L3_xattn_ln2_g, L3_xattn_ln2_b, L3_xattn_q_w, L3_xattn_q_b, L3_xattn_k_w, L3_xattn_k_b, L3_xattn_v_w, L3_xattn_v_b, L3_xattn_ca_proj_w, L3_xattn_ca_proj_b, L3_xattn_ln3_g, L3_xattn_ln3_b, L3_xattn_fc_w, L3_xattn_fc_b, L3_xattn_proj_w, L3_xattn_proj_b)
    return x

_drawn_inputs = setup_inputs


def setup_inputs(seed=0):
    import zlib

    import numpy as np

    out = dict(_drawn_inputs(seed))
    spreads = {'L0_xattn_sa_bq': (0.0, 0.8),
     'L0_xattn_sa_bk': (0.0, 2.0),
     'L0_xattn_sa_bv': (0.0, 0.1),
     'L0_xattn_sa_bo': (0.0, 0.1),
     'L0_xattn_ca_bq': (0.0, 0.8),
     'L0_xattn_ca_bk': (0.0, 2.0),
     'L0_xattn_ca_bv': (0.0, 0.1),
     'L0_xattn_ca_bo': (0.0, 0.1),
     'L0_xattn_ln1_g': (1.0, 0.2),
     'L0_xattn_ln1_b': (0.0, 0.1),
     'L0_xattn_ln2_g': (1.0, 0.2),
     'L0_xattn_ln2_b': (0.0, 0.1),
     'L0_xattn_ln3_g': (1.0, 0.2),
     'L0_xattn_ln3_b': (0.0, 0.1),
     'L0_xattn_router_b': (0.0, 0.1),
     'L0_xattn_e_b1': (0.0, 0.356),
     'L0_xattn_e_b2': (0.0, 0.1),
     'L1_xattn_ln1_g': (1.0, 0.6),
     'L1_xattn_ln1_b': (0.0, 0.8),
     'L1_xattn_ln2_g': (1.0, 0.6),
     'L1_xattn_ln2_b': (0.0, 0.8),
     'L1_xattn_ln3_g': (1.0, 0.6),
     'L1_xattn_ln3_b': (0.0, 0.8),
     'L1_xattn_a1_bo': (0.0, 0.1),
     'L1_xattn_a2_bo': (0.0, 0.1),
     'L1_xattn_ff_b1': (0.0, 0.532),
     'L1_xattn_ff_b2': (0.0, 0.1),
     'L2_xattn_ln_g': (1.0, 0.2),
     'L2_xattn_ln_b': (0.0, 0.277),
     'L3_xattn_ln1_g': (1.0, 0.6),
     'L3_xattn_ln1_b': (0.0, 0.8),
     'L3_xattn_attn_qkv_b': (0.0, 0.271),
     'L3_xattn_attn_proj_b': (0.0, 0.1),
     'L3_xattn_ln2_g': (1.0, 0.6),
     'L3_xattn_ln2_b': (0.0, 0.8),
     'L3_xattn_q_b': (0.0, 0.8),
     'L3_xattn_k_b': (0.0, 2.0),
     'L3_xattn_v_b': (0.0, 0.279),
     'L3_xattn_ca_proj_b': (0.0, 0.1),
     'L3_xattn_ln3_g': (1.0, 0.6),
     'L3_xattn_ln3_b': (0.0, 0.713),
     'L3_xattn_fc_b': (0.0, 0.1),
     'L3_xattn_proj_b': (0.0, 0.1)}
    factors = {'L0_xattn_sa_wq': 8.0,
     'L0_xattn_sa_wk': 8.0,
     'L0_xattn_ca_wq': 8.0,
     'L0_xattn_ca_wk': 8.0,
     'L1_xattn_a1_wq': 8.0,
     'L1_xattn_a1_wk': 8.0,
     'L1_xattn_a1_wo': 2.897,
     'L1_xattn_a2_wq': 8.0,
     'L1_xattn_a2_wk': 8.0,
     'L2_xattn_bq': 38.902,
     'L2_xattn_bkv': 3.143,
     'L2_xattn_bo': 3.418,
     'L3_xattn_q_w': 8.0,
     'L3_xattn_k_w': 8.0}
    for name, (base, spread) in spreads.items():
        noise = np.random.default_rng([zlib.crc32(name.encode()), seed]).standard_normal(out[name].shape)
        drawn = base * np.exp(spread * noise) if base else spread * noise
        out[name] = jnp.asarray(drawn.astype(out[name].dtype))
    for name, factor in factors.items():
        out[name] = (out[name] * factor).astype(out[name].dtype)
    return out
```

```python
from contextlib import ExitStack

import concourse.bass as bass
from concourse import mybir

F32 = mybir.dt.float32
BF16 = mybir.dt.bfloat16
U32 = mybir.dt.uint32
ALU = mybir.AluOpType
ACT = mybir.ActivationFunctionType
AX = mybir.AxisListType

B, T, D, M = 8, 112, 256, 375
H = 16
HD, HD2 = D // H, 64
KT = D // 128
C, MC = 3, M // 3
E, FF = 8, 1024
FT = FF // 128
G = 2
GT = G * T
TURNS = B // G
MAGIC = 1.5 * 2.0 ** 23
EPS = 1e-5

COLS = {}
for _name, _n in [
    ("L0_xattn_sa_bq", 2), ("L0_xattn_sa_bk", 2), ("L0_xattn_sa_bv", 2),
    ("L0_xattn_ca_bq", 2), ("L0_xattn_ca_bk", 2), ("L0_xattn_ca_bv", 2),
    ("L1_xattn_ln1_g", 2), ("L1_xattn_ln1_b", 2), ("L1_xattn_ln2_g", 2), ("L1_xattn_ln2_b", 2),
    ("L1_xattn_ln3_g", 2), ("L1_xattn_ln3_b", 2), ("L1_xattn_ff_b1", 16),
    ("L2_xattn_ln_g", 2), ("L2_xattn_ln_b", 2), ("L2_xattn_bq", 8), ("L2_xattn_bkv", 16),
    ("L3_xattn_ln1_g", 2), ("L3_xattn_ln1_b", 2), ("L3_xattn_attn_qkv_b", 6),
    ("L3_xattn_ln2_g", 2), ("L3_xattn_ln2_b", 2), ("L3_xattn_q_b", 2), ("L3_xattn_k_b", 2), ("L3_xattn_v_b", 2),
    ("L3_xattn_ln3_g", 2), ("L3_xattn_ln3_b", 2), ("L3_xattn_fc_b", 8),
    ("L1_xattn_d_q1", 1), ("L1_xattn_d_k1", 1), ("L1_xattn_d_v1", 1), ("L1_xattn_d_w1", 1),
    ("L1_xattn_d_q2", 1), ("L1_xattn_d_k2", 1), ("L1_xattn_d_v2", 1), ("L1_xattn_d_w2", 1),
    ("head_masks", 4),
]:
    COLS[_name] = (sum(n for _, n in COLS.values()), _n)
NCOL = sum(n for _, n in COLS.values())
ROWS = {name: i for i, name in enumerate([
    "L0_xattn_sa_bo", "L0_xattn_ca_bo", "L0_xattn_ln1_g", "L0_xattn_ln1_b", "L0_xattn_ln2_g", "L0_xattn_ln2_b",
    "L0_xattn_ln3_g", "L0_xattn_ln3_b", "L1_xattn_a1_bo", "L1_xattn_a2_bo", "L1_xattn_ff_b2", "L2_xattn_bo",
    "L3_xattn_attn_proj_b", "L3_xattn_ca_proj_b", "L3_xattn_proj_b"])}
NROW = len(ROWS)
WEIGHTS = {
    "L0_xattn_sa_wq": (D, D, False), "L0_xattn_sa_wk": (D, D, False), "L0_xattn_sa_wv": (D, D, False),
    "L0_xattn_sa_wo": (D, D, False), "L0_xattn_ca_wq": (D, D, False), "L0_xattn_ca_wk": (D, D, False),
    "L0_xattn_ca_wv": (D, D, False), "L0_xattn_ca_wo": (D, D, False), "L0_xattn_router_w": (D, E, False),
    "L1_xattn_a1_wq": (D, D, False), "L1_xattn_a1_wk": (D, D, False), "L1_xattn_a1_wv": (D, D, False),
    "L1_xattn_a1_wo": (D, D, False), "L1_xattn_a2_wq": (D, D, False), "L1_xattn_a2_wk": (D, D, False),
    "L1_xattn_a2_wv": (D, D, False), "L1_xattn_a2_wo": (D, D, False), "L1_xattn_ff_w1": (D, 2 * FF, False),
    "L1_xattn_ff_w2": (FF, D, False), "L2_xattn_wq": (D, H * HD2, False), "L2_xattn_wkv": (D, 2 * H * HD2, False),
    "L2_xattn_wo": (H * HD2, D, False), "L3_xattn_attn_qkv_w": (D, 3 * D, True), "L3_xattn_attn_proj_w": (D, D, True),
    "L3_xattn_q_w": (D, D, True), "L3_xattn_k_w": (D, D, True), "L3_xattn_v_w": (D, D, True),
    "L3_xattn_ca_proj_w": (D, D, True), "L3_xattn_fc_w": (D, FF, True), "L3_xattn_proj_w": (FF, D, True)}


class Layer:

    def __init__(self, name, kind, pre=None, post=None, row=None, quant=None, causal=False, cross=False, **w):
        self.name, self.kind, self.pre, self.post, self.row = name, kind, pre, post, row
        self.quant, self.causal, self.cross, self.w = quant, causal, cross, w
        self.wide = kind == "attn64"
        if kind == "attn64":
            self.groups = [[8 * half + 2 * i + par for i in range(4)] for half in range(2) for par in range(2)]
        elif cross:
            self.groups = [[h] for h in range(H)]
        else:
            self.groups = [[2 * j, 2 * j + 1, 8 + 2 * j, 9 + 2 * j] for j in range(4)]


def W(name, col=0):
    return (name, col)


PASS1 = [
    Layer("L0sa", "attn", row="L0_xattn_sa_bo", post=("L0_xattn_ln1_g", "L0_xattn_ln1_b"), causal=True,
          q=W("L0_xattn_sa_wq"), k=W("L0_xattn_sa_wk"), v=W("L0_xattn_sa_wv"), o=W("L0_xattn_sa_wo"),
          bq=("L0_xattn_sa_bq", 0), bk=("L0_xattn_sa_bk", 0), bv=("L0_xattn_sa_bv", 0)),
    Layer("L0ca", "attn", row="L0_xattn_ca_bo", post=("L0_xattn_ln2_g", "L0_xattn_ln2_b"), cross=True,
          q=W("L0_xattn_ca_wq"), k=W("L0_xattn_ca_wk"), v=W("L0_xattn_ca_wv"), o=W("L0_xattn_ca_wo"),
          bq=("L0_xattn_ca_bq", 0), bk=("L0_xattn_ca_bk", 0), bv=("L0_xattn_ca_bv", 0)),
    Layer("route", "route"),
]
PASS3 = [
    Layer("L0ln", "norm", post=("L0_xattn_ln3_g", "L0_xattn_ln3_b")),
    Layer("L1a1", "attn", pre=("L1_xattn_ln1_g", "L1_xattn_ln1_b"), row="L1_xattn_a1_bo", quant=1,
          q=W("L1_xattn_a1_wq"), k=W("L1_xattn_a1_wk"), v=W("L1_xattn_a1_wv"), o=W("L1_xattn_a1_wo")),
    Layer("L1a2", "attn", pre=("L1_xattn_ln2_g", "L1_xattn_ln2_b"), row="L1_xattn_a2_bo", quant=2, cross=True,
          q=W("L1_xattn_a2_wq"), k=W("L1_xattn_a2_wk"), v=W("L1_xattn_a2_wv"), o=W("L1_xattn_a2_wo")),
    Layer("L1ff", "geglu", pre=("L1_xattn_ln3_g", "L1_xattn_ln3_b"), row="L1_xattn_ff_b2",
          w1=W("L1_xattn_ff_w1"), w2=W("L1_xattn_ff_w2"), b1=("L1_xattn_ff_b1", 0)),
    Layer("L2at", "attn64", pre=("L2_xattn_ln_g", "L2_xattn_ln_b"), row="L2_xattn_bo", causal=True,
          q=W("L2_xattn_wq"), k=W("L2_xattn_wkv"), v=W("L2_xattn_wkv", H * HD2), o=W("L2_xattn_wo"),
          bq=("L2_xattn_bq", 0), bk=("L2_xattn_bkv", 0), bv=("L2_xattn_bkv", 8)),
    Layer("L3sa", "attn", pre=("L3_xattn_ln1_g", "L3_xattn_ln1_b"), row="L3_xattn_attn_proj_b", causal=True,
          q=W("L3_xattn_attn_qkv_w"), k=W("L3_xattn_attn_qkv_w", D), v=W("L3_xattn_attn_qkv_w", 2 * D),
          o=W("L3_xattn_attn_proj_w"), bq=("L3_xattn_attn_qkv_b", 0), bk=("L3_xattn_attn_qkv_b", 2),
          bv=("L3_xattn_attn_qkv_b", 4)),
    Layer("L3ca", "attn", pre=("L3_xattn_ln2_g", "L3_xattn_ln2_b"), row="L3_xattn_ca_proj_b", cross=True,
          q=W("L3_xattn_q_w"), k=W("L3_xattn_k_w"), v=W("L3_xattn_v_w"), o=W("L3_xattn_ca_proj_w"),
          bq=("L3_xattn_q_b", 0), bk=("L3_xattn_k_b", 0), bv=("L3_xattn_v_b", 0)),
    Layer("L3ff", "gelu", pre=("L3_xattn_ln3_g", "L3_xattn_ln3_b"), row="L3_xattn_proj_b",
          w1=W("L3_xattn_fc_w"), w2=W("L3_xattn_proj_w"), b1=("L3_xattn_fc_b", 0)),
]


def turn_steps(layers):
    steps = []

    def context(i):
        if i >= len(layers):
            return []
        L, out = layers[i], []
        if L.kind == "attn" and L.cross:
            for g in range(G):
                out += [("kc", L, g, mt) for mt in range(KT)] + [("vc", L, g, c) for c in range(C)]
        if L.kind == "attn64":
            out += [("cln", L, g) for g in range(G)] + [("ctr", L, g) for g in range(G)]
            out += [("k", L, mt) for mt in range(8)] + [("v", L, g, h) for g in range(G) for h in range(2)]
        return out

    def entry(i, g):
        if i >= len(layers):
            return [("store", layers[-1], g)]
        L, out = layers[i], []
        if L.row:
            out.append(("xb", L, g))
        if L.pre:
            out += [("lna", L, g), ("lnb", L, g)]
        if L.kind != "norm":
            out.append(("trx", L, g))
        return out

    for g in range(G):
        steps += entry(0, g)
    fill = context(0)
    for i, L in enumerate(layers):
        steps += fill
        fill = context(i + 1)

        def some(n):
            for _ in range(min(n, len(fill))):
                steps.append(fill.pop(0))

        if L.kind == "norm":
            for g in range(G):
                steps += [("pna", L, g), ("pnb", L, g)] + entry(i + 1, g)
        elif L.kind == "route":
            for g in range(G):
                steps += [("rt1", L, g)]
            for g in range(G):
                steps += [("rt2", L, g), ("rt3", L, g)] + entry(i + 1, g)
        elif L.kind in ("geglu", "gelu"):
            for m in range(FT):
                steps += ([("fg", L, m)] if L.kind == "geglu" else []) + [("fa", L, m)]
            for g in range(G):
                if g == G - 1:
                    some(4)
                steps += [("f2", L, g)] + entry(i + 1, g)
        else:
            steps += [("q", L, mt) for mt in range(8 if L.wide else KT)]
            if not L.cross and not L.wide:
                steps += [("k", L, mt) for mt in range(KT)] + [("v", L, g) for g in range(G)]
            ng = len(L.groups)
            halves = 2 if L.wide else 1
            total = G * ng
            later = {}
            for s in range(total + 8):
                if s < total:
                    steps.append(("qk", L, s // ng, s % ng))
                if L.quant and 0 <= s - 1 < total:
                    steps.append(("qt", L, (s - 1) // ng, (s - 1) % ng))
                if 0 <= s - 2 < total:
                    steps.append(("tp", L, (s - 2) // ng, (s - 2) % ng))
                if 0 <= s - 3 < total:
                    g, n = divmod(s - 3, ng)
                    steps.append(("av", L, g, n))
                    if (n + 1) % (ng // halves) == 0:
                        half = n // (ng // halves)
                        later.setdefault(s, []).append(("fin", L, g, half))
                        later.setdefault(s + 1, []).append(("tro", L, g, half))
                        if half == halves - 1:
                            later.setdefault(s + 2, []).append(("wo", L, g))
                            if L.post:
                                later.setdefault(s + 3, []).extend([("pna", L, g), ("pnb", L, g)])
                            later.setdefault(s + 4, []).extend(entry(i + 1, g))
                steps += later.get(s, [])
                if s >= total + 2:
                    some(3)
    steps += fill
    return steps


PSUM_STEPS = {"kc", "vc", "ctr", "k", "v", "q", "trx", "tro", "wo", "fg", "fa", "f2", "rt1", "rt2", "rt3"}
KEYS = ("kc", "vc", "k", "v", "q")


class Turn:

    def __init__(self, layers):
        self.steps = turn_steps(layers)
        self.layers = layers
        self.psum, self.at, self.count = {}, {}, {}
        self.quant, self.group, self.obank = {}, {}, {}
        for st in self.steps:
            kind, L = st[0], st[1]
            key = (kind, L.name) + st[2:]
            if kind in PSUM_STEPS:
                self.psum[key] = len(self.psum)
            self.at[key] = self.count.get(kind, 0)
            self.count[kind] = self.at[key] + 1
            if L.quant and kind in KEYS:
                self.quant[key] = len(self.quant)
            if kind == "qk":
                self.group[key[1:]] = len(self.group)
            if kind == "fin":
                self.obank[key[1:]] = len(self.obank)
        self.lnorm, n = {}, 0
        for st in self.steps:
            if st[0] in ("lna", "cln", "pna"):
                self.lnorm[(st[0], st[1].name) + st[2:]] = n
                n += 1


PASSES = [PASS1, PASS3]


def network(nc, t, out):
    with ExitStack() as ctx:
        def sb(name, shape, dt=F32):
            return ctx.enter_context(nc.sbuf_tensor(name, shape, dt))

        def sem(name):
            return ctx.enter_context(nc.semaphore(name))

        hT_d = nc.dram_tensor("moe_in_T", (128, KT, B * T), F32, kind="Internal").ap()
        acc_d = nc.dram_tensor("moe_acc", (B, T, D), F32, kind="Internal").ap()
        comb_d = nc.dram_tensor("moe_combine", (B, T, E), F32, kind="Internal").ap()

        ident = sb("ident", [128, 128])
        ident16 = sb("ident16", [128, 128], BF16)
        causal16 = sb("causal16", [T, 4 * T], BF16)
        iota = sb("iota", [T, E])
        cols = sb("cols", [128, NCOL])
        rb_row = sb("rb_row", [T, E])
        eb2 = sb("eb2", [E, D])
        eps = sb("eps", [128, 1])
        dinv = sb("dinv", [128, 8])
        dmul = sb("dmul", [128, 4])
        dtmp = sb("dtmp", [128, 2])

        def col(name, i=0):
            return cols[:, COLS[name][0] + i:COLS[name][0] + i + 1]

        mask_scaled = [col("head_masks", 0), col("head_masks", 1)]
        mask_plain = [col("head_masks", 2), col("head_masks", 3)]
        d_names = ["L1_xattn_d_q1", "L1_xattn_d_k1", "L1_xattn_d_v1", "L1_xattn_d_w1",
                   "L1_xattn_d_q2", "L1_xattn_d_k2", "L1_xattn_d_v2", "L1_xattn_d_w2"]

        const_in = sem("const_in")
        ready = sem("ready")
        with nc.Block() as block:
            @block.sync
            def _(sp):
                loads = [(ident[:], t["ident"]), (ident16[:], t["ident16"]), (causal16[:], t["causal16"]),
                         (iota[:], t["iota"]), (cols[:], t["cols"]),
                         (rb_row[:], t["L0_xattn_router_b"].rearrange("(o e) -> o e", o=1).to_broadcast([T, E])),
                         (eb2[:], t["L0_xattn_e_b2"])]
                for dst, src in loads:
                    sp.dma_start(dst, src).then_inc(const_in, 16)
                sp.wait_ge(const_in, 16 * len(loads))

            @block.vector
            def _(dve):
                dve.memset(eps[:], EPS)
                dve.wait_ge(const_in, 16 * 7)
                d0 = COLS["L1_xattn_d_q1"][0]
                dve.reciprocal(dinv[:], cols[:, d0:d0 + 8]).then_inc(ready, 1)
                for i in range(2):
                    dve.tensor_scalar(dmul[:, 2 * i:2 * i + 1], col(d_names[4 * i]), col(d_names[4 * i + 1]),
                                      HD ** -0.5, ALU.mult, ALU.mult)
                    dve.tensor_scalar(dmul[:, 2 * i + 1:2 * i + 2], col(d_names[4 * i + 2]),
                                      col(d_names[4 * i + 3]), None, ALU.mult)

        attention_pass(nc, t, 0, locals(), out)
        experts_pass(nc, t, locals())
        attention_pass(nc, t, 1, locals(), out)


def attention_pass(nc, t, which, env, out):
    layers = PASSES[which]
    turn = Turn(layers)
    P3 = which == 1
    ident, ident16, causal16, iota = env["ident"], env["ident16"], env["causal16"], env["iota"]
    cols, rb_row, eb2, eps = env["cols"], env["rb_row"], env["eb2"], env["eps"]
    dinv, dmul, col = env["dinv"], env["dmul"], env["col"]
    mask_scaled, mask_plain = env["mask_scaled"], env["mask_plain"]
    hT_d, acc_d, comb_d = env["hT_d"], env["acc_d"], env["comb_d"]
    pre = "c_" if P3 else "a_"
    with ExitStack() as ctx:
        def sb(name, shape, dt=F32):
            return ctx.enter_context(nc.sbuf_tensor(pre + name, shape, dt))

        def sem(name):
            return ctx.enter_context(nc.semaphore(pre + name))

        used = []
        for L in layers:
            for k, w in L.w.items():
                if not k.startswith("b") and w[0] not in used:
                    used.append(w[0])
        if not P3:
            used.append("L0_xattn_router_w")
        weight = {n: sb(n, [128, WEIGHTS[n][0] // 128, WEIGHTS[n][1]]) for n in used}
        w_in = {n: sem("in_" + n) for n in used}
        r0, nrow = (6, NROW - 6) if P3 else (0, 6)
        row_tile = sb("rows", [T, nrow, D])
        row_in = sem("row_in")

        def row(name):
            return row_tile[:, ROWS[name] - r0, :]

        x = sb("x", [T, G, D])
        xb = sb("xb", [T, G, D])
        xn = sb("xn", [T, G, D])
        hT = sb("hT", [128, KT, GT])
        cT = sb("cT", [128, KT, G, M])
        qm = [sb(f"q{p}", [128, KT, GT]) for p in ("even", "odd")]
        kS, vS = sb("kS", [128, KT, GT]), sb("vS", [T, G, D])
        kvC = sb("kvC", [128, KT * G * M + G * C * D])
        kC = kvC[:, 0:KT * G * M].rearrange("p (k g m) -> p k g m", k=KT, g=G)
        vC = kvC[0:MC, KT * G * M:].rearrange("p (g c d) -> p g c d", g=G, c=C)
        stats = sb("stats", [T, 2, 6])
        mv = sb("mv", [T, 2, 2])
        nrm = sb("nrm", [T, 2, 4])
        P = sb("P", [T, 3, 448])
        PT = sb("PT", [MC, 2, 4 * T])
        negm = sb("negm", [T, 4, 4])
        sums = sb("sums", [T, 2, H])
        rsum = sb("rsum", [T, 2, H])
        Osb = sb("Osb", [T, 2, 512])
        OT = sb("OT", [128, 2, 8, T])
        if P3:
            qmb = [sb(f"qint{p}", [128, KT, GT], BF16) for p in ("even", "odd")]
            kSb, vSb = sb("kSint", [128, KT, GT], BF16), sb("vSint", [T, G, D], BF16)
            kCb, vCb = sb("kCint", [128, KT, G, M], BF16), sb("vCint", [MC, G, C, D], BF16)
            PTb = sb("PTint", [MC, 2, 4 * T], BF16)
            negs = sb("negs", [T, 4, 4])
            rq = sb("rq", [T, 4, 4, 2])
            raw = sb("raw", [128, 2, 448])
            q2, k2 = sb("q2", [128, 8, GT]), sb("k2", [128, 8, GT])
            v2 = kvC[0:T, 0:G * H * HD2].rearrange("p (g d) -> p g d", g=G)
            ctok = sb("ctok", [T, G, D])
            cn = sb("cn", [T, G, D])
            cnT = sb("cnT", [128, KT, GT])
            hf = q2
            gl = sb("gl", [128, 2, GT])
        else:
            lg, ex, pr = sb("lg", [T, G, E]), sb("ex", [T, G, E]), sb("pr", [T, G, E])
            rt = sb("rt", [T, G, 8])
            top = sb("top", [T, G, 8])
            topi = sb("topi", [T, G, 8], U32)
            topf = sb("topf", [T, G, 8])
            c1, c2, comb = sb("c1", [T, G, E]), sb("c2", [T, G, E]), sb("comb", [T, G, E])
            cbT = sb("cbT", [E, G, T])
            acc = sb("acc", [T, G, D])

        def pb(name):
            return ctx.enter_context(nc.psum_tensor(pre + name, [128, 512], F32))

        mp = [pb(f"mix{i}") for i in range(2)]
        Sb = [pb(f"scores{i}") for i in range(2)]
        Tb = [pb(f"probsT{i}") for i in range(2)]
        Ob = [pb(f"attnout{i}") for i in range(2)]

        names = ["x_in", "ctx_in", "stored", "mp_full", "mp_free0", "mp_free1", "s_full", "max_done", "exp_done",
                 "quant_done", "tp_done", "pt_done", "av_done", "fin_done", "x_done", "xb_done", "stat_done",
                 "rstd_done", "xn_done", "ln_half", "dve_chain", "act_chain", "pool_chain", "int_done",
                 "gate_done", "rt_sum", "rt_exp", "rt_gap", "rt_w", "comb_done"]
        s = {n: sem(n) for n in names}
        mp_free = [s["mp_free0"], s["mp_free1"]]

        def drained(eng, key):
            u = turn.psum[key]
            eng.wait_ge(mp_free[u % 2], u // 2 + 1)

        def bank_free(eng, u):
            if u >= 2:
                eng.wait_ge(mp_free[u % 2], u // 2)

        def filled(eng, key):
            eng.wait_ge(s["mp_full"], turn.psum[key] + 1)

        def drain_mark(key):
            return mp_free[turn.psum[key] % 2]

        def x_ready(eng, i, g):
            if i == 0:
                eng.wait_ge(s["x_in"], 16 * G)
            elif layers[i - 1].post:
                eng.wait_ge(s["x_done"], turn.at["pnb", layers[i - 1].name, g] + 1)
            else:
                drained(eng, ("wo" if "o" in layers[i - 1].w else "f2", layers[i - 1].name, g))

        def index(L):
            return layers.index(L)

        def gpos(L, g, n):
            return turn.group[L.name, g, n]

        def heads(L, n):
            return L.groups[n]

        def shapes(L):
            return (MC, C) if L.cross else (T, 1)

        def wtile(w, kt, c0, n):
            return weight[w[0]][:, kt, w[1] + c0:w[1] + c0 + n]

        def operand(eng, key, L):
            if L.quant:
                eng.wait_ge(s["int_done"], turn.quant[key] + 1)
            else:
                drained(eng, key)

        def quant_dst(kind, a):
            if kind == "q":
                return GT, [(qmb[p][:, a[0], :], mask_plain[p]) for p in range(2)]
            if kind == "k":
                return GT, [(kSb[:, a[0], :], None)]
            if kind == "v":
                return D, [(vSb[:, a[0], :], None)]
            if kind == "kc":
                return M, [(kCb[:, a[1], a[0], :], None)]
            return D, [(vCb[:, a[0], a[1], :], None)]

        with nc.Block() as block:
            @block.sync
            def _(sp):
                sp.dma_start(row_tile[:], t["rows"][r0:r0 + nrow, :].rearrange("(o r) d -> o r d", o=1)
                             .to_broadcast([T, nrow, D])).then_inc(row_in, 16)
                sp.wait_ge(row_in, 16)
                for n in used:
                    sp.dma_start(weight[n][:], t[n].rearrange("(k p) n -> p k n", p=128)).then_inc(w_in[n], 16)

        with nc.Fori(0, TURNS) as turn_no:
            with nc.Block() as block:
                @block.sync
                def _(sp):
                    src = acc_d if P3 else t["x"]
                    for g in range(G):
                        b = bass.ds(turn_no * G + g, 1)
                        sp.dma_start(x[:, g, :], src[b, :, :].rearrange("o p n -> (o p) n")).then_inc(s["x_in"], 16)
                    for g in range(G):
                        b = bass.ds(turn_no * G + g, 1)
                        sp.dma_start(cT[:, :, g, :], t["ctxT"][b, :, :].rearrange("o (k p) m -> (o p) k m", p=128)
                                     ).then_inc(s["ctx_in"], 16)
                        if P3:
                            sp.dma_start(ctok[:, g, :], t["ctx_1024"][b, 0:T, :].rearrange("o p n -> (o p) n")
                                         ).then_inc(s["ctx_in"], 16)
                    stores = 0
                    for st in turn.steps:
                        if st[0] != "store":
                            continue
                        g = st[2]
                        b = bass.ds(turn_no * G + g, 1)
                        if P3:
                            x_ready(sp, len(layers), g)
                            sp.dma_start(out[b, :, :].rearrange("o p n -> (o p) n"), x[:, g, :]).then_inc(s["stored"], 16)
                            stores += 1
                        else:
                            drained(sp, ("rt3", "route", g))
                            sp.wait_ge(s["comb_done"], g + 1)
                            sp.dma_start(acc_d[b, :, :].rearrange("o p n -> (o p) n"), acc[:, g, :]).then_inc(s["stored"], 16)
                            sp.dma_start(comb_d[b, :, :].rearrange("o p n -> (o p) n"), comb[:, g, :]).then_inc(s["stored"], 16)
                            stores += 2
                    if not P3:
                        for g in range(G):
                            drained(sp, ("trx", "route", g))
                        sp.dma_start(hT_d[:, :, bass.ds(turn_no * GT, GT)], hT[:]).then_inc(s["stored"], 16)
                        stores += 1
                    sp.wait_ge(s["stored"], 16 * stores)

                @block.tensor
                def _(pe):
                    for st in turn.steps:
                        kind, L, a = st[0], st[1], st[2:]
                        key = (kind, L.name) + a
                        i = index(L)
                        if kind in PSUM_STEPS:
                            u = turn.psum[key]
                            bank = mp[u % 2]
                            bank_free(pe, u)
                        if kind == "trx":
                            g, = a
                            if L.pre:
                                pe.wait_ge(s["xn_done"], turn.lnorm["lna", L.name, g] + 1 - npost(turn, "lna", L, g))
                            else:
                                x_ready(pe, i, g)
                            src = xn if L.pre else x
                            for kt in range(KT):
                                last = pe.transpose(bank[:, kt * T:(kt + 1) * T], src[:, g, kt * 128:(kt + 1) * 128],
                                                    ident[0:T, 0:T])
                            last.then_inc(s["mp_full"], 1)
                        elif kind == "ctr":
                            g, = a
                            pe.wait_ge(s["xn_done"], turn.lnorm["cln", L.name, g] + 1 - npost(turn, "cln", L, g))
                            for kt in range(KT):
                                last = pe.transpose(bank[:, kt * T:(kt + 1) * T], cn[:, g, kt * 128:(kt + 1) * 128],
                                                    ident[0:T, 0:T])
                            last.then_inc(s["mp_full"], 1)
                        elif kind in ("q", "k") or kind in ("fa", "fg"):
                            m, = a
                            src = hT
                            if L.wide and kind == "k":
                                src = cnT
                                for g in range(G):
                                    drained(pe, ("ctr", L.name, g))
                            else:
                                for g in range(G):
                                    drained(pe, ("trx", L.name, g))
                            w = L.w["w1"] if kind in ("fa", "fg") else L.w[kind]
                            pe.wait_ge(w_in[w[0]], 16)
                            c0 = m * 128 + (FF if kind == "fg" else 0)
                            for kt in range(KT):
                                last = pe.matmul(bank[:, 0:GT], wtile(w, kt, c0, 128), src[:, kt, :],
                                                 start=kt == 0, stop=kt == KT - 1)
                            last.then_inc(s["mp_full"], 1)
                        elif kind == "v":
                            g = a[0]
                            c0, n = (a[1] * 512, 512) if L.wide else (0, D)
                            src = cnT if L.wide else hT
                            drained(pe, ("ctr" if L.wide else "trx", L.name, g))
                            pe.wait_ge(w_in[L.w["v"][0]], 16)
                            for kt in range(KT):
                                last = pe.matmul(bank[0:T, 0:n], src[:, kt, g * T:(g + 1) * T],
                                                 wtile(L.w["v"], kt, c0, n), start=kt == 0, stop=kt == KT - 1)
                            last.then_inc(s["mp_full"], 1)
                        elif kind == "kc":
                            g, mt = a
                            pe.wait_ge(s["ctx_in"], 16 * G * (2 if P3 else 1))
                            pe.wait_ge(w_in[L.w["k"][0]], 16)
                            for kt in range(KT):
                                last = pe.matmul(bank[:, 0:M], wtile(L.w["k"], kt, mt * 128, 128), cT[:, kt, g, :],
                                                 start=kt == 0, stop=kt == KT - 1)
                            last.then_inc(s["mp_full"], 1)
                        elif kind == "vc":
                            g, c = a
                            pe.wait_ge(s["ctx_in"], 16 * G * (2 if P3 else 1))
                            pe.wait_ge(w_in[L.w["v"][0]], 16)
                            for kt in range(KT):
                                last = pe.matmul(bank[0:MC, 0:D], cT[:, kt, g, c * MC:(c + 1) * MC],
                                                 wtile(L.w["v"], kt, 0, D), start=kt == 0, stop=kt == KT - 1)
                            last.then_inc(s["mp_full"], 1)
                        elif kind == "qk":
                            g, n = a
                            j = gpos(L, g, n)
                            if j >= 2:
                                pe.wait_ge(s["exp_done"], j - 1)
                            if n == 0:
                                for mt in range(8 if L.wide else KT):
                                    operand(pe, ("q", L.name, mt), L)
                                    if L.cross:
                                        operand(pe, ("kc", L.name, g, mt), L)
                                    else:
                                        operand(pe, ("k", L.name, mt), L)
                            Sx = Sb[j % 2]
                            kk = M if L.cross else T
                            if L.causal:
                                pe.matmul(Sx[0:T, 0:4 * T], ident16[0:T, 0:T], causal16[:], start=True, stop=False)
                            for hi, h in enumerate(heads(L, n)):
                                o = Sx[0:T, hi * kk:(hi + 1) * kk]
                                if L.wide:
                                    r = slice(64 * (h % 2), 64 * (h % 2) + 64)
                                    lhs, rhs = q2[r, h // 2, g * T:(g + 1) * T], k2[r, h // 2, g * T:(g + 1) * T]
                                else:
                                    r0 = 32 * ((h % 8) // 2)
                                    r = slice(r0, r0 + 32)
                                    qs, ks, kc_ = (qmb, kSb, kCb) if L.quant else (qm, kS, kC)
                                    lhs = qs[h % 2][r, h // 8, g * T:(g + 1) * T]
                                    rhs = kc_[r, h // 8, g, :] if L.cross else ks[r, h // 8, g * T:(g + 1) * T]
                                last = pe.matmul(o, lhs, rhs, start=not L.causal, stop=hi == len(heads(L, n)) - 1
                                                 or not L.causal)
                            last.then_inc(s["s_full"], 1)
                        elif kind == "tp":
                            g, n = a
                            j = gpos(L, g, n)
                            if L.quant:
                                pe.wait_ge(s["quant_done"], turn.at["qt", L.name, g, n] + 1)
                            else:
                                pe.wait_ge(s["exp_done"], j + 1)
                            if j >= 2:
                                pe.wait_ge(s["pt_done"], j - 1)
                            kk, nch = shapes(L)
                            for b_ in range(nch * len(heads(L, n))):
                                last = pe.transpose(Tb[j % 2][0:kk, b_ * T:(b_ + 1) * T],
                                                    P[:, j % 3, b_ * kk:(b_ + 1) * kk], ident[0:T, 0:T])
                            last.then_inc(s["tp_done"], 1)
                        elif kind == "av":
                            g, n = a
                            j = gpos(L, g, n)
                            half = n // 2 if L.wide else 0
                            ou = turn.obank[L.name, g, half]
                            if n % 2 == 0 and L.wide or n == 0:
                                if ou >= 2:
                                    pe.wait_ge(s["fin_done"], ou - 1)
                                if L.cross:
                                    for c in range(C):
                                        operand(pe, ("vc", L.name, g, c), L)
                                elif L.wide:
                                    for hv in range(2):
                                        operand(pe, ("v", L.name, g, hv), L)
                                else:
                                    operand(pe, ("v", L.name, g), L)
                            pe.wait_ge(s["pt_done"], j + 1)
                            kk, nch = shapes(L)
                            pt = PTb if L.quant else PT
                            hd = HD2 if L.wide else HD
                            for hi, h in enumerate(heads(L, n)):
                                ho = h - 8 * half
                                for c in range(nch):
                                    if L.wide:
                                        vv = v2[:, g, h * hd:(h + 1) * hd]
                                    elif L.cross:
                                        vv = (vCb if L.quant else vC)[:, g, c, h * hd:(h + 1) * hd]
                                    else:
                                        vv = (vSb if L.quant else vS)[:, g, h * hd:(h + 1) * hd]
                                    b_ = hi * nch + c
                                    last = pe.matmul(Ob[ou % 2][0:T, ho * hd:(ho + 1) * hd],
                                                     pt[0:kk, j % 2, b_ * T:(b_ + 1) * T], vv,
                                                     start=c == 0, stop=c == nch - 1)
                            last.then_inc(s["av_done"], 1)
                        elif kind == "tro":
                            g, half = a
                            ou = turn.obank[L.name, g, half]
                            pe.wait_ge(s["fin_done"], ou + 1)
                            for kt in range(4 if L.wide else KT):
                                last = pe.transpose(bank[:, kt * T:(kt + 1) * T],
                                                    Osb[:, ou % 2, kt * 128:(kt + 1) * 128], ident[0:T, 0:T])
                            last.then_inc(s["mp_full"], 1)
                        elif kind == "wo":
                            g, = a
                            nk = 8 if L.wide else KT
                            for half in range(2 if L.wide else 1):
                                drained(pe, ("tro", L.name, g, half))
                            pe.wait_ge(w_in[L.w["o"][0]], 16)
                            for kt in range(nk):
                                last = pe.matmul(bank[0:T, 0:D], OT[:, g % 2, kt, :], wtile(L.w["o"], kt, 0, D),
                                                 start=kt == 0, stop=kt == nk - 1)
                            last.then_inc(s["mp_full"], 1)
                        elif kind == "f2":
                            g, = a
                            for m in (FT - 2, FT - 1):
                                drained(pe, ("fa", L.name, m))
                            pe.wait_ge(w_in[L.w["w2"][0]], 16)
                            for m in range(FT):
                                last = pe.matmul(bank[0:T, 0:D], hf[:, m, g * T:(g + 1) * T],
                                                 wtile(L.w["w2"], m, 0, D), start=m == 0, stop=m == FT - 1)
                            last.then_inc(s["mp_full"], 1)
                        elif kind == "rt1":
                            g, = a
                            drained(pe, ("trx", L.name, g))
                            pe.wait_ge(w_in["L0_xattn_router_w"], 16)
                            for kt in range(KT):
                                last = pe.matmul(bank[0:T, 0:E], hT[:, kt, g * T:(g + 1) * T],
                                                 weight["L0_xattn_router_w"][:, kt, :], start=kt == 0, stop=kt == KT - 1)
                            last.then_inc(s["mp_full"], 1)
                        elif kind == "rt2":
                            g, = a
                            pe.wait_ge(s["comb_done"], g + 1)
                            pe.transpose(bank[0:E, 0:T], comb[:, g, :], ident[0:T, 0:T]).then_inc(s["mp_full"], 1)
                        elif kind == "rt3":
                            g, = a
                            drained(pe, ("rt2", L.name, g))
                            pe.matmul(bank[0:T, 0:D], cbT[:, g, :], eb2[:], start=True, stop=True).then_inc(s["mp_full"], 1)

                @block.scalar
                def _(act):
                    for st in turn.steps:
                        kind, L, a = st[0], st[1], st[2:]
                        key = (kind, L.name) + a
                        if kind in ("lna", "cln", "pna"):
                            ln = turn.lnorm[key]
                            act.wait_ge(s["stat_done"], ln + 1)
                            act.activation(nrm[:, ln % 2, 0:1], mv[:, ln % 2, 1:2], ACT.Ln, bias=eps[0:T, :]
                                           ).then_inc(s["ln_half"], 1)
                            act.wait_ge(s["ln_half"], ln + 1)
                            act.activation(nrm[:, ln % 2, 1:2], nrm[:, ln % 2, 0:1], ACT.Exp, scale=-0.5
                                           ).then_inc(s["rstd_done"], 1)
                        elif kind == "k" and not L.quant:
                            mt, = a
                            filled(act, key)
                            dst = k2 if L.wide else kS
                            act.activation(dst[:, mt, :], mp[turn.psum[key] % 2][:, 0:GT], ACT.Identity,
                                           bias=col(L.w["bk"][0], L.w["bk"][1] + mt)).then_inc(drain_mark(key), 1)
                        elif kind == "kc" and not L.quant:
                            g, mt = a
                            filled(act, key)
                            act.activation(kC[:, mt, g, :], mp[turn.psum[key] % 2][:, 0:M], ACT.Identity,
                                           bias=col(L.w["bk"][0], L.w["bk"][1] + mt)).then_inc(drain_mark(key), 1)
                        elif kind == "v" and not L.quant:
                            g = a[0]
                            filled(act, key)
                            if L.wide:
                                dst, n = v2[:, g, a[1] * 512:(a[1] + 1) * 512], 512
                            else:
                                dst, n = vS[:, g, :], D
                            act.activation(dst, mp[turn.psum[key] % 2][0:T, 0:n], ACT.Copy).then_inc(drain_mark(key), 1)
                        elif kind == "vc" and not L.quant:
                            g, c = a
                            filled(act, key)
                            act.activation(vC[:, g, c, :], mp[turn.psum[key] % 2][0:MC, 0:D], ACT.Copy
                                           ).then_inc(drain_mark(key), 1)
                        elif kind == "qk":
                            g, n = a
                            j = gpos(L, g, n)
                            act.wait_ge(s["max_done"], j + 1)
                            if j >= 3:
                                act.wait_ge(s["tp_done"], j - 2)
                            kk = M if L.cross else T
                            for hi, h in enumerate(heads(L, n)):
                                cs = slice(hi * kk, (hi + 1) * kk)
                                m_ = negs if L.quant else negm
                                sc = dmul[0:T, 2 * (L.quant - 1):2 * (L.quant - 1) + 1] if L.quant else 1.0
                                last = act.activation(P[:, j % 3, cs], Sb[j % 2][0:T, cs], ACT.Exp,
                                                      bias=m_[:, j % 4, hi:hi + 1], scale=sc,
                                                      accum_out=sums[:, g % 2, h:h + 1])
                            last.then_inc(s["exp_done"], 1)
                        elif kind == "fg":
                            m, = a
                            filled(act, key)
                            if m >= 2:
                                drained(act, ("fa", L.name, m - 2))
                            act.activation(gl[:, m % 2, :], mp[turn.psum[key] % 2][:, 0:GT], ACT.Gelu,
                                           bias=col(L.w["b1"][0], FT + m)).then_inc(drain_mark(key), 1)
                        elif kind == "fa" and L.kind == "gelu":
                            m, = a
                            filled(act, key)
                            act.activation(hf[:, m, :], mp[turn.psum[key] % 2][:, 0:GT], ACT.Gelu,
                                           bias=col(L.w["b1"][0], m)).then_inc(drain_mark(key), 1)
                        elif kind == "rt1":
                            g, = a
                            act.wait_ge(s["rt_sum"], g + 1)
                            act.activation(ex[:, g, :], lg[:, g, :], ACT.Exp, bias=rt[:, g, 0:1],
                                           accum_out=rt[:, g, 1:2]).then_inc(s["rt_exp"], 1)
                            act.wait_ge(s["rt_gap"], g + 1)
                            act.activation(rt[:, g, 4:5], rt[:, g, 3:4], ACT.Exp).then_inc(s["rt_w"], 1)
                        elif kind == "rt2":
                            g, = a
                            filled(act, key)
                            act.activation(cbT[:, g, :], mp[turn.psum[key] % 2][0:E, 0:T], ACT.Copy
                                           ).then_inc(drain_mark(key), 1)

                @block.gpsimd
                def _(pool):
                    chain = 0
                    for st in turn.steps:
                        kind, L, a = st[0], st[1], st[2:]
                        key = (kind, L.name) + a
                        if kind == "xb":
                            g, = a
                            x_ready(pool, index(L), g)
                            pool.tensor_tensor(xb[:, g, :], x[:, g, :], row(L.row), ALU.add
                                               ).then_inc(s["xb_done"], 1)
                        elif kind in KEYS and L.quant:
                            r = turn.quant[key]
                            drained(pool, key)
                            n, dsts = quant_dst(kind, a)
                            np_ = dsts[0][0].shape[0]
                            buf = raw[0:np_, r % 2, 0:n]
                            chain += 1
                            pool.tensor_scalar(buf, buf, 127.0, MAGIC, ALU.min, ALU.add).then_inc(s["pool_chain"], 1)
                            pool.wait_ge(s["pool_chain"], chain)
                            for dst, mask in dsts:
                                last = pool.tensor_scalar(dst, buf, MAGIC, mask, ALU.subtract,
                                                          ALU.mult if mask is not None else ALU.bypass)
                            last.then_inc(s["int_done"], 1)

                @block.vector
                def _(dve):
                    chain = [0]

                    def link(ins):
                        chain[0] += 1
                        ins.then_inc(s["dve_chain"], 1)
                        dve.wait_ge(s["dve_chain"], chain[0])

                    def statistics(src, ln):
                        link(dve.bn_stats(stats[:, ln % 2, :], src))
                        dve.bn_aggr(mv[:, ln % 2, :], stats[:, ln % 2, :]).then_inc(s["stat_done"], 1)

                    def refine(ln):
                        v = mv[:, ln % 2, 1:2]
                        n = nrm[:, ln % 2, :]
                        dve.wait_ge(s["rstd_done"], ln + 1)
                        link(dve.tensor_scalar(n[:, 2:3], v, EPS, n[:, 1:2], ALU.add, ALU.mult))
                        link(dve.tensor_scalar(n[:, 2:3], n[:, 2:3], n[:, 1:2], -0.5, ALU.mult, ALU.mult))
                        link(dve.tensor_scalar(n[:, 3:4], n[:, 2:3], 1.5, n[:, 1:2], ALU.add, ALU.mult))

                    def normalize(dst, src, ln):
                        return dve.tensor_scalar(dst, src, mv[:, ln % 2, 0:1], nrm[:, ln % 2, 3:4],
                                                 ALU.subtract, ALU.mult)

                    for st in turn.steps:
                        kind, L, a = st[0], st[1], st[2:]
                        key = (kind, L.name) + a
                        i = index(L)
                        if kind in PSUM_STEPS:
                            bank = mp[turn.psum[key] % 2]
                        if kind == "lna":
                            g, = a
                            x_ready(dve, i, g)
                            statistics(x[:, g, :], turn.lnorm[key])
                        elif kind == "lnb":
                            g, = a
                            ln = turn.lnorm["lna", L.name, g]
                            refine(ln)
                            normalize(xn[:, g, :], x[:, g, :], ln).then_inc(s["xn_done"], 1)
                        elif kind == "cln":
                            g, = a
                            ln = turn.lnorm[key]
                            dve.wait_ge(s["ctx_in"], 16 * G * 2)
                            statistics(ctok[:, g, :], ln)
                            refine(ln)
                            normalize(cn[:, g, :], ctok[:, g, :], ln).then_inc(s["xn_done"], 1)
                        elif kind == "pna":
                            g, = a
                            if L.kind == "norm":
                                x_ready(dve, i, g)
                            else:
                                drained(dve, ("wo", L.name, g))
                            statistics(x[:, g, :], turn.lnorm[key])
                        elif kind == "pnb":
                            g, = a
                            ln = turn.lnorm["pna", L.name, g]
                            refine(ln)
                            link(normalize(x[:, g, :], x[:, g, :], ln))
                            link(dve.tensor_tensor(x[:, g, :], x[:, g, :], row(L.post[0]), ALU.mult))
                            dve.tensor_tensor(x[:, g, :], x[:, g, :], row(L.post[1]), ALU.add
                                              ).then_inc(s["x_done"], 1)
                        elif kind in ("trx", "ctr"):
                            g, = a
                            filled(dve, key)
                            dst = hT if kind == "trx" else cnT
                            if L.pre:
                                for kt in range(KT):
                                    last = dve.tensor_scalar(dst[:, kt, g * T:(g + 1) * T], bank[:, kt * T:(kt + 1) * T],
                                                             col(L.pre[0], kt), col(L.pre[1], kt), ALU.mult, ALU.add)
                            else:
                                last = dve.tensor_copy(dst[:, :, g * T:(g + 1) * T],
                                                       bank[:, 0:KT * T].rearrange("p (k n) -> p k n", k=KT))
                            last.then_inc(drain_mark(key), 1)
                        elif kind in KEYS and L.quant:
                            r = turn.quant[key]
                            filled(dve, key)
                            if r >= 2:
                                dve.wait_ge(s["int_done"], r - 1)
                            n, dsts = quant_dst(kind, a)
                            np_ = dsts[0][0].shape[0]
                            di = 4 * (L.quant - 1) + {"q": 0, "k": 1, "kc": 1, "v": 2, "vc": 2}[kind]
                            dve.tensor_scalar(raw[0:np_, r % 2, 0:n], bank[0:np_, 0:n], dinv[0:np_, di:di + 1], -128.0,
                                              ALU.mult, ALU.max).then_inc(drain_mark(key), 1)
                        elif kind == "q":
                            mt, = a
                            filled(dve, key)
                            bq = col(L.w["bq"][0], L.w["bq"][1] + mt)
                            if L.wide:
                                last = dve.tensor_scalar(q2[:, mt, :], bank[:, 0:GT], bq, HD2 ** -0.5, ALU.add, ALU.mult)
                            else:
                                for p in range(2):
                                    last = dve.tensor_scalar(qm[p][:, mt, :], bank[:, 0:GT], bq, mask_scaled[p],
                                                             ALU.add, ALU.mult)
                            last.then_inc(drain_mark(key), 1)
                        elif kind == "qk":
                            g, n = a
                            j = gpos(L, g, n)
                            nh = len(heads(L, n))
                            kk = M if L.cross else T
                            dve.wait_ge(s["s_full"], j + 1)
                            ins = dve.tensor_reduce(negm[:, j % 4, 0:nh],
                                                    Sb[j % 2][0:T, 0:nh * kk].rearrange("p (h k) -> p h k", h=nh),
                                                    AX.X, ALU.max, negate=True)
                            if L.quant:
                                link(ins)
                                qi = 2 * (L.quant - 1)
                                dve.tensor_scalar(negs[:, j % 4, 0:nh], negm[:, j % 4, 0:nh], dmul[0:T, qi:qi + 1], None,
                                                  ALU.mult).then_inc(s["max_done"], 1)
                            else:
                                ins.then_inc(s["max_done"], 1)
                        elif kind == "qt":
                            g, n = a
                            j = gpos(L, g, n)
                            kk = M if L.cross else T
                            dw = dinv[0:T, 4 * L.quant - 1:4 * L.quant]
                            dve.wait_ge(s["exp_done"], j + 1)
                            for hi, h in enumerate(heads(L, n)):
                                last = dve.reciprocal(rq[:, j % 4, hi, 0:1], sums[:, g % 2, h:h + 1])
                            link(last)
                            link(dve.tensor_scalar(rq[:, j % 4, :, 1], rq[:, j % 4, :, 0], dw, None, ALU.mult)
                                 if len(heads(L, n)) == 4 else
                                 dve.tensor_scalar(rq[:, j % 4, 0:1, 1], rq[:, j % 4, 0:1, 0], dw, None, ALU.mult))
                            for hi, h in enumerate(heads(L, n)):
                                cs = slice(hi * kk, (hi + 1) * kk)
                                last = dve.tensor_scalar(P[:, j % 3, cs], P[:, j % 3, cs], rq[:, j % 4, hi, 1:2], MAGIC,
                                                         ALU.mult, ALU.add)
                            last.then_inc(s["quant_done"], 1)
                        elif kind == "tp":
                            g, n = a
                            j = gpos(L, g, n)
                            kk, nch = shapes(L)
                            w_ = nch * len(heads(L, n)) * T
                            dve.wait_ge(s["tp_done"], j + 1)
                            if j >= 2:
                                dve.wait_ge(s["av_done"], j - 1)
                            if L.quant:
                                dve.tensor_scalar(PTb[0:kk, j % 2, 0:w_], Tb[j % 2][0:kk, 0:w_], MAGIC, 255.0,
                                                  ALU.subtract, ALU.min).then_inc(s["pt_done"], 1)
                            else:
                                dve.tensor_copy(PT[0:kk, j % 2, 0:w_], Tb[j % 2][0:kk, 0:w_]).then_inc(s["pt_done"], 1)
                        elif kind == "fin":
                            g, half = a
                            ou = turn.obank[L.name, g, half]
                            last_group = (half + 1) * len(L.groups) // (2 if L.wide else 1) - 1
                            if ou >= 2:
                                prev = [k for k, v in turn.obank.items() if v == ou - 2][0]
                                dve.wait_ge(s["mp_full"], turn.psum[("tro",) + prev] + 1)
                            if L.quant:
                                dve.wait_ge(s["av_done"], gpos(L, g, last_group) + 1)
                                qi = 2 * (L.quant - 1) + 1
                                dve.tensor_scalar(Osb[:, ou % 2, 0:D], Ob[ou % 2][0:T, 0:D], dmul[0:T, qi:qi + 1], None,
                                                  ALU.mult).then_inc(s["fin_done"], 1)
                            else:
                                nh, hd = (8, HD2) if L.wide else (H, HD)
                                hs = slice(half * nh, half * nh + nh)
                                dve.wait_ge(s["exp_done"], gpos(L, g, last_group) + 1)
                                link(dve.reciprocal(rsum[:, g % 2, hs], sums[:, g % 2, hs]))
                                dve.wait_ge(s["av_done"], gpos(L, g, last_group) + 1)
                                dve.tensor_tensor(Osb[:, ou % 2, 0:nh * hd].rearrange("p (h d) -> p h d", h=nh),
                                                  Ob[ou % 2][0:T, 0:nh * hd].rearrange("p (h d) -> p h d", h=nh),
                                                  rsum[:, g % 2, hs].unsqueeze(2).to_broadcast([T, nh, hd]),
                                                  ALU.mult).then_inc(s["fin_done"], 1)
                        elif kind == "tro":
                            g, half = a
                            nk = 4 if L.wide else KT
                            filled(dve, key)
                            dst = OT[:, g % 2, half * nk:(half + 1) * nk, :]
                            src = bank[:, 0:nk * T].rearrange("p (k n) -> p k n", k=nk)
                            if "bv" in L.w:
                                c0 = COLS[L.w["bv"][0]][0] + L.w["bv"][1] + half * nk
                                ins = dve.tensor_tensor(dst, src, cols[:, c0:c0 + nk].unsqueeze(2).to_broadcast([128, nk, T]),
                                                        ALU.add)
                            else:
                                ins = dve.tensor_copy(dst, src)
                            ins.then_inc(drain_mark(key), 1)
                        elif kind in ("wo", "f2"):
                            g, = a
                            filled(dve, key)
                            dve.wait_ge(s["xb_done"], turn.at["xb", L.name, g] + 1)
                            dve.tensor_tensor(x[:, g, :], bank[0:T, 0:D], xb[:, g, :], ALU.add
                                              ).then_inc(drain_mark(key), 1)
                        elif kind == "fa" and L.kind == "geglu":
                            m, = a
                            filled(dve, key)
                            drained(dve, ("fg", L.name, m))
                            dve.scalar_tensor_tensor(hf[:, m, :], bank[:, 0:GT], col(L.w["b1"][0], m), gl[:, m % 2, :],
                                                     ALU.add, ALU.mult).then_inc(drain_mark(key), 1)
                        elif kind == "rt1":
                            g, = a
                            r = rt[:, g, :]
                            filled(dve, key)
                            dve.tensor_tensor(lg[:, g, :], bank[0:T, 0:E], rb_row[:], ALU.add
                                              ).then_inc(drain_mark(key), 1)
                            drained(dve, key)
                            dve.tensor_reduce(r[:, 0:1], lg[:, g, :], AX.X, ALU.max, negate=True).then_inc(s["rt_sum"], 1)
                            dve.wait_ge(s["rt_exp"], g + 1)
                            link(dve.reciprocal(r[:, 2:3], r[:, 1:2]))
                            link(dve.tensor_scalar(pr[:, g, :], ex[:, g, :], r[:, 2:3], None, ALU.mult))
                            link(dve.max(top[:, g, :], pr[:, g, :]))
                            link(dve.max_index(topi[:, g, :], top[:, g, :], pr[:, g, :]))
                            dve.tensor_tensor(r[:, 3:4], top[:, g, 1:2], top[:, g, 0:1], ALU.subtract).then_inc(s["rt_gap"], 1)
                            dve.tensor_copy(topf[:, g, :], topi[:, g, :])
                            dve.wait_ge(s["rt_w"], g + 1)
                            link(dve.tensor_scalar(r[:, 5:6], r[:, 4:5], 1.0, None, ALU.add))
                            link(dve.reciprocal(r[:, 6:7], r[:, 5:6]))
                            link(dve.tensor_tensor(r[:, 7:8], r[:, 6:7], r[:, 4:5], ALU.mult))
                            dve.tensor_scalar(c1[:, g, :], iota[:], topf[:, g, 0:1], r[:, 6:7], ALU.is_equal, ALU.mult)
                            link(dve.tensor_scalar(c2[:, g, :], iota[:], topf[:, g, 1:2], r[:, 7:8], ALU.is_equal, ALU.mult))
                            dve.tensor_tensor(comb[:, g, :], c1[:, g, :], c2[:, g, :], ALU.add).then_inc(s["comb_done"], 1)
                        elif kind == "rt3":
                            g, = a
                            filled(dve, key)
                            dve.tensor_tensor(acc[:, g, :], bank[0:T, 0:D], x[:, g, :], ALU.add
                                              ).then_inc(drain_mark(key), 1)

            with nc.Block() as block:
                @block.sync
                def _(sp):
                    for v in s.values():
                        sp.sem_clear(v)


def npost(turn, kind, L, g):
    at = turn.lnorm[kind, L.name, g]
    return sum(1 for k, v in turn.lnorm.items() if v < at and k[0] == "pna")


def experts_pass(nc, t, env):
    hT_d, acc_d, comb_d = env["hT_d"], env["acc_d"], env["comb_d"]
    HALF = B * T // 2
    BH = B // 2
    with ExitStack() as ctx:
        def sb(name, shape, dt=F32):
            return ctx.enter_context(nc.sbuf_tensor("b_" + name, shape, dt))

        def sem(name):
            return ctx.enter_context(nc.semaphore("b_" + name))

        h = sb("h", [128, KT, B * T])
        acc = sb("acc", [T, B, D])
        comb = sb("comb", [T, B, E])
        ce = sb("ce", [T, 2, B])
        w1 = sb("w1", [128, 2, KT, FF])
        w2 = sb("w2", [128, 2, FT, D])
        b1 = sb("b1", [128, 2, FT])
        hid = sb("hid", [128, 2, FT, HALF])
        hp = [ctx.enter_context(nc.psum_tensor(f"b_hidden{i}", [128, 512], F32)) for i in range(4)]
        yp = [ctx.enter_context(nc.psum_tensor(f"b_out{i}", [128, 512], F32)) for i in range(4)]
        in_once = sem("in_once")
        w_in = [sem("w_in0"), sem("w_in1")]
        turn_sems = {n: sem(n) for n in ["h_full", "h_free", "y_full", "y_free", "ce_done"]}
        h_full, h_free, y_full, y_free, ce_done = turn_sems.values()
        stored = sem("stored")

        def load_expert(sp, slot, e):
            e = bass.ds(e, 1)
            sp.dma_start(w1[:, slot], t["L0_xattn_e_w1"][e, :, :].rearrange("o (k p) n -> (o p) k n", p=128)
                         ).then_inc(w_in[slot], 16)
            sp.dma_start(b1[:, slot], t["e_b1T"][e, :, :].rearrange("o p n -> (o p) n")).then_inc(w_in[slot], 16)
            sp.dma_start(w2[:, slot], t["L0_xattn_e_w2"][e, :, :].rearrange("o (k p) n -> (o p) k n", p=128)
                         ).then_inc(w_in[slot], 16)

        with nc.Block() as block:
            @block.sync
            def _(sp):
                load_expert(sp, 0, 0)
                sp.dma_start(h[:], hT_d).then_inc(in_once, 16)
                sp.dma_start(acc[:], acc_d.rearrange("b p n -> p b n")).then_inc(in_once, 16)
                sp.dma_start(comb[:], comb_d.rearrange("b p n -> p b n")).then_inc(in_once, 16)
                sp.wait_ge(in_once, 48)

        units = [(slot, half) for slot in range(2) for half in range(2)]
        with nc.Fori(0, E // 2) as pair:
            with nc.Block() as block:
                @block.sync
                def _(sp):
                    load_expert(sp, 1, pair * 2 + 1)
                    sp.wait_ge(y_full, 2 * BH)
                    load_expert(sp, 0, (pair * 2 + 2) % E)

                @block.tensor
                def _(pe):
                    for n, (slot, half) in enumerate(units):
                        pe.wait_ge(w_in[slot], 48 * (pair + 1))
                        for m in range(FT):
                            u = n * FT + m
                            if u >= 4:
                                pe.wait_ge(h_free, u - 3)
                            for kt in range(KT):
                                last = pe.matmul(hp[u % 4][:, 0:HALF], w1[:, slot, kt, m * 128:(m + 1) * 128],
                                                 h[:, kt, half * HALF:(half + 1) * HALF], start=kt == 0, stop=kt == KT - 1)
                            last.then_inc(h_full, 1)
                        pe.wait_ge(h_free, (n + 1) * FT)
                        for b in range(BH):
                            u = n * BH + b
                            if u >= 4:
                                pe.wait_ge(y_free, u - 3)
                            for m in range(FT):
                                last = pe.matmul(yp[u % 4][0:T, 0:D], hid[:, n % 2, m, b * T:(b + 1) * T],
                                                 w2[:, slot, m, :], start=m == 0, stop=m == FT - 1)
                            last.then_inc(y_full, 1)

                @block.scalar
                def _(act):
                    for n, (slot, half) in enumerate(units):
                        act.wait_ge(w_in[slot], 48 * (pair + 1))
                        if n >= 2:
                            act.wait_ge(y_full, (n - 1) * BH)
                        for m in range(FT):
                            u = n * FT + m
                            act.wait_ge(h_full, u + 1)
                            act.activation(hid[:, n % 2, m, :], hp[u % 4][:, 0:HALF], ACT.Gelu,
                                           bias=b1[:, slot, m:m + 1]).then_inc(h_free, 1)

                @block.vector
                def _(dve):
                    for slot in range(2):
                        dve.tensor_copy(ce[:, slot, :], comb[:, :, bass.ds(pair * 2 + slot, 1)].rearrange("p b o -> p (b o)")
                                        ).then_inc(ce_done, 1)
                    dve.wait_ge(ce_done, 2)
                    for n, (slot, half) in enumerate(units):
                        for b in range(BH):
                            u = n * BH + b
                            tile = half * BH + b
                            dve.wait_ge(y_full, u + 1)
                            if n >= 2:
                                dve.wait_ge(y_free, (n - 2) * BH + b + 1)
                            dve.scalar_tensor_tensor(acc[:, tile, :], yp[u % 4][0:T, 0:D], ce[:, slot, tile:tile + 1],
                                                     acc[:, tile, :], ALU.mult, ALU.add).then_inc(y_free, 1)
            with nc.Block() as block:
                @block.sync
                def _(sp):
                    for v in turn_sems.values():
                        sp.sem_clear(v)

        with nc.Block() as block:
            @block.sync
            def _(sp):
                sp.wait_ge(w_in[0], 48 * (E // 2 + 1))
                sp.dma_start(acc_d.rearrange("b p n -> p b n"), acc[:]).then_inc(stored, 16)
                sp.wait_ge(stored, 16)


_NAMES = ["x", "ctx_1024", "L0_xattn_e_w1", "L0_xattn_e_w2", "L0_xattn_e_b2", "L0_xattn_router_b"]


def kernel(**inputs):
    import numpy as _np
    import concourse.bacc as _bacc
    from concourse.bass_utils import run_bass_kernel_spmd as _run

    given = {n: _np.asarray(a) for n, a in inputs.items()}
    arrays = {n: given[n] for n in _NAMES}
    arrays["ctxT"] = given["ctx_1024"].transpose(0, 2, 1)
    arrays["e_b1T"] = given["L0_xattn_e_b1"].reshape(E, FT, 128).transpose(0, 2, 1)
    for name, (_, _, turned) in WEIGHTS.items():
        arrays[name] = given[name].T if turned else given[name]
    bf16 = mybir.dt.np(BF16)
    arrays["ident"] = _np.eye(128, dtype=_np.float32)
    arrays["ident16"] = _np.eye(128).astype(bf16)
    arrays["causal16"] = _np.tile(_np.where(_np.tri(T) > 0, 0.0, -1e30), (1, 4)).astype(bf16)
    arrays["iota"] = _np.tile(_np.arange(E, dtype=_np.float32), (T, 1))
    even = (_np.arange(128) // HD % 2 == 0).astype(_np.float32)
    masks = _np.stack([even * HD ** -0.5, (1 - even) * HD ** -0.5, even, 1 - even], axis=1).astype(_np.float32)
    parts = []
    for name, (_, n) in COLS.items():
        if name == "head_masks":
            parts.append(masks)
        elif n == 1:
            parts.append(_np.broadcast_to(given[name].reshape(1, 1), (128, 1)))
        else:
            parts.append(given[name].reshape(n, 128).T)
    arrays["cols"] = _np.concatenate(parts, axis=1)
    arrays["rows"] = _np.stack([given[name] for name in ROWS])

    nc = _bacc.Bacc("TRN2", target_bir_lowering=False, num_devices=1)
    feed, aps = {}, {}
    for name, a in arrays.items():
        a = _np.ascontiguousarray(a)
        feed[f"in_{name}_dram"] = a
        aps[name] = nc.dram_tensor(f"in_{name}_dram", a.shape, mybir.dt.from_np(a.dtype), kind="ExternalInput").ap()
    out = nc.dram_tensor("out_dram", (B, T, D), F32, kind="ExternalOutput").ap()
    network(nc, aps, out)
    return _run(nc, [feed], core_ids=[0]).results[0]["out_dram"]
```

```python
from contextlib import ExitStack

import concourse.bass as bass
from concourse import mybir

F32 = mybir.dt.float32
BF16 = mybir.dt.bfloat16
F16 = mybir.dt.float16
U32 = mybir.dt.uint32
ALU = mybir.AluOpType
ACT = mybir.ActivationFunctionType
AX = mybir.AxisListType

B, T, D, M = 8, 112, 256, 375
H = 16
HD, HD2 = D // H, 64
KT = D // 128
C, MC = 3, M // 3
E, FF = 8, 1024
FT = FF // 128
G = 4
GT = G * T
PT2 = 2 * T
TURNS = B // G
RP = 4
MAGIC = 1.5 * 2.0 ** 23
EPS = 1e-5

COLS = {}
for _name, _n in [
    ("L0_xattn_sa_bq", 2), ("L0_xattn_sa_bk", 2), ("L0_xattn_sa_bv", 2),
    ("L0_xattn_ca_bq", 2), ("L0_xattn_ca_bk", 2), ("L0_xattn_ca_bv", 2),
    ("L1_xattn_ln1_g", 2), ("L1_xattn_ln1_b", 2), ("L1_xattn_ln2_g", 2), ("L1_xattn_ln2_b", 2),
    ("L1_xattn_ln3_g", 2), ("L1_xattn_ln3_b", 2), ("L1_xattn_ff_b1", 16),
    ("L2_xattn_ln_g", 2), ("L2_xattn_ln_b", 2), ("L2_xattn_bq", 8), ("L2_xattn_bkv", 16),
    ("L3_xattn_ln1_g", 2), ("L3_xattn_ln1_b", 2), ("L3_xattn_attn_qkv_b", 6),
    ("L3_xattn_ln2_g", 2), ("L3_xattn_ln2_b", 2), ("L3_xattn_q_b", 2), ("L3_xattn_k_b", 2), ("L3_xattn_v_b", 2),
    ("L3_xattn_ln3_g", 2), ("L3_xattn_ln3_b", 2), ("L3_xattn_fc_b", 8),
    ("L1_xattn_d_q1", 1), ("L1_xattn_d_k1", 1), ("L1_xattn_d_v1", 1), ("L1_xattn_d_w1", 1),
    ("L1_xattn_d_q2", 1), ("L1_xattn_d_k2", 1), ("L1_xattn_d_v2", 1), ("L1_xattn_d_w2", 1),
    ("head_masks", 8),
]:
    COLS[_name] = (sum(n for _, n in COLS.values()), _n)
NCOL = sum(n for _, n in COLS.values())
ROWS = {name: i for i, name in enumerate([
    "L0_xattn_sa_bo", "L0_xattn_ca_bo", "L0_xattn_ln1_g", "L0_xattn_ln1_b", "L0_xattn_ln2_g", "L0_xattn_ln2_b",
    "L0_xattn_ln3_g", "L0_xattn_ln3_b", "L1_xattn_a1_bo", "L1_xattn_a2_bo", "L1_xattn_ff_b2", "L2_xattn_bo",
    "L3_xattn_attn_proj_b", "L3_xattn_ca_proj_b", "L3_xattn_proj_b"])}
NROW = len(ROWS)
WEIGHTS = {
    "L0_xattn_sa_wq": (D, D, False), "L0_xattn_sa_wk": (D, D, False), "L0_xattn_sa_wv": (D, D, False),
    "L0_xattn_sa_wo": (D, D, False), "L0_xattn_ca_wq": (D, D, False), "L0_xattn_ca_wk": (D, D, False),
    "L0_xattn_ca_wv": (D, D, False), "L0_xattn_ca_wo": (D, D, False), "L0_xattn_router_w": (D, E, False),
    "L1_xattn_a1_wq": (D, D, False), "L1_xattn_a1_wk": (D, D, False), "L1_xattn_a1_wv": (D, D, False),
    "L1_xattn_a1_wo": (D, D, False), "L1_xattn_a2_wq": (D, D, False), "L1_xattn_a2_wk": (D, D, False),
    "L1_xattn_a2_wv": (D, D, False), "L1_xattn_a2_wo": (D, D, False), "L1_xattn_ff_w1": (D, 2 * FF, False),
    "L1_xattn_ff_w2": (FF, D, False), "L2_xattn_wq": (D, H * HD2, False), "L2_xattn_wkv": (D, 2 * H * HD2, False),
    "L2_xattn_wo": (H * HD2, D, False), "L3_xattn_attn_qkv_w": (D, 3 * D, True), "L3_xattn_attn_proj_w": (D, D, True),
    "L3_xattn_q_w": (D, D, True), "L3_xattn_k_w": (D, D, True), "L3_xattn_v_w": (D, D, True),
    "L3_xattn_ca_proj_w": (D, D, True), "L3_xattn_fc_w": (D, FF, True), "L3_xattn_proj_w": (FF, D, True)}


class Layer:

    def __init__(self, name, kind, pre=None, post=None, row=None, quant=None, causal=False, cross=False, **w):
        self.name, self.kind, self.pre, self.post, self.row = name, kind, pre, post, row
        self.quant, self.causal, self.cross, self.w = quant, causal, cross, w
        self.wide = kind == "attn64"
        if kind == "attn64":
            self.groups = [[8 * half + 2 * i + par for i in range(4)] for half in range(2) for par in range(2)]
        elif cross:
            self.groups = [[h] for h in range(H)]
        else:
            self.groups = [[2 * j, 2 * j + 1, 8 + 2 * j, 9 + 2 * j] for j in range(4)]


def W(name, col=0):
    return (name, col)


PASS1 = [
    Layer("L0sa", "attn", row="L0_xattn_sa_bo", post=("L0_xattn_ln1_g", "L0_xattn_ln1_b"), causal=True,
          q=W("L0_xattn_sa_wq"), k=W("L0_xattn_sa_wk"), v=W("L0_xattn_sa_wv"), o=W("L0_xattn_sa_wo"),
          bq=("L0_xattn_sa_bq", 0), bk=("L0_xattn_sa_bk", 0), bv=("L0_xattn_sa_bv", 0)),
    Layer("L0ca", "attn", row="L0_xattn_ca_bo", post=("L0_xattn_ln2_g", "L0_xattn_ln2_b"), cross=True,
          q=W("L0_xattn_ca_wq"), k=W("L0_xattn_ca_wk"), v=W("L0_xattn_ca_wv"), o=W("L0_xattn_ca_wo"),
          bq=("L0_xattn_ca_bq", 0), bk=("L0_xattn_ca_bk", 0), bv=("L0_xattn_ca_bv", 0)),
    Layer("route", "route"),
]
PASS3 = [
    Layer("L0ln", "norm", post=("L0_xattn_ln3_g", "L0_xattn_ln3_b")),
    Layer("L1a1", "attn", pre=("L1_xattn_ln1_g", "L1_xattn_ln1_b"), row="L1_xattn_a1_bo", quant=1,
          q=W("L1_xattn_a1_wq"), k=W("L1_xattn_a1_wk"), v=W("L1_xattn_a1_wv"), o=W("L1_xattn_a1_wo")),
    Layer("L1a2", "attn", pre=("L1_xattn_ln2_g", "L1_xattn_ln2_b"), row="L1_xattn_a2_bo", quant=2, cross=True,
          q=W("L1_xattn_a2_wq"), k=W("L1_xattn_a2_wk"), v=W("L1_xattn_a2_wv"), o=W("L1_xattn_a2_wo")),
    Layer("L1ff", "geglu", pre=("L1_xattn_ln3_g", "L1_xattn_ln3_b"), row="L1_xattn_ff_b2",
          w1=W("L1_xattn_ff_w1"), w2=W("L1_xattn_ff_w2"), b1=("L1_xattn_ff_b1", 0)),
]
PASS4 = [
    Layer("L2at", "attn64", pre=("L2_xattn_ln_g", "L2_xattn_ln_b"), row="L2_xattn_bo", causal=True,
          q=W("L2_xattn_wq"), k=W("L2_xattn_wkv"), v=W("L2_xattn_wkv", H * HD2), o=W("L2_xattn_wo"),
          bq=("L2_xattn_bq", 0), bk=("L2_xattn_bkv", 0), bv=("L2_xattn_bkv", 8)),
    Layer("L3sa", "attn", pre=("L3_xattn_ln1_g", "L3_xattn_ln1_b"), row="L3_xattn_attn_proj_b", causal=True,
          q=W("L3_xattn_attn_qkv_w"), k=W("L3_xattn_attn_qkv_w", D), v=W("L3_xattn_attn_qkv_w", 2 * D),
          o=W("L3_xattn_attn_proj_w"), bq=("L3_xattn_attn_qkv_b", 0), bk=("L3_xattn_attn_qkv_b", 2),
          bv=("L3_xattn_attn_qkv_b", 4)),
    Layer("L3ca", "attn", pre=("L3_xattn_ln2_g", "L3_xattn_ln2_b"), row="L3_xattn_ca_proj_b", cross=True,
          q=W("L3_xattn_q_w"), k=W("L3_xattn_k_w"), v=W("L3_xattn_v_w"), o=W("L3_xattn_ca_proj_w"),
          bq=("L3_xattn_q_b", 0), bk=("L3_xattn_k_b", 0), bv=("L3_xattn_v_b", 0)),
    Layer("L3ff", "gelu", pre=("L3_xattn_ln3_g", "L3_xattn_ln3_b"), row="L3_xattn_proj_b",
          w1=W("L3_xattn_fc_w"), w2=W("L3_xattn_proj_w"), b1=("L3_xattn_fc_b", 0)),
]


LAG_SPLIT, LAG_ROUND, LAG_TURN, LAG_AV = 1, 2, 3, 4
MRUN = 4


def context_steps(L, g):
    if L.kind == "attn" and L.cross:
        return [("kc", L, g, mt) for mt in range(KT)] + [("vc", L, g, c) for c in range(C)]
    if L.kind == "attn64":
        return ([("cln", L, g), ("cnb", L, g), ("ctr", L, g)] + [("k", L, g, mt) for mt in range(8)]
                + [("v", L, g, h) for h in range(2)])
    return []


WAIT = None


def before_scores(L, g):
    out = []
    if L.row:
        out.append(("xb", L, g))
    if L.pre:
        out += [("lna", L, g), WAIT, ("lnb", L, g), WAIT]
    if L.kind == "norm":
        return out + [("pna", L, g), WAIT, ("pnb", L, g), WAIT]
    out += [("trx", L, g), WAIT]
    if L.kind == "route":
        return out + [("rt1", L, g), ("rt2", L, g), ("rt3", L, g)]
    if L.kind in ("geglu", "gelu"):
        if g % 2 == 1:
            for m0 in range(0, FT, MRUN):
                run = range(m0, m0 + MRUN)
                out.append([(kind, L, g // 2, m) for kind in (("fg", "fa") if L.kind == "geglu" else ("fa",)) for m in run])
            out += [("f2", L, g - 1), ("f2", L, g)]
        return out
    nq = 8 if L.wide else KT
    own = not L.cross and not L.wide
    for mt in range(nq):
        out.append(("q", L, g, mt))
        if own:
            out.append(("k", L, g, mt))
        if mt:
            out.append(("ql", L, g, mt - 1))
    if own:
        out.append(("v", L, g))
    return out + [("ql", L, g, nq - 1)]


def turn_steps(layers):
    attn = [L for L in layers if L.kind in ("attn", "attn64")]
    slots = [(L, g, n) for L in attn for g in range(G) for n in range(len(L.groups))]
    first = {(L.name, g): slots.index((L, g, 0)) for L in attn for g in range(G)}
    steps = []
    queue = []

    def onward(i, g):
        out = []
        while i < len(layers):
            out += before_scores(layers[i], g)
            if layers[i] in attn:
                return out, first[layers[i].name, g]
            i += 1
        if layers[-1].kind == "route":
            out.append(("store", layers[-1], g))
        elif g % 2 == 1:
            out += [("store", layers[-1], g - 1), ("store", layers[-1], g)]
        return out, len(slots) + LAG_AV + 2

    def emit_due(slot):
        for q in list(queue):
            items, due, free_from = q
            if slot < free_from:
                continue
            left = max(1, due - slot)
            for _ in range(len(items) if due <= slot else -(-len(items) // left)):
                item = items.pop(0)
                if item is not WAIT:
                    steps.extend(item if isinstance(item, list) else [item])
            if not items:
                queue.remove(q)

    def emit_fills(slot):
        ahead, most = 0, 0
        for items, due, _ in fills:
            ahead += len(items)
            if ahead:
                most = max(most, ahead if due <= slot + 1 else -(-ahead // (due - slot - 1)))
        for items, due, free_from in fills:
            while items and most > 0 and slot >= free_from:
                steps.append(items.pop(0))
                most -= 1

    for g in range(G):
        queue.append((*onward(0, g), -1))
    fills = []
    for k, L in enumerate(attn):
        for g in range(G):
            items = context_steps(L, g)
            if items:
                after = 0
                if L.cross and any(a.wide for a in attn[:k]):
                    wide = next(a for a in attn if a.wide)
                    after = first[wide.name, g] + len(wide.groups) + LAG_AV
                fills.append((items, first[L.name, g], after))
    for s in range(len(slots) + LAG_AV + 2):
        emit_due(s)
        emit_fills(s)
        if s < len(slots):
            steps.append(("qk",) + slots[s])
        if 0 <= s - LAG_SPLIT < len(slots):
            steps.append(("sp",) + slots[s - LAG_SPLIT])
        if 0 <= s - LAG_ROUND < len(slots) and slots[s - LAG_ROUND][0].quant:
            steps.append(("sr",) + slots[s - LAG_ROUND])
        if 0 <= s - LAG_TURN < len(slots):
            steps.append(("tp",) + slots[s - LAG_TURN])
        if 0 <= s - LAG_AV < len(slots):
            L, g, n = slots[s - LAG_AV]
            steps.append(("av", L, g, n))
            halves = 2 if L.wide else 1
            per = len(L.groups) // halves
            if (n + 1) % per == 0:
                half = n // per
                steps.append(("fin", L, g, half))
                out = [WAIT, ("tro", L, g, half)]
                due = s + 1
                if half == halves - 1:
                    out += [WAIT, ("wo", L, g), WAIT]
                    if L.post:
                        out += [("pna", L, g), WAIT, ("pnb", L, g), WAIT]
                    more, due = onward(layers.index(L) + 1, g)
                    out += more
                queue.append((out, due, -1))
    emit_due(len(slots) + LAG_AV + 2)
    return steps


PSUM_STEPS = {"kc", "vc", "ctr", "k", "v", "q", "trx", "tro", "wo", "fg", "fa", "f2", "rt1", "rt2", "rt3"}
KEYS = ("kc", "vc", "k", "v", "q")


class Turn:

    def __init__(self, layers):
        self.steps = turn_steps(layers)
        self.layers = layers
        self.psum, self.at, self.count = {}, {}, {}
        self.raw, self.raw_users = {}, []
        self.plain, self.whole, self.scaled = {}, {}, {}
        self.quant, self.split, self.group, self.obank = {}, {}, {}, {}
        for st in self.steps:
            kind, L = st[0], st[1]
            key = (kind, L.name) + st[2:]
            if kind in PSUM_STEPS:
                self.psum[key] = len(self.psum)
            self.at[key] = self.count.get(kind, 0)
            self.count[kind] = self.at[key] + 1
            if L.quant and kind in KEYS:
                self.quant[key] = len(self.quant)
            elif kind in KEYS:
                same = [k for k in self.split if (k[0] == "q") == (kind == "q")]
                self.split[key] = len(same)
            if kind == "qk":
                self.group[key[1:]] = len(self.group)
                if not L.quant:
                    self.plain[key[1:]] = len(self.plain)
                else:
                    self.whole[key[1:]] = len(self.whole)
                    if L.cross:
                        self.scaled[key[1:]] = len(self.scaled)
            if kind in KEYS and L.quant:
                self.raw[key] = len(self.raw)
                self.raw_users.append(key)
            if kind == "fin":
                self.obank[key[1:]] = len(self.obank)
        self.lnorm, n = {}, 0
        for st in self.steps:
            if st[0] in ("lna", "cln", "pna"):
                self.lnorm[(st[0], st[1].name) + st[2:]] = n
                n += 1
        self.mask_dve, self.mask_pool = {}, {}
        for st in self.steps:
            if st[0] == "ql":
                key = ("ql", st[1].name) + st[2:]
                if not (st[1].quant and st[3] == 1):
                    self.mask_dve[key] = len(self.mask_dve)
                if not st[1].wide and not (st[1].quant and st[3] == 0):
                    self.mask_pool[key] = len(self.mask_pool)
        self.raw_before, last_q = {}, {}
        for st in self.steps:
            if st[0] == "q":
                self.raw_before[("q", st[1].name) + st[2:]] = last_q.get((st[2], st[3] % 2))
                last_q[st[2], st[3] % 2] = ("ql", st[1].name) + st[2:]
        self.xn = {}
        for st in self.steps:
            if st[0] in ("lnb", "cnb"):
                self.xn[(st[0], st[1].name) + st[2:]] = len(self.xn)


PASSES = [PASS1, PASS3, PASS4]


def network(nc, t, out):
    with ExitStack() as ctx:
        def sb(name, shape, dt=F32):
            return ctx.enter_context(nc.sbuf_tensor(name, shape, dt))

        def sem(name):
            return ctx.enter_context(nc.semaphore(name))

        hT_d = nc.dram_tensor("moe_in_T", (128, KT, B * T), F32, kind="Internal").ap()
        acc_d = nc.dram_tensor("moe_acc", (B, T, D), F32, kind="Internal").ap()
        comb_d = nc.dram_tensor("moe_combine", (B, T, E), F32, kind="Internal").ap()
        x_d = nc.dram_tensor("after_L1", (B, T, D), F32, kind="Internal").ap()

        ident = sb("ident", [128, 128])
        ident16 = sb("ident16", [128, 128], BF16)
        identh = sb("identh", [128, 128], F16)
        causal16 = sb("causal16", [T, 4 * T], BF16)
        cols = sb("cols", [128, NCOL])
        neghalf = sb("neghalf", [128, 1])
        dinv = sb("dinv", [128, 8])
        dmul = sb("dmul", [128, 4])
        w1_ctx = ctx.enter_context(ExitStack())
        iota = w1_ctx.enter_context(nc.sbuf_tensor("iota", [T, E], F32))
        rb_row = w1_ctx.enter_context(nc.sbuf_tensor("rb_row", [T, E], F32))
        eb2 = w1_ctx.enter_context(nc.sbuf_tensor("eb2", [E, D], F32))

        def col(name, i=0):
            return cols[:, COLS[name][0] + i:COLS[name][0] + i + 1]

        head_mask = [col("head_masks", h8) for h8 in range(8)]
        head_masks = cols[:, COLS["head_masks"][0]:COLS["head_masks"][0] + 8]
        d_names = ["L1_xattn_d_q1", "L1_xattn_d_k1", "L1_xattn_d_v1", "L1_xattn_d_w1",
                   "L1_xattn_d_q2", "L1_xattn_d_k2", "L1_xattn_d_v2", "L1_xattn_d_w2"]

        const_in = sem("const_in")
        ready = sem("ready")
        with nc.Block() as block:
            @block.sync
            def _(sp):
                loads = [(ident[:], t["ident"]), (ident16[:], t["ident16"]), (identh[:], t["identh"]), (causal16[:], t["causal16"]),
                         (iota[:], t["iota"]), (cols[:], t["cols"]),
                         (rb_row[:], t["L0_xattn_router_b"].rearrange("(o e) -> o e", o=1).to_broadcast([T, E])),
                         (eb2[:], t["L0_xattn_e_b2"])]
                for dst, src in loads:
                    sp.dma_start(dst, src).then_inc(const_in, 16)
                sp.wait_ge(const_in, 16 * len(loads))

            @block.vector
            def _(dve):
                dve.memset(neghalf[:], -0.5)
                dve.wait_ge(const_in, 16 * 8)
                d0 = COLS["L1_xattn_d_q1"][0]
                dve.reciprocal(dinv[:], cols[:, d0:d0 + 8]).then_inc(ready, 1)
                for i in range(2):
                    dve.tensor_scalar(dmul[:, 2 * i:2 * i + 1], col(d_names[4 * i]), col(d_names[4 * i + 1]),
                                      HD ** -0.5, ALU.mult, ALU.mult)
                    dve.tensor_scalar(dmul[:, 2 * i + 1:2 * i + 2], col(d_names[4 * i + 2]),
                                      col(d_names[4 * i + 3]), None, ALU.mult)

        env = locals()
        with w1_ctx:
            attention_pass(nc, t, 0, env, pass_weights(nc, t, 0, w1_ctx, True), out)
        with ExitStack() as w4_ctx:
            w4 = pass_weights(nc, t, 2, w4_ctx, False)
            with ExitStack() as w3_ctx:
                w3 = pass_weights(nc, t, 1, w3_ctx, False)
                experts_pass(nc, t, env, w3, w4["tiles"])
                with nc.Block() as block:
                    @block.sync
                    def _(sp):
                        load_weights(sp, t, w4)
                attention_pass(nc, t, 1, env, w3, out)
            attention_pass(nc, t, 2, env, w4, out)


def pass_weights(nc, t, which, ctx, load):
    pre = f"p{which}_"
    used = []
    for L in PASSES[which]:
        for k, w in L.w.items():
            if not k.startswith("b") and w[0] not in used:
                used.append(w[0])
    if which == 0:
        used.append("L0_xattn_router_w")
    tiles = {n: ctx.enter_context(nc.sbuf_tensor(pre + n, [128, WEIGHTS[n][0] // 128, WEIGHTS[n][1]], F32)) for n in used}
    sems = {n: ctx.enter_context(nc.semaphore(pre + "in_" + n)) for n in used}
    r0, nrow = [(0, 6), (6, 5), (11, 4)][which]
    rows = ctx.enter_context(nc.sbuf_tensor(pre + "rows", [T, nrow, D], F32))
    row_in = ctx.enter_context(nc.semaphore(pre + "row_in"))
    w = dict(tiles=tiles, sems=sems, rows=rows, row_in=row_in, r0=r0, nrow=nrow)
    if load:
        with nc.Block() as block:
            @block.sync
            def _(sp):
                load_weights(sp, t, w)
    return w


def load_weights(sp, t, w):
    r0, nrow = w["r0"], w["nrow"]
    sp.dma_start(w["rows"][:], t["rows"][r0:r0 + nrow, :].rearrange("(o r) d -> o r d", o=1)
                 .to_broadcast([T, nrow, D])).then_inc(w["row_in"], 16)
    for n, tile in w["tiles"].items():
        sp.dma_start(tile[:], t[n].rearrange("(k p) n -> p k n", p=128)).then_inc(w["sems"][n], 16)


def attention_pass(nc, t, which, env, w, out):
    layers = PASSES[which]
    turn = Turn(layers)
    QUANT = which == 1
    L2IN = which == 2
    NRAW = 4 if QUANT else 2 * G
    halves = 1 if QUANT else 2
    ident, ident16, causal16, iota = env["ident"], env["ident16"], env["causal16"], env["iota"]
    cols, rb_row, eb2, neghalf = env["cols"], env["rb_row"], env["eb2"], env["neghalf"]
    identh = env["identh"]
    dinv, dmul, col = env["dinv"], env["dmul"], env["col"]
    head_mask, head_masks = env["head_mask"], env["head_masks"]
    hT_d, acc_d, comb_d = env["hT_d"], env["acc_d"], env["comb_d"]
    x_d = env["x_d"]
    weight, w_in = w["tiles"], w["sems"]
    pre = ["a_", "c_", "d_"][which]
    with ExitStack() as ctx:
        def sb(name, shape, dt=F32):
            return ctx.enter_context(nc.sbuf_tensor(pre + name, shape, dt))

        def sem(name):
            return ctx.enter_context(nc.semaphore(pre + name))

        def row(name):
            return w["rows"][:, ROWS[name] - w["r0"], :]

        x = sb("x", [T, G, D])
        xb = sb("xb", [T, G, D])
        xn = sb("xn", [T, G, D])
        hT = sb("hT", [128, KT, GT])
        cT = sb("cT", [128, KT, G, M])
        qm = sb("q_split", [128, G, halves, KT, 8, T], F16)
        qs = sb("q_halves", [128, G, halves, KT, T], F16)
        kS, vS = sb("kS", [128, halves, KT, GT], F16), sb("vS", [T, G, H, halves, HD], F16)
        raw = sb("raw", [128, NRAW, M if QUANT else T])
        nk, nv = halves * KT * M, halves * C * D
        kvC = sb("kvC", [128, G, max(nk + nv, 2 * 8 * T + 2 * H * HD2) if L2IN else nk + nv], F16)
        kC = [kvC[:, g, 0:nk].rearrange("p (l k m) -> p l k m", l=halves, k=KT) for g in range(G)]
        vC = [kvC[0:MC, g, nk:nk + nv].rearrange("p (c h l d) -> p c h l d", c=C, h=H, l=halves) for g in range(G)]
        stats = sb("stats", [T, 2 * G, 6])
        mv = sb("mv", [T, 2 * G, 2])
        nrm = sb("nrm", [T, 2 * G, 4])
        P = sb("P", [T, RP, 448])
        Ps = sb("P_split", [T, RP, 2 * 448 + 16], F16)
        PT = sb("PT", [MC, 2, 8 * T + 16], F16)
        negm = sb("negm", [T, 4, 4])
        sums = sb("sums", [T, G, H])
        rsum = sb("rsum", [T, G, H])
        Osb = sb("Osb", [T, 2, 512 if L2IN else D])
        OT = sb("OT", [128, 2, 8 if L2IN else KT, T])
        hf = [qm[:, 2 * pair:2 * pair + 2].rearrange("p g l k h n -> p (g l k h n)")[:, 0:2 * FT * PT2].bitcast(F32)
              .rearrange("p (m n) -> p m n", m=FT) for pair in range(G // 2)]
        if QUANT:
            qmb, qsb = qm[:].bitcast(BF16), qs[:].bitcast(BF16)
            kSb, vSb = kS[:, 0].bitcast(BF16), vS[:].rearrange("p g h l d -> p g (h l d)").bitcast(BF16)
            kCb = [k[:, 0].bitcast(BF16) for k in kC]
            vCb = [v.rearrange("p c h l d -> p c (h l d)").bitcast(BF16) for v in vC]
            Psb, PTb = Ps[:].bitcast(BF16), PT[:].bitcast(BF16)
            negs = sb("negs", [T, 4, 4])
            rq = sb("rq", [T, 4, 2, 4])
            gl = sb("gl", [128, MRUN, PT2])
        elif L2IN:
            q2 = [qm[:, g, 0].rearrange("p k h n -> p (k h n)").rearrange("p (m l n) -> p m l n", m=8, l=2)
                  for g in range(G)]
            k2 = [kvC[:, g, 0:2 * 8 * T].rearrange("p (m l n) -> p m l n", m=8, l=2) for g in range(G)]
            v2 = [kvC[0:T, g, 2 * 8 * T:2 * 8 * T + 2 * H * HD2].rearrange("p (l d) -> p l d", l=2) for g in range(G)]
            ctok = sb("ctok", [T, G, D])
            cnT = sb("cnT", [128, KT, GT])
        else:
            lg, ex, pr = sb("lg", [T, G, E]), sb("ex", [T, G, E]), sb("pr", [T, G, E])
            rt = sb("rt", [T, G, 8])
            top = sb("top", [T, G, 8])
            topi = sb("topi", [T, G, 8], U32)
            topf = sb("topf", [T, G, 8])
            c1, c2, comb = sb("c1", [T, G, E]), sb("c2", [T, G, E]), sb("comb", [T, G, E])
            cbT = sb("cbT", [E, G, T])
            acc = sb("acc", [T, G, D])

        def pb(name):
            return ctx.enter_context(nc.psum_tensor(pre + name, [128, 512], F32))

        mp = [pb(f"mix{i}") for i in range(2)]
        Sb = [pb(f"scores{i}") for i in range(3)]
        Tb = [ctx.enter_context(nc.psum_tensor(pre + f"probsT{i}", [128, 1024], F16)) for i in range(2)]
        Tbb = [b[:].bitcast(BF16) for b in Tb]
        Ob = pb("attnout")

        names = ["x_in", "ctx_in", "stored", "mp_full", "mp_free0", "mp_free1", "s_full", "max_done", "exp_done",
                 "sp_hi", "split_lo", "split_int", "rq_done", "scaled", "kv_hi", "q_hi", "q_dve", "q_pool", "q_sub", "tp_done", "pt_done", "av_done", "fin_done", "x_done", "xb_done", "stat_done",
                 "rstd_done", "xn_done", "ln_half", "dve_chain", "act_chain", "clipped", "int_done",
                 "gate_done", "rt_sum", "rt_exp", "rt_gap", "rt_w", "comb_done"]
        s = {n: sem(n) for n in names}
        mp_free = [s["mp_free0"], s["mp_free1"]]

        def drained(eng, key):
            u = turn.psum[key]
            eng.wait_ge(mp_free[u % 2], u // 2 + 1)

        def bank_free(eng, u):
            if u >= 2:
                eng.wait_ge(mp_free[u % 2], u // 2)

        def filled(eng, key):
            eng.wait_ge(s["mp_full"], turn.psum[key] + 1)

        def drain_mark(key):
            return mp_free[turn.psum[key] % 2]

        def x_ready(eng, i, g):
            if i == 0:
                eng.wait_ge(s["x_in"], 16 * G)
            elif layers[i - 1].post:
                eng.wait_ge(s["x_done"], turn.at["pnb", layers[i - 1].name, g] + 1)
            else:
                drained(eng, ("wo" if "o" in layers[i - 1].w else "f2", layers[i - 1].name, g))

        def index(L):
            return layers.index(L)

        def gpos(L, g, n):
            return turn.group[L.name, g, n]

        by_pos = {v: (next(L for L in layers if L.name == k[0]), k[1], k[2]) for k, v in turn.group.items()}

        def heads(L, n):
            return L.groups[n]

        def norm_slot(key):
            return key[2] + (G if key[0] == "cln" else 0)

        def shapes(L):
            return (MC, C) if L.cross else (T, 1)

        def wtile(w, kt, c0, n):
            return weight[w[0]][:, kt, w[1] + c0:w[1] + c0 + n]

        def operand(eng, key, L):
            if L.quant:
                eng.wait_ge(s["int_done"], turn.quant[key] + 1)
            else:
                drained(eng, key)

        def raw_free(eng, key, L):
            if L.quant:
                r = turn.raw[key]
                if r >= NRAW:
                    eng.wait_ge(s["int_done"], turn.quant[turn.raw_users[r - NRAW]] + 1)
            elif turn.raw_before[key]:
                eng.wait_ge(s["q_dve"], turn.mask_dve[turn.raw_before[key]] + 1)

        def raw_slot(key, L):
            if L.quant:
                return raw[:, turn.raw[key] % NRAW]
            return raw[:, 2 * key[2] + key[3] % 2]

        def quant_dst(kind, a):
            if kind == "q":
                return T, qsb[:, a[0], 0, a[1], :]
            if kind == "k":
                return T, kSb[:, a[1], a[0] * T:(a[0] + 1) * T]
            if kind == "v":
                return D, vSb[:, a[0], :]
            if kind == "kc":
                return M, kCb[a[0]][:, a[1], :]
            return D, vCb[a[0]][:, a[1], :]

        def kv_split(key, L):
            kind, a = key[0], key[2:]
            bank = mp[turn.psum[key] % 2]
            if kind == "k":
                g, mt = a
                lo_hi = [k2[g][:, mt, l, :] if L.wide else kS[:, l, mt, g * T:(g + 1) * T] for l in range(2)]
                return bank[:, 0:T], *lo_hi, col(L.w["bk"][0], L.w["bk"][1] + mt)
            if kind == "kc":
                g, mt = a
                return bank[:, 0:M], kC[g][:, 0, mt, :], kC[g][:, 1, mt, :], col(L.w["bk"][0], L.w["bk"][1] + mt)
            if L.wide:
                g, h = a
                return bank[0:T, 0:512], v2[g][:, 0, h * 512:(h + 1) * 512], v2[g][:, 1, h * 512:(h + 1) * 512], None
            np_, dst = (T, vS[:, a[0]]) if kind == "v" else (MC, vC[a[0]][:, a[1]])
            return bank[0:np_, 0:D].rearrange("p (h d) -> p h d", h=H), dst[:, :, 0, :], dst[:, :, 1, :], None

        def split_ready(eng, L, g, n):
            if L.quant:
                eng.wait_ge(s["split_int"], turn.whole[L.name, g, n] + 1)
            else:
                eng.wait_ge(s["split_lo"], turn.plain[L.name, g, n] + 1)

        with nc.Block() as block:
            @block.vector
            def _(dve):
                dve.memset(Ps[:], 0.0)
                dve.memset(PT[:], 0.0)

            @block.sync
            def _(sp):
                sp.wait_ge(w["row_in"], 16)

        with nc.Fori(0, TURNS) as turn_no:
            with nc.Block() as block:
                @block.sync
                def _(sp):
                    src = [t["x"], acc_d, x_d][which]
                    for g in range(G):
                        b = bass.ds(turn_no * G + g, 1)
                        sp.dma_start(x[:, g, :], src[b, :, :].rearrange("o p n -> (o p) n")).then_inc(s["x_in"], 16)
                    for g in range(G):
                        b = bass.ds(turn_no * G + g, 1)
                        sp.dma_start(cT[:, :, g, :], t["ctxT"][b, :, :].rearrange("o (k p) m -> (o p) k m", p=128)
                                     ).then_inc(s["ctx_in"], 16)
                        if L2IN:
                            sp.dma_start(ctok[:, g, :], t["ctx_1024"][b, 0:T, :].rearrange("o p n -> (o p) n")
                                         ).then_inc(s["ctx_in"], 16)
                    stores = 0
                    for st in turn.steps:
                        if st[0] != "store":
                            continue
                        g = st[2]
                        b = bass.ds(turn_no * G + g, 1)
                        if which:
                            x_ready(sp, len(layers), g)
                            dst = out if L2IN else x_d
                            sp.dma_start(dst[b, :, :].rearrange("o p n -> (o p) n"), x[:, g, :]).then_inc(s["stored"], 16)
                            stores += 1
                        else:
                            drained(sp, ("rt3", "route", g))
                            sp.wait_ge(s["comb_done"], g + 1)
                            sp.dma_start(acc_d[b, :, :].rearrange("o p n -> (o p) n"), acc[:, g, :]).then_inc(s["stored"], 16)
                            sp.dma_start(comb_d[b, :, :].rearrange("o p n -> (o p) n"), comb[:, g, :]).then_inc(s["stored"], 16)
                            stores += 2
                    if not which:
                        for g in range(G):
                            drained(sp, ("trx", "route", g))
                        sp.dma_start(hT_d[:, :, bass.ds(turn_no * GT, GT)], hT[:]).then_inc(s["stored"], 16)
                        stores += 1
                    sp.wait_ge(s["stored"], 16 * stores)

                @block.tensor
                def _(pe):
                    for st in turn.steps:
                        kind, L, a = st[0], st[1], st[2:]
                        key = (kind, L.name) + a
                        i = index(L)
                        if kind in PSUM_STEPS:
                            u = turn.psum[key]
                            bank = mp[u % 2]
                            bank_free(pe, u)
                        if kind == "trx":
                            g, = a
                            if L.pre:
                                pe.wait_ge(s["xn_done"], turn.xn["lnb", L.name, g] + 1)
                            else:
                                x_ready(pe, i, g)
                            src = xn if L.pre else x
                            for kt in range(KT):
                                last = pe.transpose(bank[:, kt * T:(kt + 1) * T], src[:, g, kt * 128:(kt + 1) * 128],
                                                    ident[0:T, 0:T])
                            last.then_inc(s["mp_full"], 1)
                        elif kind == "ctr":
                            g, = a
                            pe.wait_ge(s["xn_done"], turn.xn["cnb", L.name, g] + 1)
                            for kt in range(KT):
                                last = pe.transpose(bank[:, kt * T:(kt + 1) * T], ctok[:, g, kt * 128:(kt + 1) * 128],
                                                    ident[0:T, 0:T])
                            last.then_inc(s["mp_full"], 1)
                        elif kind in ("fa", "fg"):
                            pair, m = a
                            for g in (2 * pair, 2 * pair + 1):
                                drained(pe, ("trx", L.name, g))
                            pe.wait_ge(w_in[L.w["w1"][0]], 16)
                            c0 = m * 128 + (FF if kind == "fg" else 0)
                            for kt in range(KT):
                                last = pe.matmul(bank[:, 0:PT2], wtile(L.w["w1"], kt, c0, 128),
                                                 hT[:, kt, pair * PT2:(pair + 1) * PT2], start=kt == 0, stop=kt == KT - 1)
                            last.then_inc(s["mp_full"], 1)
                        elif kind in ("q", "k"):
                            g, m = a
                            src = hT
                            if L.wide and kind == "k":
                                src = cnT
                                drained(pe, ("ctr", L.name, g))
                            else:
                                drained(pe, ("trx", L.name, g))
                            pe.wait_ge(w_in[L.w[kind][0]], 16)
                            c0 = m * 128
                            for kt in range(KT):
                                last = pe.matmul(bank[:, 0:T], wtile(L.w[kind], kt, c0, 128), src[:, kt, g * T:(g + 1) * T],
                                                 start=kt == 0, stop=kt == KT - 1)
                            last.then_inc(s["mp_full"], 1)
                        elif kind == "v":
                            g = a[0]
                            c0, n = (a[1] * 512, 512) if L.wide else (0, D)
                            src = cnT if L.wide else hT
                            drained(pe, ("ctr" if L.wide else "trx", L.name, g))
                            pe.wait_ge(w_in[L.w["v"][0]], 16)
                            for kt in range(KT):
                                last = pe.matmul(bank[0:T, 0:n], src[:, kt, g * T:(g + 1) * T],
                                                 wtile(L.w["v"], kt, c0, n), start=kt == 0, stop=kt == KT - 1)
                            last.then_inc(s["mp_full"], 1)
                        elif kind == "kc":
                            g, mt = a
                            pe.wait_ge(s["ctx_in"], 16 * G * (2 if L2IN else 1))
                            pe.wait_ge(w_in[L.w["k"][0]], 16)
                            for kt in range(KT):
                                last = pe.matmul(bank[:, 0:M], wtile(L.w["k"], kt, mt * 128, 128), cT[:, kt, g, :],
                                                 start=kt == 0, stop=kt == KT - 1)
                            last.then_inc(s["mp_full"], 1)
                        elif kind == "vc":
                            g, c = a
                            pe.wait_ge(s["ctx_in"], 16 * G * (2 if L2IN else 1))
                            pe.wait_ge(w_in[L.w["v"][0]], 16)
                            for kt in range(KT):
                                last = pe.matmul(bank[0:MC, 0:D], cT[:, kt, g, c * MC:(c + 1) * MC],
                                                 wtile(L.w["v"], kt, 0, D), start=kt == 0, stop=kt == KT - 1)
                            last.then_inc(s["mp_full"], 1)
                        elif kind == "qk":
                            g, n = a
                            j = gpos(L, g, n)
                            if j >= 3:
                                pe.wait_ge(s["exp_done"], j - 2)
                            if n == 0:
                                nq = 8 if L.wide else KT
                                last_dve = max(turn.mask_dve.get(("ql", L.name, g, mt), -1) for mt in range(nq))
                                last_pool = max(turn.mask_pool.get(("ql", L.name, g, mt), -1) for mt in range(nq))
                                pe.wait_ge(s["q_dve"], last_dve + 1)
                                if last_pool >= 0:
                                    pe.wait_ge(s["q_pool"], last_pool + 1)
                                for mt in range(8 if L.wide else KT):
                                    operand(pe, ("kc" if L.cross else "k", L.name, g, mt), L)
                            Sx = Sb[j % 3]
                            kk = M if L.cross else T
                            if L.causal:
                                pe.matmul(Sx[0:T, 0:4 * T], ident16[0:T, 0:T], causal16[:], start=True, stop=False)
                            for hi, h in enumerate(heads(L, n)):
                                o = Sx[0:T, hi * kk:(hi + 1) * kk]
                                gs = slice(g * T, (g + 1) * T)
                                mt, par = h // (2 if L.wide else 8), h % 2
                                if L.wide:
                                    r = slice(64 * par, 64 * par + 64)
                                    q = lambda l: q2[g][r, mt, l, :]
                                    k = lambda l: k2[g][r, mt, l, :]
                                else:
                                    if L.quant:
                                        q = lambda l: qmb[:, g, 0, mt, h % 8, :]
                                        k = lambda l: kCb[g][:, mt, :] if L.cross else kSb[:, mt, gs]
                                    else:
                                        q = lambda l: qm[:, g, l, mt, h % 8, :]
                                        k = lambda l: kC[g][:, l, mt, :] if L.cross else kS[:, l, mt, gs]
                                terms = [(0, 0)] if L.quant else [(0, 0), (0, 1), (1, 0)]
                                for ti, (lq, lk) in enumerate(terms):
                                    last = pe.matmul(o, q(lq), k(lk), start=ti == 0 and not L.causal,
                                                     stop=ti == len(terms) - 1 and
                                                     (not L.causal or hi == len(heads(L, n)) - 1))
                            last.then_inc(s["s_full"], 1)
                        elif kind == "tp":
                            g, n = a
                            j = gpos(L, g, n)
                            split_ready(pe, L, g, n)
                            if j >= 2:
                                pe.wait_ge(s["pt_done"], j - 1)
                            kk, nch = shapes(L)
                            nb = nch * len(heads(L, n))
                            for b_ in range(nb if L.quant else 2 * nb):
                                src, dst, one = (Psb, Tbb, ident16) if L.quant else (Ps, Tb, identh)
                                at = b_ * kk
                                last = pe.transpose(dst[j % 2][:, b_ * T:(b_ + 1) * T],
                                                    src[:, j % RP, at:at + 128], one[0:T, 0:T])
                            last.then_inc(s["tp_done"], 1)
                        elif kind == "av":
                            g, n = a
                            j = gpos(L, g, n)
                            half = n // 2 if L.wide else 0
                            ou = turn.obank[L.name, g, half]
                            if n % 2 == 0 and L.wide or n == 0:
                                if ou >= 1:
                                    pe.wait_ge(s["fin_done"], ou)
                                if L.cross:
                                    for c in range(C):
                                        operand(pe, ("vc", L.name, g, c), L)
                                elif L.wide:
                                    for hv in range(2):
                                        operand(pe, ("v", L.name, g, hv), L)
                                else:
                                    operand(pe, ("v", L.name, g), L)
                            pe.wait_ge(s["pt_done"], j + 1)
                            kk, nch = shapes(L)
                            pt = PTb if L.quant else PT
                            nb = nch * len(heads(L, n))
                            for hi, h in enumerate(heads(L, n)):
                                for c in range(nch):
                                    if L.wide:
                                        ho = h - 8 * half
                                        o = Ob[:, ho * HD2:(ho + 1) * HD2]
                                        parts = [(0, v2[g][:, 0, h * HD2:(h + 1) * HD2]),
                                                 (0, v2[g][:, 1, h * HD2:(h + 1) * HD2]),
                                                 (1, v2[g][:, 0, h * HD2:(h + 1) * HD2])]
                                    elif L.quant:
                                        o = Ob[:, h * HD:(h + 1) * HD]
                                        vv = vCb[g][:, c, h * HD:(h + 1) * HD] if L.cross else vSb[:, g, h * HD:(h + 1) * HD]
                                        parts = [(0, vv)]
                                    else:
                                        o = Ob[:, h * 2 * HD:(h + 1) * 2 * HD]
                                        vv = vC[g][:, c, h] if L.cross else vS[:, g, h]
                                        vv = vv.rearrange("p l d -> p (l d)")
                                        parts = [(0, vv), (1, vv)]
                                    for pi, (l, vv) in enumerate(parts):
                                        b_ = l * nb + hi * nch + c
                                        last = pe.matmul(o, pt[0:kk, j % 2, b_ * T:b_ * T + 128], vv,
                                                         start=c == 0 and pi == 0,
                                                         stop=c == nch - 1 and pi == len(parts) - 1)
                            last.then_inc(s["av_done"], 1)
                        elif kind == "tro":
                            g, half = a
                            ou = turn.obank[L.name, g, half]
                            pe.wait_ge(s["fin_done"], ou + 1)
                            for kt in range(4 if L.wide else KT):
                                last = pe.transpose(bank[:, kt * T:(kt + 1) * T],
                                                    Osb[:, ou % 2, kt * 128:(kt + 1) * 128], ident[0:T, 0:T])
                            last.then_inc(s["mp_full"], 1)
                        elif kind == "wo":
                            g, = a
                            nk = 8 if L.wide else KT
                            for half in range(2 if L.wide else 1):
                                drained(pe, ("tro", L.name, g, half))
                            pe.wait_ge(w_in[L.w["o"][0]], 16)
                            for kt in range(nk):
                                last = pe.matmul(bank[0:T, 0:D], OT[:, g % 2, kt, :], wtile(L.w["o"], kt, 0, D),
                                                 start=kt == 0, stop=kt == nk - 1)
                            last.then_inc(s["mp_full"], 1)
                        elif kind == "f2":
                            g, = a
                            for m in (FT - 2, FT - 1):
                                drained(pe, ("fa", L.name, g // 2, m))
                            pe.wait_ge(w_in[L.w["w2"][0]], 16)
                            for m in range(FT):
                                last = pe.matmul(bank[0:T, 0:D], hf[g // 2][:, m, (g % 2) * T:(g % 2 + 1) * T],
                                                 wtile(L.w["w2"], m, 0, D), start=m == 0, stop=m == FT - 1)
                            last.then_inc(s["mp_full"], 1)
                        elif kind == "rt1":
                            g, = a
                            drained(pe, ("trx", L.name, g))
                            pe.wait_ge(w_in["L0_xattn_router_w"], 16)
                            for kt in range(KT):
                                last = pe.matmul(bank[0:T, 0:E], hT[:, kt, g * T:(g + 1) * T],
                                                 weight["L0_xattn_router_w"][:, kt, :], start=kt == 0, stop=kt == KT - 1)
                            last.then_inc(s["mp_full"], 1)
                        elif kind == "rt2":
                            g, = a
                            pe.wait_ge(s["comb_done"], g + 1)
                            pe.transpose(bank[0:E, 0:T], comb[:, g, :], ident[0:T, 0:T]).then_inc(s["mp_full"], 1)
                        elif kind == "rt3":
                            g, = a
                            drained(pe, ("rt2", L.name, g))
                            pe.matmul(bank[0:T, 0:D], cbT[:, g, :], eb2[:], start=True, stop=True).then_inc(s["mp_full"], 1)

                @block.scalar
                def _(act):
                    for st in turn.steps:
                        kind, L, a = st[0], st[1], st[2:]
                        key = (kind, L.name) + a
                        if kind in KEYS and L.quant:
                            n, dst = quant_dst(kind, a)
                            act.wait_ge(s["clipped"], turn.quant[key] + 1)
                            act.activation(dst, raw_slot(key, L)[0:dst.shape[0], 0:n], ACT.Copy, bias=-MAGIC
                                           ).then_inc(s["int_done"], 1)
                        elif kind in ("k", "kc", "v", "vc") and not L.quant:
                            src, hi, _, bias = kv_split(key, L)
                            filled(act, key)
                            if bias is None:
                                ins = act.activation(hi, src, ACT.Copy)
                            else:
                                ins = act.activation(hi, src, ACT.Identity, bias=bias)
                            ins.then_inc(s["kv_hi"], 1)
                        elif kind == "q" and not L.quant:
                            g, mt = a
                            drained(act, key)
                            dst = q2[g][:, mt, 0, :] if L.wide else qs[:, g, 0, mt, :]
                            last = act.activation(dst, raw_slot(key, L)[:, 0:T], ACT.Copy)
                            last.then_inc(s["q_hi"], 1)
                        elif kind == "qk":
                            g, n = a
                            j = gpos(L, g, n)
                            act.wait_ge(s["max_done"], j + 1)
                            if j >= RP:
                                split_ready(act, *by_pos[j - RP])
                            kk = M if L.cross else T
                            for hi, h in enumerate(heads(L, n)):
                                cs = slice(hi * kk, (hi + 1) * kk)
                                m_ = negs if L.quant else negm
                                sc = dmul[0:T, 2 * (L.quant - 1):2 * (L.quant - 1) + 1] if L.quant else 1.0
                                last = act.activation(P[:, j % RP, cs], Sb[j % 3][0:T, cs], ACT.Exp,
                                                      bias=m_[:, j % 4, hi:hi + 1], scale=sc,
                                                      accum_out=sums[:, g, h:h + 1])
                            last.then_inc(s["exp_done"], 1)
                        elif kind == "sp" and L.cross:
                            g, n = a
                            j = gpos(L, g, n)
                            act.wait_ge(s["exp_done"], j + 1)
                            if L.quant:
                                act.wait_ge(s["rq_done"], turn.scaled[L.name, g, n] + 1)
                                act.activation(P[:, j % RP, 0:M], P[:, j % RP, 0:M], ACT.Copy, bias=MAGIC,
                                               scale=rq[:, j % 4, 1, 0:1]).then_inc(s["scaled"], 1)
                            else:
                                if j >= RP:
                                    act.wait_ge(s["tp_done"], j - RP + 1)
                                act.activation(Ps[:, j % RP, 0:M], P[:, j % RP, 0:M], ACT.Copy).then_inc(s["sp_hi"], 1)
                        elif kind == "fg":
                            g, m = a
                            filled(act, key)
                            if turn.at[key] >= MRUN:
                                drained(act, ("fa", L.name) + divmod(turn.at[key] - MRUN, FT))
                            act.activation(gl[:, m % MRUN, :], mp[turn.psum[key] % 2][:, 0:PT2], ACT.Gelu,
                                           bias=col(L.w["b1"][0], FT + m)).then_inc(drain_mark(key), 1)
                        elif kind == "fa" and L.kind == "gelu":
                            g, m = a
                            filled(act, key)
                            act.activation(hf[g][:, m, :], mp[turn.psum[key] % 2][:, 0:PT2], ACT.Gelu,
                                           bias=col(L.w["b1"][0], m)).then_inc(drain_mark(key), 1)
                        elif kind == "rt1":
                            g, = a
                            act.wait_ge(s["rt_sum"], g + 1)
                            act.activation(ex[:, g, :], lg[:, g, :], ACT.Exp, bias=rt[:, g, 0:1],
                                           accum_out=rt[:, g, 1:2]).then_inc(s["rt_exp"], 1)
                            act.wait_ge(s["rt_gap"], g + 1)
                            act.activation(rt[:, g, 4:5], rt[:, g, 3:4], ACT.Exp).then_inc(s["rt_w"], 1)
                        elif kind == "rt2":
                            g, = a
                            filled(act, key)
                            act.activation(cbT[:, g, :], mp[turn.psum[key] % 2][0:E, 0:T], ACT.Copy
                                           ).then_inc(drain_mark(key), 1)

                @block.gpsimd
                def _(pool):
                    for st in turn.steps:
                        kind, L, a = st[0], st[1], st[2:]
                        key = (kind, L.name) + a
                        if kind == "xb":
                            g, = a
                            x_ready(pool, index(L), g)
                            pool.tensor_tensor(xb[:, g, :], x[:, g, :], row(L.row), ALU.add
                                               ).then_inc(s["xb_done"], 1)
                        elif kind == "ql" and key in turn.mask_pool:
                            g, mt = a
                            if L.quant:
                                operand(pool, ("q", L.name, g, mt), L)
                                src, dst = qsb[:, g, 0, mt, :], qmb[:, g, 0, mt]
                            else:
                                pool.wait_ge(s["q_sub"], turn.mask_pool[key] + 1)
                                src, dst = qs[:, g, 1, mt, :], qm[:, g, 1, mt]
                            pool.tensor_tensor(dst, src.unsqueeze(1).to_broadcast([128, 8, T]),
                                               head_masks.unsqueeze(2).to_broadcast([128, 8, T]), ALU.mult
                                               ).then_inc(s["q_pool"], 1)
                        elif kind in ("lna", "cln", "pna"):
                            ln, slot = turn.lnorm[key], norm_slot(key)
                            pool.wait_ge(s["stat_done"], ln + 1)
                            pool.tensor_scalar(nrm[:, slot, 0:1], mv[:, slot, 1:2], EPS, None, ALU.add
                                               ).then_inc(s["ln_half"], 1)
                            pool.wait_ge(s["ln_half"], ln + 1)
                            pool.tensor_tensor(nrm[:, slot, 1:2], nrm[:, slot, 0:1], neghalf[0:T, :], ALU.pow
                                               ).then_inc(s["rstd_done"], 1)
                        elif kind == "sp":
                            g, n = a
                            j = gpos(L, g, n)
                            w_ = len(heads(L, n)) * (M if L.cross else T)
                            if not L.quant:
                                pool.wait_ge(s["sp_hi"], turn.plain[L.name, g, n] + 1)
                                pool.tensor_tensor(Ps[:, j % RP, w_:2 * w_], P[:, j % RP, 0:w_], Ps[:, j % RP, 0:w_],
                                                   ALU.subtract).then_inc(s["split_lo"], 1)

                @block.vector
                def _(dve):
                    chain = [0]

                    def link(ins):
                        chain[0] += 1
                        ins.then_inc(s["dve_chain"], 1)
                        dve.wait_ge(s["dve_chain"], chain[0])

                    def statistics(src, key):
                        slot = norm_slot(key)
                        link(dve.bn_stats(stats[:, slot, :], src))
                        dve.bn_aggr(mv[:, slot, :], stats[:, slot, :]).then_inc(s["stat_done"], 1)

                    def refine(key):
                        ln, slot = turn.lnorm[key], norm_slot(key)
                        v = mv[:, slot, 1:2]
                        n = nrm[:, slot, :]
                        dve.wait_ge(s["rstd_done"], ln + 1)
                        link(dve.tensor_scalar(n[:, 2:3], v, EPS, n[:, 1:2], ALU.add, ALU.mult))
                        link(dve.tensor_scalar(n[:, 2:3], n[:, 2:3], n[:, 1:2], -0.5, ALU.mult, ALU.mult))
                        link(dve.tensor_scalar(n[:, 3:4], n[:, 2:3], 1.5, n[:, 1:2], ALU.add, ALU.mult))

                    def normalize(dst, src, key):
                        slot = norm_slot(key)
                        return dve.tensor_scalar(dst, src, mv[:, slot, 0:1], nrm[:, slot, 3:4],
                                                 ALU.subtract, ALU.mult)

                    for st in turn.steps:
                        kind, L, a = st[0], st[1], st[2:]
                        key = (kind, L.name) + a
                        i = index(L)
                        if kind in PSUM_STEPS:
                            bank = mp[turn.psum[key] % 2]
                        if kind == "ql" and L.quant:
                            g, mt = a
                            if key in turn.mask_dve:
                                operand(dve, ("q", L.name, g, mt), L)
                                for h8 in range(8):
                                    last = dve.tensor_scalar(qmb[:, g, 0, mt, h8, :], qsb[:, g, 0, mt, :],
                                                             head_mask[h8], None, ALU.mult)
                                last.then_inc(s["q_dve"], 1)
                        elif kind == "lna":
                            g, = a
                            x_ready(dve, i, g)
                            statistics(x[:, g, :], key)
                        elif kind == "lnb":
                            g, = a
                            norm = ("lna", L.name, g)
                            refine(norm)
                            normalize(xn[:, g, :], x[:, g, :], norm).then_inc(s["xn_done"], 1)
                        elif kind == "cln":
                            g, = a
                            dve.wait_ge(s["ctx_in"], 16 * G * 2)
                            statistics(ctok[:, g, :], key)
                        elif kind == "cnb":
                            g, = a
                            norm = ("cln", L.name, g)
                            refine(norm)
                            normalize(ctok[:, g, :], ctok[:, g, :], norm).then_inc(s["xn_done"], 1)
                        elif kind == "pna":
                            g, = a
                            if L.kind == "norm":
                                x_ready(dve, i, g)
                            else:
                                drained(dve, ("wo", L.name, g))
                            statistics(x[:, g, :], key)
                        elif kind == "pnb":
                            g, = a
                            norm = ("pna", L.name, g)
                            refine(norm)
                            link(normalize(x[:, g, :], x[:, g, :], norm))
                            link(dve.tensor_tensor(x[:, g, :], x[:, g, :], row(L.post[0]), ALU.mult))
                            dve.tensor_tensor(x[:, g, :], x[:, g, :], row(L.post[1]), ALU.add
                                              ).then_inc(s["x_done"], 1)
                        elif kind in ("trx", "ctr"):
                            g, = a
                            filled(dve, key)
                            dst = hT if kind == "trx" else cnT
                            if L.pre:
                                for kt in range(KT):
                                    last = dve.tensor_scalar(dst[:, kt, g * T:(g + 1) * T], bank[:, kt * T:(kt + 1) * T],
                                                             col(L.pre[0], kt), col(L.pre[1], kt), ALU.mult, ALU.add)
                            else:
                                last = dve.tensor_copy(dst[:, :, g * T:(g + 1) * T],
                                                       bank[:, 0:KT * T].rearrange("p (k n) -> p k n", k=KT))
                            last.then_inc(drain_mark(key), 1)
                        elif kind in KEYS and L.quant:
                            filled(dve, key)
                            raw_free(dve, key, L)
                            n, dst = quant_dst(kind, a)
                            np_ = dst.shape[0]
                            di = 4 * (L.quant - 1) + {"q": 0, "k": 1, "kc": 1, "v": 2, "vc": 2}[kind]
                            buf = raw_slot(key, L)[0:np_, 0:n]
                            dve.tensor_scalar(buf, bank[0:np_, 0:n], dinv[0:np_, di:di + 1], MAGIC,
                                              ALU.mult, ALU.add).then_inc(drain_mark(key), 1)
                            drained(dve, key)
                            dve.tensor_scalar(buf, buf, MAGIC - 128.0, MAGIC + 127.0, ALU.max, ALU.min
                                              ).then_inc(s["clipped"], 1)
                        elif kind in ("k", "kc", "v", "vc"):
                            src, hi, lo, bias = kv_split(key, L)
                            dve.wait_ge(s["kv_hi"], turn.split[key] + 1)
                            if bias is None:
                                ins = dve.tensor_tensor(lo, src, hi, ALU.subtract)
                            else:
                                ins = dve.scalar_tensor_tensor(lo, src, bias, hi, ALU.add, ALU.subtract)
                            ins.then_inc(drain_mark(key), 1)
                        elif kind == "q":
                            g, mt = a
                            filled(dve, key)
                            raw_free(dve, key, L)
                            bq = col(L.w["bq"][0], L.w["bq"][1] + mt)
                            dve.tensor_scalar(raw_slot(key, L)[:, 0:T], bank[:, 0:T], bq, (HD2 if L.wide else HD) ** -0.5,
                                              ALU.add, ALU.mult).then_inc(drain_mark(key), 1)
                        elif kind == "ql":
                            g, mt = a
                            raw_q = raw_slot(key, L)[:, 0:T]
                            dve.wait_ge(s["q_hi"], turn.split["q", L.name, g, mt] + 1)
                            if L.wide:
                                dve.tensor_tensor(q2[g][:, mt, 1, :], raw_q, q2[g][:, mt, 0, :], ALU.subtract
                                                  ).then_inc(s["q_dve"], 1)
                            else:
                                dve.tensor_tensor(qs[:, g, 1, mt, :], raw_q, qs[:, g, 0, mt, :], ALU.subtract
                                                  ).then_inc(s["q_sub"], 1)
                                for h8 in range(8):
                                    last = dve.tensor_scalar(qm[:, g, 0, mt, h8, :], qs[:, g, 0, mt, :], head_mask[h8],
                                                             None, ALU.mult)
                                last.then_inc(s["q_dve"], 1)
                        elif kind == "qk":
                            g, n = a
                            j = gpos(L, g, n)
                            nh = len(heads(L, n))
                            kk = M if L.cross else T
                            dve.wait_ge(s["s_full"], j + 1)
                            ins = dve.tensor_reduce(negm[:, j % 4, 0:nh],
                                                    Sb[j % 3][0:T, 0:nh * kk].rearrange("p (h k) -> p h k", h=nh),
                                                    AX.X, ALU.max, negate=True)
                            if L.quant:
                                link(ins)
                                qi = 2 * (L.quant - 1)
                                dve.tensor_scalar(negs[:, j % 4, 0:nh], negm[:, j % 4, 0:nh], dmul[0:T, qi:qi + 1], None,
                                                  ALU.mult).then_inc(s["max_done"], 1)
                            else:
                                ins.then_inc(s["max_done"], 1)
                        elif kind == "sp" and not L.quant:
                            if not L.cross:
                                g, n = a
                                j = gpos(L, g, n)
                                w_ = len(heads(L, n)) * T
                                dve.wait_ge(s["exp_done"], j + 1)
                                if j >= RP:
                                    dve.wait_ge(s["tp_done"], j - RP + 1)
                                dve.tensor_copy(Ps[:, j % RP, 0:w_], P[:, j % RP, 0:w_]).then_inc(s["sp_hi"], 1)
                        elif kind == "sp":
                            g, n = a
                            j = gpos(L, g, n)
                            nh = len(heads(L, n))
                            kk = M if L.cross else T
                            dw = dinv[0:T, 4 * L.quant - 1:4 * L.quant]
                            dve.wait_ge(s["exp_done"], j + 1)
                            for hi, h in enumerate(heads(L, n)):
                                last = dve.reciprocal(rq[:, j % 4, 0, hi:hi + 1], sums[:, g, h:h + 1])
                            link(last)
                            ins = dve.tensor_scalar(rq[:, j % 4, 1, 0:nh], rq[:, j % 4, 0, 0:nh], dw, None, ALU.mult)
                            if L.cross:
                                ins.then_inc(s["rq_done"], 1)
                            else:
                                link(ins)
                            if not L.cross:
                                for hi, h in enumerate(heads(L, n)):
                                    cs = slice(hi * kk, (hi + 1) * kk)
                                    last = dve.tensor_scalar(P[:, j % RP, cs], P[:, j % RP, cs], rq[:, j % 4, 1, hi:hi + 1],
                                                             MAGIC, ALU.mult, ALU.add)
                                link(last)
                        elif kind == "sr":
                            g, n = a
                            j = gpos(L, g, n)
                            w_ = len(heads(L, n)) * (M if L.cross else T)
                            if L.cross:
                                dve.wait_ge(s["scaled"], turn.scaled[L.name, g, n] + 1)
                            if j >= RP:
                                dve.wait_ge(s["tp_done"], j - RP + 1)
                            dve.tensor_scalar(Psb[:, j % RP, 0:w_], P[:, j % RP, 0:w_], MAGIC, 255.0,
                                              ALU.subtract, ALU.min).then_inc(s["split_int"], 1)
                        elif kind == "tp":
                            g, n = a
                            j = gpos(L, g, n)
                            kk, nch = shapes(L)
                            w_ = nch * len(heads(L, n)) * T * (1 if L.quant else 2)
                            dve.wait_ge(s["tp_done"], j + 1)
                            if j >= 2:
                                dve.wait_ge(s["av_done"], j - 1)
                            dve.tensor_copy(PT[0:kk, j % 2, 0:w_], Tb[j % 2][0:kk, 0:w_]).then_inc(s["pt_done"], 1)
                        elif kind == "fin":
                            g, half = a
                            ou = turn.obank[L.name, g, half]
                            last_group = (half + 1) * len(L.groups) // (2 if L.wide else 1) - 1
                            if ou >= 2:
                                prev = [k for k, v in turn.obank.items() if v == ou - 2][0]
                                dve.wait_ge(s["mp_full"], turn.psum[("tro",) + prev] + 1)
                            if L.quant:
                                dve.wait_ge(s["av_done"], gpos(L, g, last_group) + 1)
                                qi = 2 * (L.quant - 1) + 1
                                dve.tensor_scalar(Osb[:, ou % 2, 0:D], Ob[0:T, 0:D], dmul[0:T, qi:qi + 1], None,
                                                  ALU.mult).then_inc(s["fin_done"], 1)
                            else:
                                nh, hd = (8, HD2) if L.wide else (H, HD)
                                hs = slice(half * nh, half * nh + nh)
                                dve.wait_ge(s["exp_done"], gpos(L, g, last_group) + 1)
                                link(dve.reciprocal(rsum[:, g % 2, hs], sums[:, g, hs]))
                                dve.wait_ge(s["av_done"], gpos(L, g, last_group) + 1)
                                osb = Osb[:, ou % 2, 0:nh * hd].rearrange("p (h d) -> p h d", h=nh)
                                if L.wide:
                                    src = Ob[0:T, 0:nh * hd].rearrange("p (h d) -> p h d", h=nh)
                                else:
                                    src = osb
                                    link(dve.tensor_reduce(osb, Ob[0:T, 0:2 * nh * hd].rearrange(
                                        "p (h l d) -> p h d l", h=nh, l=2), AX.X, ALU.add))
                                dve.tensor_tensor(osb, src, rsum[:, g % 2, hs].unsqueeze(2).to_broadcast([T, nh, hd]),
                                                  ALU.mult).then_inc(s["fin_done"], 1)
                        elif kind == "tro":
                            g, half = a
                            nk = 4 if L.wide else KT
                            filled(dve, key)
                            dst = OT[:, g % 2, half * nk:(half + 1) * nk, :]
                            src = bank[:, 0:nk * T].rearrange("p (k n) -> p k n", k=nk)
                            if "bv" in L.w:
                                c0 = COLS[L.w["bv"][0]][0] + L.w["bv"][1] + half * nk
                                ins = dve.tensor_tensor(dst, src, cols[:, c0:c0 + nk].unsqueeze(2).to_broadcast([128, nk, T]),
                                                        ALU.add)
                            else:
                                ins = dve.tensor_copy(dst, src)
                            ins.then_inc(drain_mark(key), 1)
                        elif kind in ("wo", "f2"):
                            g, = a
                            filled(dve, key)
                            dve.wait_ge(s["xb_done"], turn.at["xb", L.name, g] + 1)
                            dve.tensor_tensor(x[:, g, :], bank[0:T, 0:D], xb[:, g, :], ALU.add
                                              ).then_inc(drain_mark(key), 1)
                        elif kind == "fa" and L.kind == "geglu":
                            g, m = a
                            filled(dve, key)
                            drained(dve, ("fg", L.name, g, m))
                            dve.scalar_tensor_tensor(hf[g][:, m, :], bank[:, 0:PT2], col(L.w["b1"][0], m), gl[:, m % MRUN, :],
                                                     ALU.add, ALU.mult).then_inc(drain_mark(key), 1)
                        elif kind == "rt1":
                            g, = a
                            r = rt[:, g, :]
                            filled(dve, key)
                            dve.tensor_tensor(lg[:, g, :], bank[0:T, 0:E], rb_row[:], ALU.add
                                              ).then_inc(drain_mark(key), 1)
                            drained(dve, key)
                            dve.tensor_reduce(r[:, 0:1], lg[:, g, :], AX.X, ALU.max, negate=True).then_inc(s["rt_sum"], 1)
                            dve.wait_ge(s["rt_exp"], g + 1)
                            link(dve.reciprocal(r[:, 2:3], r[:, 1:2]))
                            link(dve.tensor_scalar(pr[:, g, :], ex[:, g, :], r[:, 2:3], None, ALU.mult))
                            link(dve.max(top[:, g, :], pr[:, g, :]))
                            link(dve.max_index(topi[:, g, :], top[:, g, :], pr[:, g, :]))
                            dve.tensor_tensor(r[:, 3:4], top[:, g, 1:2], top[:, g, 0:1], ALU.subtract).then_inc(s["rt_gap"], 1)
                            dve.tensor_copy(topf[:, g, :], topi[:, g, :])
                            dve.wait_ge(s["rt_w"], g + 1)
                            link(dve.tensor_scalar(r[:, 5:6], r[:, 4:5], 1.0, None, ALU.add))
                            link(dve.reciprocal(r[:, 6:7], r[:, 5:6]))
                            link(dve.tensor_tensor(r[:, 7:8], r[:, 6:7], r[:, 4:5], ALU.mult))
                            dve.tensor_scalar(c1[:, g, :], iota[:], topf[:, g, 0:1], r[:, 6:7], ALU.is_equal, ALU.mult)
                            link(dve.tensor_scalar(c2[:, g, :], iota[:], topf[:, g, 1:2], r[:, 7:8], ALU.is_equal, ALU.mult))
                            dve.tensor_tensor(comb[:, g, :], c1[:, g, :], c2[:, g, :], ALU.add).then_inc(s["comb_done"], 1)
                        elif kind == "rt3":
                            g, = a
                            filled(dve, key)
                            dve.tensor_tensor(acc[:, g, :], bank[0:T, 0:D], x[:, g, :], ALU.add
                                              ).then_inc(drain_mark(key), 1)

            with nc.Block() as block:
                @block.sync
                def _(sp):
                    for v in s.values():
                        sp.sem_clear(v)


SCALE = 256.0


def experts_pass(nc, t, env, next_weights, scratch):
    hT_d, acc_d, comb_d = env["hT_d"], env["acc_d"], env["comb_d"]
    HALF = B * T // 2
    BH = B // 2
    NW1, NW2 = KT * FF, FT * D
    RH = 4
    with ExitStack() as ctx:
        def sb(name, shape, dt=F32):
            return ctx.enter_context(nc.sbuf_tensor("b_" + name, shape, dt))

        def sem(name):
            return ctx.enter_context(nc.semaphore("b_" + name))

        h_in = scratch["L3_xattn_fc_w"][:].rearrange("p k n -> p (k n)")[:, 0:KT * B * T]
        stage = [(scratch["L2_xattn_wq"][:].rearrange("p k n -> p (k n)"), scratch["L2_xattn_wo"][:].rearrange("p k n -> p (k n)"))]
        wkv = scratch["L2_xattn_wkv"][:].rearrange("p k n -> p (k n)")
        stage.append((wkv[:, 0:NW1], wkv[:, NW1:NW1 + NW2]))
        h = sb("h", [128, 2, KT * B * T], F16)
        acc = sb("acc", [T, B, D])
        comb = sb("comb", [T, B, E])
        ce = sb("ce", [T, 2, B])
        w1 = sb("w1", [128, 2, 2, NW1], F16)
        w2 = sb("w2", [128, 2, 2, NW2], F16)
        b1 = sb("b1", [128, 2, FT])
        hid = sb("hid", [128, RH, HALF])
        hs = sb("hid_split", [128, 2, 2, FT, HALF + 128 - T], F16)
        hp = [ctx.enter_context(nc.psum_tensor(f"b_hidden{i}", [128, 512], F32)) for i in range(4)]
        yp = [ctx.enter_context(nc.psum_tensor(f"b_out{i}", [128, 512], F32)) for i in range(4)]
        in_once, pad_done = sem("in_once"), sem("pad_done")
        w_in = [sem("w_in0"), sem("w_in1")]
        turn_sems = {n: sem(n) for n in ["w_hi", "w_lo", "h_full", "h_free", "hid_hi", "hid_lo", "y_full", "y_free",
                                         "ce_done"]}
        w_hi, w_lo, h_full, h_free, hid_hi, hid_lo, y_full, y_free, ce_done = turn_sems.values()
        stored = sem("stored")
        h_hi, h_done = sem("in_hi"), sem("in_lo")
        TERMS = [(0, 0), (0, 1), (1, 0)]

        def load_expert(sp, slot, e):
            e = bass.ds(e, 1)
            sp.dma_start(stage[slot][0].rearrange("p (k n) -> p k n", k=KT),
                         t["L0_xattn_e_w1"][e, :, :].rearrange("o (k p) n -> (o p) k n", p=128)).then_inc(w_in[slot], 16)
            sp.dma_start(b1[:, slot], t["e_b1T"][e, :, :].rearrange("o p n -> (o p) n")).then_inc(w_in[slot], 16)
            sp.dma_start(stage[slot][1].rearrange("p (k n) -> p k n", k=FT),
                         t["L0_xattn_e_w2"][e, :, :].rearrange("o (k p) n -> (o p) k n", p=128)).then_inc(w_in[slot], 16)

        with nc.Block() as block:
            @block.sync
            def _(sp):
                load_expert(sp, 0, 0)
                sp.dma_start(h_in.rearrange("p (k n) -> p k n", k=KT), hT_d).then_inc(in_once, 16)
                sp.dma_start(acc[:], acc_d.rearrange("b p n -> p b n")).then_inc(in_once, 16)
                sp.dma_start(comb[:], comb_d.rearrange("b p n -> p b n")).then_inc(in_once, 16)
                load_expert(sp, 1, 1)
                load_weights(sp, t, next_weights)
                sp.wait_ge(in_once, 48)

            @block.vector
            def _(dve):
                dve.memset(hs[:].rearrange("p s l m n -> p (s l m) n")[:, :, HALF:], 0.0).then_inc(pad_done, 1)
                dve.wait_ge(in_once, 48)
                dve.wait_ge(h_hi, 1)
                dve.scalar_tensor_tensor(h[:, 1, :], h_in, SCALE, h[:, 0, :], ALU.mult, ALU.subtract
                                         ).then_inc(h_done, 1)
                dve.wait_ge(h_done, 1)

            @block.scalar
            def _(act):
                act.wait_ge(in_once, 48)
                act.activation(h[:, 0, :], h_in, ACT.Copy, scale=SCALE).then_inc(h_hi, 1)

        units = [(slot, half) for slot in range(2) for half in range(2)]
        with nc.Fori(0, E // 2) as pair:
            with nc.Block() as block:
                @block.sync
                def _(sp):
                    for slot in range(2):
                        sp.wait_ge(w_lo, 2 * slot + 2)
                        sp.wait_ge(h_free, 2 * FT * (slot + 1))
                        load_expert(sp, slot, (pair * 2 + 2 + slot) % E)

                @block.tensor
                def _(pe):
                    def hidden(n):
                        slot, half = units[n]
                        pe.wait_ge(w_lo, 2 * slot + 1)
                        for m in range(FT):
                            u = n * FT + m
                            if u >= 4:
                                pe.wait_ge(h_free, u - 3)
                            for kt in range(KT):
                                for ti, (lw, lh) in enumerate(TERMS):
                                    last = pe.matmul(hp[u % 4][:, 0:HALF],
                                                     w1[:, slot, lw, kt * FF + m * 128:kt * FF + (m + 1) * 128],
                                                     h[:, lh, kt * B * T + half * HALF:kt * B * T + (half + 1) * HALF],
                                                     start=kt == 0 and ti == 0, stop=kt == KT - 1 and ti == 2)
                            last.then_inc(h_full, 1)

                    def output(n):
                        slot, half = units[n]
                        pe.wait_ge(w_lo, 2 * slot + 2)
                        pe.wait_ge(hid_lo, (n + 1) * FT)
                        for b in range(BH):
                            u = n * BH + b
                            if u >= 4:
                                pe.wait_ge(y_free, u - 3)
                            for m in range(FT):
                                for ti, (lh, lw) in enumerate(TERMS):
                                    last = pe.matmul(yp[u % 4][:, 0:D], hs[:, n % 2, lh, m, b * T:b * T + 128],
                                                     w2[:, slot, lw, m * D:(m + 1) * D],
                                                     start=m == 0 and ti == 0, stop=m == FT - 1 and ti == 2)
                            last.then_inc(y_full, 1)

                    hidden(0)
                    for n in range(1, len(units)):
                        hidden(n)
                        output(n - 1)
                    output(len(units) - 1)

                @block.scalar
                def _(act):
                    def split_high(slot):
                        act.wait_ge(w_in[slot], 48 * (pair + 1))
                        for i, w in enumerate((w1, w2)):
                            act.activation(w[:, slot, 0, :], stage[slot][i], ACT.Copy, scale=SCALE).then_inc(w_hi, 1)

                    split_high(0)
                    for n, (slot, half) in enumerate(units):
                        for m in range(FT):
                            u = n * FT + m
                            act.wait_ge(h_full, u + 1)
                            if u >= RH:
                                act.wait_ge(hid_lo, u - RH + 1)
                            act.activation(hid[:, u % RH, :], hp[u % 4][:, 0:HALF], ACT.Gelu,
                                           bias=b1[:, slot, m:m + 1], scale=SCALE ** -2).then_inc(h_free, 1)
                        if n == 0:
                            split_high(1)

                @block.vector
                def _(dve):
                    def split_low(slot):
                        for i, w in enumerate((w1, w2)):
                            dve.wait_ge(w_hi, 2 * slot + i + 1)
                            dve.scalar_tensor_tensor(w[:, slot, 1, :], stage[slot][i], SCALE, w[:, slot, 0, :],
                                                     ALU.mult, ALU.subtract).then_inc(w_lo, 1)

                    def weigh(n, b):
                        slot, half = units[n]
                        u = n * BH + b
                        tile = half * BH + b
                        dve.wait_ge(y_full, u + 1)
                        if n >= 2:
                            dve.wait_ge(y_free, (n - 2) * BH + b + 1)
                        dve.scalar_tensor_tensor(acc[:, tile, :], yp[u % 4][0:T, 0:D], ce[:, slot, tile:tile + 1],
                                                 acc[:, tile, :], ALU.mult, ALU.add).then_inc(y_free, 1)

                    split_low(0)
                    for slot in range(2):
                        dve.tensor_scalar(ce[:, slot, :], comb[:, :, bass.ds(pair * 2 + slot, 1)].rearrange("p b o -> p (b o)"),
                                          SCALE ** -1, None, ALU.mult).then_inc(ce_done, 1)
                    dve.wait_ge(ce_done, 2)
                    for n, (slot, half) in enumerate(units):
                        for m in range(FT):
                            u = n * FT + m
                            dve.wait_ge(h_free, u + 1)
                            if n >= 2 and m == 0:
                                dve.wait_ge(y_full, (n - 1) * BH)
                            dve.tensor_copy(hs[:, n % 2, 0, m, 0:HALF], hid[:, u % RH, :]).then_inc(hid_hi, 1)
                            dve.wait_ge(hid_hi, u + 1)
                            dve.tensor_tensor(hs[:, n % 2, 1, m, 0:HALF], hid[:, u % RH, :], hs[:, n % 2, 0, m, 0:HALF],
                                              ALU.subtract).then_inc(hid_lo, 1)
                            if n >= 2 and m % 2 == 1:
                                weigh(n - 2, m // 2)
                        if n == 0:
                            split_low(1)
                    for n in (len(units) - 2, len(units) - 1):
                        for b in range(BH):
                            weigh(n, b)
            with nc.Block() as block:
                @block.sync
                def _(sp):
                    for v in turn_sems.values():
                        sp.sem_clear(v)

        with nc.Block() as block:
            @block.sync
            def _(sp):
                for w in w_in:
                    sp.wait_ge(w, 48 * (E // 2 + 1))
                sp.dma_start(acc_d.rearrange("b p n -> p b n"), acc[:]).then_inc(stored, 16)
                sp.wait_ge(stored, 16)


_NAMES = ["x", "ctx_1024", "L0_xattn_e_w1", "L0_xattn_e_w2", "L0_xattn_e_b2", "L0_xattn_router_b"]


def kernel(**inputs):
    import numpy as _np
    import concourse.bacc as _bacc
    from concourse.bass_utils import run_bass_kernel_spmd as _run

    given = {n: _np.asarray(a) for n, a in inputs.items()}
    arrays = {n: given[n] for n in _NAMES}
    arrays["ctxT"] = given["ctx_1024"].transpose(0, 2, 1)
    arrays["e_b1T"] = given["L0_xattn_e_b1"].reshape(E, FT, 128).transpose(0, 2, 1)
    for name, (_, _, turned) in WEIGHTS.items():
        arrays[name] = given[name].T if turned else given[name]
    bf16 = mybir.dt.np(BF16)
    arrays["ident"] = _np.eye(128, dtype=_np.float32)
    arrays["ident16"] = _np.eye(128).astype(bf16)
    arrays["identh"] = _np.eye(128, dtype=_np.float16)
    arrays["causal16"] = _np.tile(_np.where(_np.tri(T) > 0, 0.0, -1e30), (1, 4)).astype(bf16)
    arrays["iota"] = _np.tile(_np.arange(E, dtype=_np.float32), (T, 1))
    masks = (_np.arange(128)[:, None] // HD == _np.arange(8)).astype(_np.float32)
    parts = []
    for name, (_, n) in COLS.items():
        if name == "head_masks":
            parts.append(masks)
        elif n == 1:
            parts.append(_np.broadcast_to(given[name].reshape(1, 1), (128, 1)))
        else:
            parts.append(given[name].reshape(n, 128).T)
    arrays["cols"] = _np.concatenate(parts, axis=1)
    arrays["rows"] = _np.stack([given[name] for name in ROWS])

    nc = _bacc.Bacc("TRN2", target_bir_lowering=False, num_devices=1)
    feed, aps = {}, {}
    for name, a in arrays.items():
        a = _np.ascontiguousarray(a)
        feed[f"in_{name}_dram"] = a
        aps[name] = nc.dram_tensor(f"in_{name}_dram", a.shape, mybir.dt.from_np(a.dtype), kind="ExternalInput").ap()
    out = nc.dram_tensor("out_dram", (B, T, D), F32, kind="ExternalOutput").ap()
    network(nc, aps, out)
    return _run(nc, [feed], core_ids=[0]).results[0]["out_dram"]
```

```python
from contextlib import ExitStack

import concourse.bass as bass
from concourse import mybir

F32 = mybir.dt.float32
BF16 = mybir.dt.bfloat16
F16 = mybir.dt.float16
U32 = mybir.dt.uint32
ALU = mybir.AluOpType
ACT = mybir.ActivationFunctionType
AX = mybir.AxisListType

B, T, D, M = 8, 112, 256, 375
H = 16
HD, HD2 = D // H, 64
KT = D // 128
C, MC = 3, M // 3
E, FF = 8, 1024
FT = FF // 128
G = 4
GT = G * T
PT2 = 2 * T
TURNS = B // G
RP = 4
MAGIC = 1.5 * 2.0 ** 23
EPS = 1e-5

COLS = {}
for _name, _n in [
    ("L0_xattn_sa_bq", 2), ("L0_xattn_sa_bk", 2), ("L0_xattn_sa_bv", 2),
    ("L0_xattn_ca_bq", 2), ("L0_xattn_ca_bk", 2), ("L0_xattn_ca_bv", 2),
    ("L1_xattn_ln1_g", 2), ("L1_xattn_ln1_b", 2), ("L1_xattn_ln2_g", 2), ("L1_xattn_ln2_b", 2),
    ("L1_xattn_ln3_g", 2), ("L1_xattn_ln3_b", 2), ("L1_xattn_ff_b1", 16),
    ("L2_xattn_ln_g", 2), ("L2_xattn_ln_b", 2), ("L2_xattn_bq", 8), ("L2_xattn_bkv", 16),
    ("L3_xattn_ln1_g", 2), ("L3_xattn_ln1_b", 2), ("L3_xattn_attn_qkv_b", 6),
    ("L3_xattn_ln2_g", 2), ("L3_xattn_ln2_b", 2), ("L3_xattn_q_b", 2), ("L3_xattn_k_b", 2), ("L3_xattn_v_b", 2),
    ("L3_xattn_ln3_g", 2), ("L3_xattn_ln3_b", 2), ("L3_xattn_fc_b", 8),
    ("L1_xattn_d_q1", 1), ("L1_xattn_d_k1", 1), ("L1_xattn_d_v1", 1), ("L1_xattn_d_w1", 1),
    ("L1_xattn_d_q2", 1), ("L1_xattn_d_k2", 1), ("L1_xattn_d_v2", 1), ("L1_xattn_d_w2", 1),
    ("head_masks", 8), ("head_masks_scaled", 8),
]:
    COLS[_name] = (sum(n for _, n in COLS.values()), _n)
NCOL = sum(n for _, n in COLS.values())
ROWS = {name: i for i, name in enumerate([
    "L0_xattn_sa_bo", "L0_xattn_ca_bo", "L0_xattn_ln1_g", "L0_xattn_ln1_b", "L0_xattn_ln2_g", "L0_xattn_ln2_b",
    "L0_xattn_ln3_g", "L0_xattn_ln3_b", "L1_xattn_a1_bo", "L1_xattn_a2_bo", "L1_xattn_ff_b2", "L2_xattn_bo",
    "L3_xattn_attn_proj_b", "L3_xattn_ca_proj_b", "L3_xattn_proj_b"])}
NROW = len(ROWS)
WEIGHTS = {
    "L0_xattn_sa_wq": (D, D, False), "L0_xattn_sa_wk": (D, D, False), "L0_xattn_sa_wv": (D, D, False),
    "L0_xattn_sa_wo": (D, D, False), "L0_xattn_ca_wq": (D, D, False), "L0_xattn_ca_wk": (D, D, False),
    "L0_xattn_ca_wv": (D, D, False), "L0_xattn_ca_wo": (D, D, False), "L0_xattn_router_w": (D, E, False),
    "L1_xattn_a1_wq": (D, D, False), "L1_xattn_a1_wk": (D, D, False), "L1_xattn_a1_wv": (D, D, False),
    "L1_xattn_a1_wo": (D, D, False), "L1_xattn_a2_wq": (D, D, False), "L1_xattn_a2_wk": (D, D, False),
    "L1_xattn_a2_wv": (D, D, False), "L1_xattn_a2_wo": (D, D, False), "L1_xattn_ff_w1": (D, 2 * FF, False),
    "L1_xattn_ff_w2": (FF, D, False), "L2_xattn_wq": (D, H * HD2, False), "L2_xattn_wkv": (D, 2 * H * HD2, False),
    "L2_xattn_wo": (H * HD2, D, False), "L3_xattn_attn_qkv_w": (D, 3 * D, True), "L3_xattn_attn_proj_w": (D, D, True),
    "L3_xattn_q_w": (D, D, True), "L3_xattn_k_w": (D, D, True), "L3_xattn_v_w": (D, D, True),
    "L3_xattn_ca_proj_w": (D, D, True), "L3_xattn_fc_w": (D, FF, True), "L3_xattn_proj_w": (FF, D, True)}


class Layer:

    def __init__(self, name, kind, pre=None, post=None, row=None, quant=None, causal=False, cross=False, **w):
        self.name, self.kind, self.pre, self.post, self.row = name, kind, pre, post, row
        self.quant, self.causal, self.cross, self.w = quant, causal, cross, w
        self.wide = kind == "attn64"
        if kind == "attn64":
            self.groups = [[8 * half + 2 * i + par for i in range(4)] for half in range(2) for par in range(2)]
        elif cross:
            self.groups = [[h] for h in range(H)]
        else:
            self.groups = [[2 * j, 2 * j + 1, 8 + 2 * j, 9 + 2 * j] for j in range(4)]


def W(name, col=0):
    return (name, col)


PASS_L0 = [
    Layer("L0sa", "attn", row="L0_xattn_sa_bo", post=("L0_xattn_ln1_g", "L0_xattn_ln1_b"), causal=True,
          q=W("L0_xattn_sa_wq"), k=W("L0_xattn_sa_wk"), v=W("L0_xattn_sa_wv"), o=W("L0_xattn_sa_wo"),
          bq=("L0_xattn_sa_bq", 0), bk=("L0_xattn_sa_bk", 0), bv=("L0_xattn_sa_bv", 0)),
    Layer("L0ca", "attn", row="L0_xattn_ca_bo", post=("L0_xattn_ln2_g", "L0_xattn_ln2_b"), cross=True,
          q=W("L0_xattn_ca_wq"), k=W("L0_xattn_ca_wk"), v=W("L0_xattn_ca_wv"), o=W("L0_xattn_ca_wo"),
          bq=("L0_xattn_ca_bq", 0), bk=("L0_xattn_ca_bk", 0), bv=("L0_xattn_ca_bv", 0)),
    Layer("route", "route"),
]
PASS_L1 = [
    Layer("L0ln", "norm", post=("L0_xattn_ln3_g", "L0_xattn_ln3_b")),
    Layer("L1a1", "attn", pre=("L1_xattn_ln1_g", "L1_xattn_ln1_b"), row="L1_xattn_a1_bo", quant=1,
          q=W("L1_xattn_a1_wq"), k=W("L1_xattn_a1_wk"), v=W("L1_xattn_a1_wv"), o=W("L1_xattn_a1_wo")),
    Layer("L1a2", "attn", pre=("L1_xattn_ln2_g", "L1_xattn_ln2_b"), row="L1_xattn_a2_bo", quant=2, cross=True,
          q=W("L1_xattn_a2_wq"), k=W("L1_xattn_a2_wk"), v=W("L1_xattn_a2_wv"), o=W("L1_xattn_a2_wo")),
    Layer("L1ff", "geglu", pre=("L1_xattn_ln3_g", "L1_xattn_ln3_b"), row="L1_xattn_ff_b2",
          w1=W("L1_xattn_ff_w1"), w2=W("L1_xattn_ff_w2"), b1=("L1_xattn_ff_b1", 0)),
]
PASS_L23 = [
    Layer("L2at", "attn64", pre=("L2_xattn_ln_g", "L2_xattn_ln_b"), row="L2_xattn_bo", causal=True,
          q=W("L2_xattn_wq"), k=W("L2_xattn_wkv"), v=W("L2_xattn_wkv", H * HD2), o=W("L2_xattn_wo"),
          bq=("L2_xattn_bq", 0), bk=("L2_xattn_bkv", 0), bv=("L2_xattn_bkv", 8)),
    Layer("L3sa", "attn", pre=("L3_xattn_ln1_g", "L3_xattn_ln1_b"), row="L3_xattn_attn_proj_b", causal=True,
          q=W("L3_xattn_attn_qkv_w"), k=W("L3_xattn_attn_qkv_w", D), v=W("L3_xattn_attn_qkv_w", 2 * D),
          o=W("L3_xattn_attn_proj_w"), bq=("L3_xattn_attn_qkv_b", 0), bk=("L3_xattn_attn_qkv_b", 2),
          bv=("L3_xattn_attn_qkv_b", 4)),
    Layer("L3ca", "attn", pre=("L3_xattn_ln2_g", "L3_xattn_ln2_b"), row="L3_xattn_ca_proj_b", cross=True,
          q=W("L3_xattn_q_w"), k=W("L3_xattn_k_w"), v=W("L3_xattn_v_w"), o=W("L3_xattn_ca_proj_w"),
          bq=("L3_xattn_q_b", 0), bk=("L3_xattn_k_b", 0), bv=("L3_xattn_v_b", 0)),
    Layer("L3ff", "gelu", pre=("L3_xattn_ln3_g", "L3_xattn_ln3_b"), row="L3_xattn_proj_b",
          w1=W("L3_xattn_fc_w"), w2=W("L3_xattn_proj_w"), b1=("L3_xattn_fc_b", 0)),
]


LAG_EXP, LAG_SPLIT, LAG_ROUND, LAG_TURN, LAG_AV = 1, 2, 3, 4, 5
MRUN = 4


def context_steps(L, g):
    if L.kind == "attn" and L.cross:
        return [("kc", L, g, mt) for mt in range(KT)] + [("vc", L, g, c) for c in range(C)]
    if L.kind == "attn64":
        return ([("cln", L, g), ("cnb", L, g), ("ctr", L, g)] + [("k", L, g, mt) for mt in range(8)]
                + [("v", L, g, h) for h in range(2)])
    return []


WAIT = None


def before_scores(L, g):
    out = []
    if L.row:
        out.append(("xb", L, g))
    if L.pre:
        out += [("lna", L, g), WAIT, ("lnb", L, g), WAIT]
    if L.kind == "norm":
        return out + [("pna", L, g), WAIT, ("pnb", L, g), WAIT]
    out += [("trx", L, g), WAIT]
    if L.kind == "route":
        return out + [("rt1", L, g), ("rt2", L, g), ("rt3", L, g)]
    if L.kind in ("geglu", "gelu"):
        if g % 2 == 1:
            for m0 in range(0, FT, MRUN):
                run = range(m0, m0 + MRUN)
                out.append([(kind, L, g // 2, m) for kind in (("fg", "fa") if L.kind == "geglu" else ("fa",)) for m in run])
            out += [("f2", L, g - 1), ("f2", L, g)]
        return out
    nq = 8 if L.wide else KT
    own = not L.cross and not L.wide
    for mt in range(nq):
        out.append(("q", L, g, mt))
        if own:
            out.append(("k", L, g, mt))
        if mt and not L.wide:
            out.append(("ql", L, g, mt - 1))
    if own:
        out.append(("v", L, g))
    return out if L.wide else out + [("ql", L, g, nq - 1)]


def turn_steps(layers):
    attn = [L for L in layers if L.kind in ("attn", "attn64")]
    slots = [(L, g, n) for L in attn for g in range(G) for n in range(len(L.groups))]
    first = {(L.name, g): slots.index((L, g, 0)) for L in attn for g in range(G)}
    steps = []
    queue = []

    def onward(i, g):
        out = []
        while i < len(layers):
            out += before_scores(layers[i], g)
            if layers[i] in attn:
                return out, first[layers[i].name, g]
            i += 1
        if layers[-1].kind == "route":
            out.append(("store", layers[-1], g))
        elif g % 2 == 1:
            out += [("store", layers[-1], g - 1), ("store", layers[-1], g)]
        return out, len(slots) + LAG_AV + 2

    def emit_due(slot):
        for q in list(queue):
            items, due, free_from = q
            if slot < free_from:
                continue
            left = max(1, due - slot)
            for _ in range(len(items) if due <= slot else -(-len(items) // left)):
                item = items.pop(0)
                if item is not WAIT:
                    steps.extend(item if isinstance(item, list) else [item])
            if not items:
                queue.remove(q)

    def emit_fills(slot):
        ahead, most = 0, 0
        for items, due, _ in fills:
            ahead += len(items)
            if ahead:
                most = max(most, ahead if due <= slot + 1 else -(-ahead // (due - slot - 1)))
        for items, due, free_from in fills:
            while items and most > 0 and slot >= free_from:
                steps.append(items.pop(0))
                most -= 1

    for g in range(G):
        queue.append((*onward(0, g), -1))
    fills = []
    for k, L in enumerate(attn):
        for g in range(G):
            items = context_steps(L, g)
            if items:
                after = 0
                if L.cross and any(a.wide for a in attn[:k]):
                    wide = next(a for a in attn if a.wide)
                    after = first[wide.name, g] + len(wide.groups) + LAG_AV
                fills.append((items, first[L.name, g], after))
    for s in range(len(slots) + LAG_AV + 2):
        emit_due(s)
        emit_fills(s)
        if 0 <= s - LAG_EXP < len(slots):
            steps.append(("ex",) + slots[s - LAG_EXP])
        if s < len(slots):
            steps.append(("qk",) + slots[s])
        if 0 <= s - LAG_SPLIT < len(slots):
            steps.append(("sp",) + slots[s - LAG_SPLIT])
        if 0 <= s - LAG_ROUND < len(slots) and slots[s - LAG_ROUND][0].quant:
            steps.append(("sr",) + slots[s - LAG_ROUND])
        if 0 <= s - LAG_TURN < len(slots):
            steps.append(("tp",) + slots[s - LAG_TURN])
        if 0 <= s - LAG_AV < len(slots):
            L, g, n = slots[s - LAG_AV]
            steps.append(("av", L, g, n))
            halves = 2 if L.wide else 1
            per = len(L.groups) // halves
            if (n + 1) % per == 0:
                half = n // per
                steps.append(("fin", L, g, half))
                out = [WAIT, ("tro", L, g, half)]
                due = s + 1
                if half == halves - 1:
                    out += [WAIT, ("wo", L, g), WAIT]
                    if L.post:
                        out += [("pna", L, g), WAIT, ("pnb", L, g), WAIT]
                    more, due = onward(layers.index(L) + 1, g)
                    out += more
                queue.append((out, due, -1))
    emit_due(len(slots) + LAG_AV + 2)
    return steps


PSUM_STEPS = {"kc", "vc", "ctr", "k", "v", "q", "trx", "tro", "wo", "fg", "fa", "f2", "rt1", "rt2", "rt3"}
KEYS = ("kc", "vc", "k", "v", "q")


class Turn:

    def __init__(self, layers):
        self.steps = turn_steps(layers)
        self.psum, self.at, self.count = {}, {}, {}
        self.raw, self.raw_users = {}, []
        self.high_act, self.high_dve = {}, {}
        self.plain, self.whole, self.scaled, self.rescaled, self.unscaled = {}, {}, {}, {}, {}
        self.quant, self.split, self.group, self.obank = {}, {}, {}, {}
        for st in self.steps:
            kind, L = st[0], st[1]
            key = (kind, L.name) + st[2:]
            if kind in PSUM_STEPS:
                self.psum[key] = len(self.psum)
            self.at[key] = self.count.get(kind, 0)
            self.count[kind] = self.at[key] + 1
            if L.quant and kind in KEYS:
                self.quant[key] = len(self.quant)
            elif kind in KEYS:
                self.split[key] = len(self.split)
            if kind == "qk":
                self.group[key[1:]] = len(self.group)
                if L.quant or L.wide:
                    self.rescaled[key[1:]] = len(self.rescaled)
                else:
                    self.unscaled[key[1:]] = len(self.unscaled)
                if not L.quant:
                    self.plain[key[1:]] = len(self.plain)
                    high = self.high_act if L.cross else self.high_dve
                    high[key[1:]] = len(high)
                else:
                    self.whole[key[1:]] = len(self.whole)
                    if L.cross:
                        self.scaled[key[1:]] = len(self.scaled)
            if kind in KEYS and L.quant:
                self.raw[key] = len(self.raw)
                self.raw_users.append(key)
            if kind == "fin":
                self.obank[key[1:]] = len(self.obank)
        self.lnorm, n = {}, 0
        for st in self.steps:
            if st[0] in ("lna", "cln", "pna"):
                self.lnorm[(st[0], st[1].name) + st[2:]] = n
                n += 1
        self.mask_dve, self.mask_pool = {}, {}
        for st in self.steps:
            if st[0] == "ql":
                key = ("ql", st[1].name) + st[2:]
                if not (st[1].quant and st[3] == 1):
                    self.mask_dve[key] = len(self.mask_dve)
                if not (st[1].quant and st[3] == 0):
                    self.mask_pool[key] = len(self.mask_pool)
        self.xn = {}
        for st in self.steps:
            if st[0] in ("lnb", "cnb"):
                self.xn[(st[0], st[1].name) + st[2:]] = len(self.xn)


PASSES = [PASS_L0, PASS_L1, PASS_L23]


def network(nc, t, out):
    with ExitStack() as ctx:
        def sb(name, shape, dt=F32):
            return ctx.enter_context(nc.sbuf_tensor(name, shape, dt))

        def sem(name):
            return ctx.enter_context(nc.semaphore(name))

        hT_d = nc.dram_tensor("moe_in_T", (128, KT, B * T), F32, kind="Internal").ap()
        acc_d = nc.dram_tensor("moe_acc", (B, T, D), F32, kind="Internal").ap()
        comb_d = nc.dram_tensor("moe_combine", (B, T, E), F32, kind="Internal").ap()
        x_d = nc.dram_tensor("after_L1", (B, T, D), F32, kind="Internal").ap()

        ident = sb("ident", [128, 128])
        ident16 = sb("ident16", [128, 128], BF16)
        identh = sb("identh", [128, 128], F16)
        causal16 = sb("causal16", [T, 4 * T], BF16)
        cols = sb("cols", [128, NCOL])
        neghalf = sb("neghalf", [128, 1])
        dinv = sb("dinv", [128, 8])
        dmul = sb("dmul", [128, 4])
        w4 = pass_weights(nc, t, 2, ctx)
        expert_in = [sem(f"expert_in{i}") for i in range(2)]
        w1_ctx = ctx.enter_context(ExitStack())
        iota = w1_ctx.enter_context(nc.sbuf_tensor("iota", [T, E], F32))
        rb_row = w1_ctx.enter_context(nc.sbuf_tensor("rb_row", [T, E], F32))
        eb2 = w1_ctx.enter_context(nc.sbuf_tensor("eb2", [E, D], F32))

        def col(name, i=0):
            return cols[:, COLS[name][0] + i:COLS[name][0] + i + 1]

        d_names = ["L1_xattn_d_q1", "L1_xattn_d_k1", "L1_xattn_d_v1", "L1_xattn_d_w1",
                   "L1_xattn_d_q2", "L1_xattn_d_k2", "L1_xattn_d_v2", "L1_xattn_d_w2"]

        const_in = sem("const_in")
        ready = sem("ready")
        with nc.Block() as block:
            @block.sync
            def _(sp):
                loads = [(ident[:], t["ident"]), (ident16[:], t["ident16"]), (identh[:], t["identh"]), (causal16[:], t["causal16"]),
                         (iota[:], t["iota"]), (cols[:], t["cols"]),
                         (rb_row[:], t["L0_xattn_router_b"].rearrange("(o e) -> o e", o=1).to_broadcast([T, E])),
                         (eb2[:], t["L0_xattn_e_b2"])]
                for dst, src in loads:
                    sp.dma_start(dst, src).then_inc(const_in, 16)
                sp.wait_ge(const_in, 16 * len(loads))

            @block.vector
            def _(dve):
                dve.memset(neghalf[:], -0.5)
                dve.wait_ge(const_in, 16 * 8)
                d0 = COLS["L1_xattn_d_q1"][0]
                dve.reciprocal(dinv[:], cols[:, d0:d0 + 8]).then_inc(ready, 1)
                for i in range(2):
                    dve.tensor_scalar(dmul[:, 2 * i:2 * i + 1], col(d_names[4 * i]), col(d_names[4 * i + 1]),
                                      HD ** -0.5, ALU.mult, ALU.mult)
                    dve.tensor_scalar(dmul[:, 2 * i + 1:2 * i + 2], col(d_names[4 * i + 2]),
                                      col(d_names[4 * i + 3]), None, ALU.mult)

        env = locals()
        with w1_ctx:
            w1 = pass_weights(nc, t, 0, w1_ctx)
            with nc.Block() as block:
                @block.sync
                def _(sp):
                    load_weights(sp, t, w1)
            attention_pass(nc, t, 0, env, w1, out, first_experts=(w4["tiles"], expert_in))
        with ExitStack() as w3_ctx:
            w3 = pass_weights(nc, t, 1, w3_ctx)
            experts_pass(nc, t, env, w3, w4["tiles"], expert_in)
            attention_pass(nc, t, 1, env, w3, out, next_weights=w4)
        attention_pass(nc, t, 2, env, w4, out)


def expert_stage(tiles, slot):
    flat = {n: tiles[n][:].rearrange("p k n -> p (k n)") for n in ("L2_xattn_wq", "L2_xattn_wo", "L2_xattn_wkv")}
    if slot == 0:
        return flat["L2_xattn_wq"], flat["L2_xattn_wo"]
    return flat["L2_xattn_wkv"][:, 0:KT * FF], flat["L2_xattn_wkv"][:, KT * FF:KT * FF + FT * D]


def load_expert(sp, t, tiles, slot, e, done, part=0, parts=1):
    e = bass.ds(e, 1)
    for name, k, n, place in zip(("L0_xattn_e_w1", "L0_xattn_e_w2"), (KT, FT), (FF, D), expert_stage(tiles, slot)):
        cs = bass.ds(part * (n // parts), n // parts)
        sp.dma_start(place.rearrange("p (k n) -> p k n", k=k)[:, :, cs],
                     t[name][e, :, cs].rearrange("o (k p) n -> (o p) k n", p=128)).then_inc(done, 16)


def pass_weights(nc, t, which, ctx):
    pre = f"p{which}_"
    used = []
    for L in PASSES[which]:
        for k, w in L.w.items():
            if not k.startswith("b") and w[0] not in used:
                used.append(w[0])
    if which == 0:
        used.append("L0_xattn_router_w")
    tiles = {n: ctx.enter_context(nc.sbuf_tensor(pre + n, [128, WEIGHTS[n][0] // 128, WEIGHTS[n][1]], F32)) for n in used}
    sems = {n: ctx.enter_context(nc.semaphore(pre + "in_" + n)) for n in used}
    r0, nrow = [(0, 6), (6, 5), (11, 4)][which]
    rows = ctx.enter_context(nc.sbuf_tensor(pre + "rows", [T, nrow, D], F32))
    row_in = ctx.enter_context(nc.semaphore(pre + "row_in"))
    w = dict(tiles=tiles, sems=sems, rows=rows, row_in=row_in, r0=r0, nrow=nrow)
    return w


def load_weights(sp, t, w):
    load_rows(sp, t, w)
    for n, tile in w["tiles"].items():
        sp.dma_start(tile[:], t[n].rearrange("(k p) n -> p k n", p=128)).then_inc(w["sems"][n], 16)


def load_part(sp, t, w, part, parts):
    for n, tile in w["tiles"].items():
        cs = bass.ds(part * (WEIGHTS[n][1] // parts), WEIGHTS[n][1] // parts)
        sp.dma_start(tile[:, :, cs], t[n][:, cs].rearrange("(k p) n -> p k n", p=128)).then_inc(w["sems"][n], 16)


def load_rows(sp, t, w):
    r0, nrow = w["r0"], w["nrow"]
    sp.dma_start(w["rows"][:], t["rows"][r0:r0 + nrow, :].rearrange("(o r) d -> o r d", o=1)
                 .to_broadcast([T, nrow, D])).then_inc(w["row_in"], 16)


def attention_pass(nc, t, which, env, w, out, first_experts=None, next_weights=None):
    layers = PASSES[which]
    turn = Turn(layers)
    QUANT = which == 1
    L2IN = which == 2
    NRAW = 4
    halves = 1 if QUANT else 2
    NM, NS, NT = (4, 2, 1) if QUANT else (4, 2, 1)
    ident, ident16, causal16, iota = env["ident"], env["ident16"], env["causal16"], env["iota"]
    cols, rb_row, eb2, neghalf = env["cols"], env["rb_row"], env["eb2"], env["neghalf"]
    identh = env["identh"]
    dinv, dmul, col = env["dinv"], env["dmul"], env["col"]
    m0 = COLS["head_masks" if QUANT else "head_masks_scaled"][0]
    head_masks = cols[:, m0:m0 + 8]
    head_mask = [cols[:, m0 + h8:m0 + h8 + 1] for h8 in range(8)]
    hT_d, acc_d, comb_d = env["hT_d"], env["acc_d"], env["comb_d"]
    x_d = env["x_d"]
    loaded = 16 * TURNS if L2IN else 16
    weight, w_in = w["tiles"], w["sems"]
    pre = ["a_", "c_", "d_"][which]
    with ExitStack() as ctx:
        def sb(name, shape, dt=F32):
            return ctx.enter_context(nc.sbuf_tensor(pre + name, shape, dt))

        def sem(name):
            return ctx.enter_context(nc.semaphore(pre + name))

        def row(name):
            return w["rows"][:, ROWS[name] - w["r0"], :]

        x = sb("x", [T, G, D])
        xb = sb("xb", [T, G, D])
        xn = sb("xn", [T, G, D])
        hT = sb("hT", [128, KT, GT])
        cT = sb("cT", [128, KT, G, M])
        qm = sb("q_split", [128, G, halves, KT, 8, T], F16)
        qs = sb("q_halves", [128, G, halves, KT, T], F16)
        kS, vS = sb("kS", [128, halves, KT, GT], F16), sb("vS", [T, G, H, halves, HD], F16)
        nk, nv = halves * KT * M, halves * C * D
        kvC = sb("kvC", [128, G, max(nk + nv, 2 * 8 * T + 2 * H * HD2) if L2IN else nk + nv], F16)
        kC = [kvC[:, g, 0:nk].rearrange("p (l k m) -> p l k m", l=halves, k=KT) for g in range(G)]
        vC = [kvC[0:MC, g, nk:nk + nv].rearrange("p (c h l d) -> p c h l d", c=C, h=H, l=halves) for g in range(G)]
        stats = sb("stats", [T, 2 * G, 6])
        mv = sb("mv", [T, 2 * G, 2])
        nrm = sb("nrm", [T, 2 * G, 4])
        P = sb("P", [T, RP, 448])
        Ps = sb("P_split", [T, RP, 2 * 448 + 16], F16)
        PT = sb("PT", [MC, 2, 8 * T + 16], F16)
        negm = sb("negm", [T, 4, 4])
        negs = sb("negs", [T, 4, 4])
        sums = sb("sums", [T, G, H])
        rsum = sb("rsum", [T, G, H])
        Osb = sb("Osb", [T, 2, 512 if L2IN else D])
        OT = sb("OT", [128, 2, 8 if L2IN else KT, T])
        hf = [qm[:, 2 * pair:2 * pair + 2].rearrange("p g l k h n -> p (g l k h n)")[:, 0:2 * FT * PT2].bitcast(F32)
              .rearrange("p (m n) -> p m n", m=FT) for pair in range(G // 2)]
        if QUANT:
            qmb, qsb = qm[:].bitcast(BF16), qs[:].bitcast(BF16)
            kSb, vSb = kS[:, 0].bitcast(BF16), vS[:].rearrange("p g h l d -> p g (h l d)").bitcast(BF16)
            kCb = [k[:, 0].bitcast(BF16) for k in kC]
            vCb = [v.rearrange("p c h l d -> p c (h l d)").bitcast(BF16) for v in vC]
            Psb, PTb = Ps[:].bitcast(BF16), PT[:].bitcast(BF16)
            raw = sb("raw", [128, NRAW, M])
            rinv, rq = sb("rinv", [T, 4, 4]), sb("rq", [T, 4, 4])
            gl = sb("gl", [128, MRUN, PT2])
        elif L2IN:
            q2 = [qm[:, g, 0].rearrange("p k h n -> p (k h n)").rearrange("p (m l n) -> p m l n", m=8, l=2)
                  for g in range(G)]
            k2 = [kvC[:, g, 0:2 * 8 * T].rearrange("p (m l n) -> p m l n", m=8, l=2) for g in range(G)]
            v2 = [kvC[0:T, g, 2 * 8 * T:2 * 8 * T + 2 * H * HD2].rearrange("p (l d) -> p l d", l=2) for g in range(G)]
            ctok = sb("ctok", [T, G, D])
            cnT = sb("cnT", [128, KT, GT])
        else:
            lg, ex, pr = sb("lg", [T, G, E]), sb("ex", [T, G, E]), sb("pr", [T, G, E])
            rt = sb("rt", [T, G, 8])
            top = sb("top", [T, G, 8])
            topi = sb("topi", [T, G, 8], U32)
            topf = sb("topf", [T, G, 8])
            c1, c2, comb = sb("c1", [T, G, E]), sb("c2", [T, G, E]), sb("comb", [T, G, E])
            acc, cbT = xn, xb[0:E, :, 0:T]

        def pb(name):
            return ctx.enter_context(nc.psum_tensor(pre + name, [128, 512], F32))

        mp = [pb(f"mix{i}") for i in range(NM)]
        Sb = [pb(f"scores{i}") for i in range(NS)]
        Tb = [ctx.enter_context(nc.psum_tensor(pre + f"probsT{i}", [128, 1024], F16))[:] for i in range(NT)]
        Tbb = [b.bitcast(BF16) for b in Tb]
        Ob = pb("attnout")

        names = ["x_in", "ctx_in", "stored", "mp_full", "s_full", "neg_max", "neg_scaled", "max_done",
                 "exp_done", "hi_act", "hi_dve", "split_lo", "split_int", "rq_done", "scaled", "scaled_dve",
                 "kv_hi", "q_dve", "q_pool", "tp_done", "pt_done", "av_done", "fin_done", "x_done", "xb_done",
                 "stat_done", "rstd_done", "xn_done", "ln_half", "dve_chain", "clipped", "int_done", "rt_sum",
                 "rt_exp", "rt_gap", "rt_w", "comb_done"]
        s = {n: sem(n) for n in names + [f"mp_free{i}" for i in range(NM)]}
        mp_free = [s[f"mp_free{i}"] for i in range(NM)]

        def drained(eng, key):
            u = turn.psum[key]
            eng.wait_ge(mp_free[u % NM], u // NM + 1)

        def bank_free(eng, u):
            if u >= NM:
                eng.wait_ge(mp_free[u % NM], u // NM)

        def filled(eng, key):
            eng.wait_ge(s["mp_full"], turn.psum[key] + 1)

        def drain_mark(key):
            return mp_free[turn.psum[key] % NM]

        def x_ready(eng, i, g):
            if i == 0:
                eng.wait_ge(s["x_in"], 16 * G)
            elif layers[i - 1].post:
                eng.wait_ge(s["x_done"], turn.at["pnb", layers[i - 1].name, g] + 1)
            else:
                drained(eng, ("wo" if "o" in layers[i - 1].w else "f2", layers[i - 1].name, g))

        def index(L):
            return layers.index(L)

        def gpos(L, g, n):
            return turn.group[L.name, g, n]

        by_pos = {v: (next(L for L in layers if L.name == k[0]), k[1], k[2]) for k, v in turn.group.items()}

        def heads(L, n):
            return L.groups[n]

        def norm_slot(key):
            return key[2] + (G if key[0] == "cln" else 0)

        def shapes(L):
            return (MC, C) if L.cross else (T, 1)

        def wtile(w, kt, c0, n):
            return weight[w[0]][:, kt, w[1] + c0:w[1] + c0 + n]

        def operand(eng, key, L):
            if L.quant:
                eng.wait_ge(s["int_done"], turn.quant[key] + 1)
            else:
                drained(eng, key)

        def raw_free(eng, key):
            r = turn.raw[key]
            if r >= NRAW:
                eng.wait_ge(s["int_done"], turn.quant[turn.raw_users[r - NRAW]] + 1)

        def quant_buffer(key):
            kind, L = key[0], next(l for l in layers if l.name == key[1])
            n, dst = quant_dst(kind, key[2:])
            c = 4 * (L.quant - 1) + {"q": 0, "k": 1, "kc": 1, "v": 2, "vc": 2}[kind]
            return raw[0:dst.shape[0], turn.raw[key] % NRAW, 0:n], dst, dinv[0:dst.shape[0], c:c + 1]

        def quant_dst(kind, a):
            if kind == "q":
                return T, qsb[:, a[0], 0, a[1], :]
            if kind == "k":
                return T, kSb[:, a[1], a[0] * T:(a[0] + 1) * T]
            if kind == "v":
                return D, vSb[:, a[0], :]
            if kind == "kc":
                return M, kCb[a[0]][:, a[1], :]
            return D, vCb[a[0]][:, a[1], :]

        def kv_split(key, L):
            kind, a = key[0], key[2:]
            bank = mp[turn.psum[key] % NM]
            if kind == "q":
                g, mt = a
                hi_lo = [q2[g][:, mt, l, :] if L.wide else qs[:, g, l, mt, :] for l in range(2)]
                return bank[:, 0:T], *hi_lo, col(L.w["bq"][0], L.w["bq"][1] + mt)
            if kind == "k":
                g, mt = a
                lo_hi = [k2[g][:, mt, l, :] if L.wide else kS[:, l, mt, g * T:(g + 1) * T] for l in range(2)]
                return bank[:, 0:T], *lo_hi, col(L.w["bk"][0], L.w["bk"][1] + mt)
            if kind == "kc":
                g, mt = a
                return bank[:, 0:M], kC[g][:, 0, mt, :], kC[g][:, 1, mt, :], col(L.w["bk"][0], L.w["bk"][1] + mt)
            if L.wide:
                g, h = a
                return bank[0:T, 0:512], v2[g][:, 0, h * 512:(h + 1) * 512], v2[g][:, 1, h * 512:(h + 1) * 512], None
            np_, dst = (T, vS[:, a[0]]) if kind == "v" else (MC, vC[a[0]][:, a[1]])
            return bank[0:np_, 0:D].rearrange("p (h d) -> p h d", h=H), dst[:, :, 0, :], dst[:, :, 1, :], None

        def split_ready(eng, L, g, n):
            if L.quant:
                eng.wait_ge(s["split_int"], turn.whole[L.name, g, n] + 1)
            else:
                eng.wait_ge(s["split_lo"], turn.plain[L.name, g, n] + 1)

        with nc.Block() as block:
            @block.vector
            def _(dve):
                dve.memset(Ps[:], 0.0)
                dve.memset(PT[:], 0.0)

            @block.sync
            def _(sp):
                if L2IN:
                    load_rows(sp, t, w)
                sp.wait_ge(w["row_in"], 16)

        with nc.Fori(0, TURNS) as turn_no:
            with nc.Block() as block:
                @block.sync
                def _(sp):
                    src = [t["x"], acc_d, x_d][which]
                    for g in range(G):
                        b = bass.ds(turn_no * G + g, 1)
                        sp.dma_start(x[:, g, :], src[b, :, :].rearrange("o p n -> (o p) n")).then_inc(s["x_in"], 16)
                    for g in range(G):
                        b = bass.ds(turn_no * G + g, 1)
                        sp.dma_start(cT[:, :, g, :], t["ctxT"][b, :, :].rearrange("o (k p) m -> (o p) k m", p=128)
                                     ).then_inc(s["ctx_in"], 16)
                        if L2IN:
                            sp.dma_start(ctok[:, g, :], t["ctx_1024"][b, 0:T, :].rearrange("o p n -> (o p) n")
                                         ).then_inc(s["ctx_in"], 16)
                    if first_experts:
                        for slot in range(2):
                            load_expert(sp, t, first_experts[0], slot, slot, first_experts[1][slot], turn_no, TURNS)
                    if next_weights:
                        load_part(sp, t, next_weights, turn_no, TURNS)
                    stores = 0
                    for st in turn.steps:
                        if st[0] != "store":
                            continue
                        g = st[2]
                        b = bass.ds(turn_no * G + g, 1)
                        if which:
                            x_ready(sp, len(layers), g)
                            dst = out if L2IN else x_d
                            sp.dma_start(dst[b, :, :].rearrange("o p n -> (o p) n"), x[:, g, :]).then_inc(s["stored"], 16)
                            stores += 1
                        else:
                            drained(sp, ("rt3", "route", g))
                            sp.wait_ge(s["comb_done"], g + 1)
                            sp.dma_start(acc_d[b, :, :].rearrange("o p n -> (o p) n"), acc[:, g, :]).then_inc(s["stored"], 16)
                            sp.dma_start(comb_d[b, :, :].rearrange("o p n -> (o p) n"), comb[:, g, :]).then_inc(s["stored"], 16)
                            stores += 2
                    if not which:
                        for g in range(G):
                            drained(sp, ("trx", "route", g))
                        sp.dma_start(hT_d[:, :, bass.ds(turn_no * GT, GT)], hT[:]).then_inc(s["stored"], 16)
                        stores += 1
                    sp.wait_ge(s["stored"], 16 * stores)

                @block.tensor
                def _(pe):
                    for st in turn.steps:
                        kind, L, a = st[0], st[1], st[2:]
                        key = (kind, L.name) + a
                        i = index(L)
                        if kind in PSUM_STEPS:
                            u = turn.psum[key]
                            bank = mp[u % NM]
                            bank_free(pe, u)
                        if kind == "trx":
                            g, = a
                            if L.pre:
                                pe.wait_ge(s["xn_done"], turn.xn["lnb", L.name, g] + 1)
                            else:
                                x_ready(pe, i, g)
                            src = xn if L.pre else x
                            for kt in range(KT):
                                last = pe.transpose(bank[:, kt * T:(kt + 1) * T], src[:, g, kt * 128:(kt + 1) * 128],
                                                    ident[0:T, 0:T])
                            last.then_inc(s["mp_full"], 1)
                        elif kind == "ctr":
                            g, = a
                            pe.wait_ge(s["xn_done"], turn.xn["cnb", L.name, g] + 1)
                            for kt in range(KT):
                                last = pe.transpose(bank[:, kt * T:(kt + 1) * T], ctok[:, g, kt * 128:(kt + 1) * 128],
                                                    ident[0:T, 0:T])
                            last.then_inc(s["mp_full"], 1)
                        elif kind in ("fa", "fg"):
                            pair, m = a
                            for g in (2 * pair, 2 * pair + 1):
                                drained(pe, ("trx", L.name, g))
                            pe.wait_ge(w_in[L.w["w1"][0]], loaded)
                            c0 = m * 128 + (FF if kind == "fg" else 0)
                            for kt in range(KT):
                                last = pe.matmul(bank[:, 0:PT2], wtile(L.w["w1"], kt, c0, 128),
                                                 hT[:, kt, pair * PT2:(pair + 1) * PT2], start=kt == 0, stop=kt == KT - 1)
                            last.then_inc(s["mp_full"], 1)
                        elif kind in ("q", "k"):
                            g, m = a
                            src = hT
                            if L.wide and kind == "k":
                                src = cnT
                                drained(pe, ("ctr", L.name, g))
                            else:
                                drained(pe, ("trx", L.name, g))
                            pe.wait_ge(w_in[L.w[kind][0]], loaded)
                            c0 = m * 128
                            for kt in range(KT):
                                last = pe.matmul(bank[:, 0:T], wtile(L.w[kind], kt, c0, 128), src[:, kt, g * T:(g + 1) * T],
                                                 start=kt == 0, stop=kt == KT - 1)
                            last.then_inc(s["mp_full"], 1)
                        elif kind == "v":
                            g = a[0]
                            c0, n = (a[1] * 512, 512) if L.wide else (0, D)
                            src = cnT if L.wide else hT
                            drained(pe, ("ctr" if L.wide else "trx", L.name, g))
                            pe.wait_ge(w_in[L.w["v"][0]], loaded)
                            for kt in range(KT):
                                last = pe.matmul(bank[0:T, 0:n], src[:, kt, g * T:(g + 1) * T],
                                                 wtile(L.w["v"], kt, c0, n), start=kt == 0, stop=kt == KT - 1)
                            last.then_inc(s["mp_full"], 1)
                        elif kind == "kc":
                            g, mt = a
                            pe.wait_ge(s["ctx_in"], 16 * G * (2 if L2IN else 1))
                            pe.wait_ge(w_in[L.w["k"][0]], loaded)
                            for kt in range(KT):
                                last = pe.matmul(bank[:, 0:M], wtile(L.w["k"], kt, mt * 128, 128), cT[:, kt, g, :],
                                                 start=kt == 0, stop=kt == KT - 1)
                            last.then_inc(s["mp_full"], 1)
                        elif kind == "vc":
                            g, c = a
                            pe.wait_ge(s["ctx_in"], 16 * G * (2 if L2IN else 1))
                            pe.wait_ge(w_in[L.w["v"][0]], loaded)
                            for kt in range(KT):
                                last = pe.matmul(bank[0:MC, 0:D], cT[:, kt, g, c * MC:(c + 1) * MC],
                                                 wtile(L.w["v"], kt, 0, D), start=kt == 0, stop=kt == KT - 1)
                            last.then_inc(s["mp_full"], 1)
                        elif kind == "qk":
                            g, n = a
                            j = gpos(L, g, n)
                            if j >= NS:
                                pe.wait_ge(s["exp_done"], j - NS + 1)
                            if n == 0:
                                if L.wide:
                                    for mt in range(8):
                                        drained(pe, ("q", L.name, g, mt))
                                else:
                                    keys = [("ql", L.name, g, mt) for mt in range(KT)]
                                    pe.wait_ge(s["q_dve"], max(turn.mask_dve.get(k, -1) for k in keys) + 1)
                                    pe.wait_ge(s["q_pool"], max(turn.mask_pool.get(k, -1) for k in keys) + 1)
                                for mt in range(8 if L.wide else KT):
                                    operand(pe, ("kc" if L.cross else "k", L.name, g, mt), L)
                            Sx = Sb[j % NS]
                            kk = M if L.cross else T
                            if L.causal:
                                pe.matmul(Sx[0:T, 0:4 * T], ident16[0:T, 0:T], causal16[:], start=True, stop=False)
                            for hi, h in enumerate(heads(L, n)):
                                o = Sx[0:T, hi * kk:(hi + 1) * kk]
                                gs = slice(g * T, (g + 1) * T)
                                mt, par = h // (2 if L.wide else 8), h % 2
                                if L.wide:
                                    r = slice(64 * par, 64 * par + 64)
                                    q = lambda l: q2[g][r, mt, l, :]
                                    k = lambda l: k2[g][r, mt, l, :]
                                else:
                                    if L.quant:
                                        q = lambda l: qmb[:, g, 0, mt, h % 8, :]
                                        k = lambda l: kCb[g][:, mt, :] if L.cross else kSb[:, mt, gs]
                                    else:
                                        q = lambda l: qm[:, g, l, mt, h % 8, :]
                                        k = lambda l: kC[g][:, l, mt, :] if L.cross else kS[:, l, mt, gs]
                                terms = [(0, 0)] if L.quant else [(0, 0), (0, 1), (1, 0)]
                                for ti, (lq, lk) in enumerate(terms):
                                    last = pe.matmul(o, q(lq), k(lk), start=ti == 0 and not L.causal,
                                                     stop=ti == len(terms) - 1 and
                                                     (not L.causal or hi == len(heads(L, n)) - 1))
                            last.then_inc(s["s_full"], 1)
                        elif kind == "tp":
                            g, n = a
                            j = gpos(L, g, n)
                            split_ready(pe, L, g, n)
                            if j >= NT:
                                pe.wait_ge(s["pt_done"], j - NT + 1)
                            kk, nch = shapes(L)
                            nb = nch * len(heads(L, n))
                            for b_ in range(nb if L.quant else 2 * nb):
                                src, dst, one = (Psb, Tbb, ident16) if L.quant else (Ps, Tb, identh)
                                at = b_ * kk
                                last = pe.transpose(dst[j % NT][:, b_ * T:(b_ + 1) * T],
                                                    src[:, j % RP, at:at + 128], one[0:T, 0:T])
                            last.then_inc(s["tp_done"], 1)
                        elif kind == "av":
                            g, n = a
                            j = gpos(L, g, n)
                            half = n // 2 if L.wide else 0
                            ou = turn.obank[L.name, g, half]
                            if n % 2 == 0 and L.wide or n == 0:
                                if ou >= 1:
                                    pe.wait_ge(s["fin_done"], ou)
                                if L.cross:
                                    for c in range(C):
                                        operand(pe, ("vc", L.name, g, c), L)
                                elif L.wide:
                                    for hv in range(2):
                                        operand(pe, ("v", L.name, g, hv), L)
                                else:
                                    operand(pe, ("v", L.name, g), L)
                            pe.wait_ge(s["pt_done"], j + 1)
                            kk, nch = shapes(L)
                            pt = PTb if L.quant else PT
                            nb = nch * len(heads(L, n))
                            for hi, h in enumerate(heads(L, n)):
                                for c in range(nch):
                                    if L.wide:
                                        ho = h - 8 * half
                                        o = Ob[:, ho * HD2:(ho + 1) * HD2]
                                        parts = [(0, v2[g][:, 0, h * HD2:(h + 1) * HD2]),
                                                 (0, v2[g][:, 1, h * HD2:(h + 1) * HD2]),
                                                 (1, v2[g][:, 0, h * HD2:(h + 1) * HD2])]
                                    elif L.quant:
                                        o = Ob[:, h * HD:(h + 1) * HD]
                                        vv = vCb[g][:, c, h * HD:(h + 1) * HD] if L.cross else vSb[:, g, h * HD:(h + 1) * HD]
                                        parts = [(0, vv)]
                                    else:
                                        o = Ob[:, h * 2 * HD:(h + 1) * 2 * HD]
                                        vv = vC[g][:, c, h] if L.cross else vS[:, g, h]
                                        vv = vv.rearrange("p l d -> p (l d)")
                                        parts = [(0, vv), (1, vv)]
                                    for pi, (l, vv) in enumerate(parts):
                                        b_ = l * nb + hi * nch + c
                                        last = pe.matmul(o, pt[0:kk, j % 2, b_ * T:b_ * T + 128], vv,
                                                         start=c == 0 and pi == 0,
                                                         stop=c == nch - 1 and pi == len(parts) - 1)
                            last.then_inc(s["av_done"], 1)
                        elif kind == "tro":
                            g, half = a
                            ou = turn.obank[L.name, g, half]
                            pe.wait_ge(s["fin_done"], ou + 1)
                            for kt in range(4 if L.wide else KT):
                                last = pe.transpose(bank[:, kt * T:(kt + 1) * T],
                                                    Osb[:, ou % 2, kt * 128:(kt + 1) * 128], ident[0:T, 0:T])
                            last.then_inc(s["mp_full"], 1)
                        elif kind == "wo":
                            g, = a
                            nk = 8 if L.wide else KT
                            for half in range(2 if L.wide else 1):
                                drained(pe, ("tro", L.name, g, half))
                            pe.wait_ge(w_in[L.w["o"][0]], loaded)
                            for kt in range(nk):
                                last = pe.matmul(bank[0:T, 0:D], OT[:, g % 2, kt, :], wtile(L.w["o"], kt, 0, D),
                                                 start=kt == 0, stop=kt == nk - 1)
                            last.then_inc(s["mp_full"], 1)
                        elif kind == "f2":
                            g, = a
                            for m in range(FT):
                                drained(pe, ("fa", L.name, g // 2, m))
                            pe.wait_ge(w_in[L.w["w2"][0]], loaded)
                            for m in range(FT):
                                last = pe.matmul(bank[0:T, 0:D], hf[g // 2][:, m, (g % 2) * T:(g % 2 + 1) * T],
                                                 wtile(L.w["w2"], m, 0, D), start=m == 0, stop=m == FT - 1)
                            last.then_inc(s["mp_full"], 1)
                        elif kind == "rt1":
                            g, = a
                            drained(pe, ("trx", L.name, g))
                            pe.wait_ge(w_in["L0_xattn_router_w"], loaded)
                            for kt in range(KT):
                                last = pe.matmul(bank[0:T, 0:E], hT[:, kt, g * T:(g + 1) * T],
                                                 weight["L0_xattn_router_w"][:, kt, :], start=kt == 0, stop=kt == KT - 1)
                            last.then_inc(s["mp_full"], 1)
                        elif kind == "rt2":
                            g, = a
                            pe.wait_ge(s["comb_done"], g + 1)
                            pe.transpose(bank[0:E, 0:T], comb[:, g, :], ident[0:T, 0:T]).then_inc(s["mp_full"], 1)
                        elif kind == "rt3":
                            g, = a
                            drained(pe, ("rt2", L.name, g))
                            pe.matmul(bank[0:T, 0:D], cbT[:, g, :], eb2[:], start=True, stop=True).then_inc(s["mp_full"], 1)

                @block.scalar
                def _(act):
                    for st in turn.steps:
                        kind, L, a = st[0], st[1], st[2:]
                        key = (kind, L.name) + a
                        if kind in KEYS and L.quant:
                            buf, _, inv = quant_buffer(key)
                            filled(act, key)
                            raw_free(act, key)
                            act.activation(buf, mp[turn.psum[key] % NM][0:buf.shape[0], 0:buf.shape[1]], ACT.Copy,
                                           bias=MAGIC, scale=inv).then_inc(drain_mark(key), 1)
                        elif kind in KEYS:
                            src, hi, _, bias = kv_split(key, L)
                            filled(act, key)
                            if bias is None:
                                ins = act.activation(hi, src, ACT.Copy)
                            else:
                                ins = act.activation(hi, src, ACT.Identity, bias=bias)
                            ins.then_inc(s["kv_hi"], 1)
                        elif kind == "ex":
                            g, n = a
                            j = gpos(L, g, n)
                            if L.quant or L.wide:
                                act.wait_ge(s["neg_scaled"], turn.rescaled[L.name, g, n] + 1)
                            else:
                                act.wait_ge(s["max_done"], turn.unscaled[L.name, g, n] + 1)
                            if j >= RP:
                                split_ready(act, *by_pos[j - RP])
                            kk = M if L.cross else T
                            for hi, h in enumerate(heads(L, n)):
                                cs = slice(hi * kk, (hi + 1) * kk)
                                m_ = negs if L.quant or L.wide else negm
                                sc = dmul[0:T, 2 * (L.quant - 1):2 * (L.quant - 1) + 1] if L.quant else (
                                    HD2 ** -0.5 if L.wide else 1.0)
                                last = act.activation(P[:, j % RP, cs], Sb[j % NS][0:T, cs], ACT.Exp,
                                                      bias=m_[:, j % 4, hi:hi + 1], scale=sc,
                                                      accum_out=sums[:, g, h:h + 1])
                            last.then_inc(s["exp_done"], 1)
                        elif kind == "sp" and L.cross:
                            g, n = a
                            j = gpos(L, g, n)
                            act.wait_ge(s["exp_done"], j + 1)
                            if L.quant:
                                act.wait_ge(s["rq_done"], turn.scaled[L.name, g, n] + 1)
                                act.activation(P[:, j % RP, 0:M], P[:, j % RP, 0:M], ACT.Copy, bias=MAGIC,
                                               scale=rq[:, j % 4, 0:1]).then_inc(s["scaled"], 1)
                            else:
                                if j >= RP:
                                    act.wait_ge(s["tp_done"], j - RP + 1)
                                act.activation(Ps[:, j % RP, 0:M], P[:, j % RP, 0:M], ACT.Copy).then_inc(s["hi_act"], 1)
                        elif kind == "fg":
                            g, m = a
                            filled(act, key)
                            if turn.at[key] >= MRUN:
                                drained(act, ("fa", L.name) + divmod(turn.at[key] - MRUN, FT))
                            act.activation(gl[:, m % MRUN, :], mp[turn.psum[key] % NM][:, 0:PT2], ACT.Gelu,
                                           bias=col(L.w["b1"][0], FT + m)).then_inc(drain_mark(key), 1)
                        elif kind == "fa" and L.kind == "gelu":
                            g, m = a
                            filled(act, key)
                            act.activation(hf[g][:, m, :], mp[turn.psum[key] % NM][:, 0:PT2], ACT.Gelu,
                                           bias=col(L.w["b1"][0], m)).then_inc(drain_mark(key), 1)
                        elif kind == "rt1":
                            g, = a
                            act.wait_ge(s["rt_sum"], g + 1)
                            act.activation(ex[:, g, :], lg[:, g, :], ACT.Exp, bias=rt[:, g, 0:1],
                                           accum_out=rt[:, g, 1:2]).then_inc(s["rt_exp"], 1)
                            act.wait_ge(s["rt_gap"], g + 1)
                            act.activation(rt[:, g, 4:5], rt[:, g, 3:4], ACT.Exp).then_inc(s["rt_w"], 1)
                        elif kind == "rt2":
                            g, = a
                            filled(act, key)
                            act.activation(cbT[:, g, :], mp[turn.psum[key] % NM][0:E, 0:T], ACT.Copy
                                           ).then_inc(drain_mark(key), 1)

                @block.gpsimd
                def _(pool):
                    for st in turn.steps:
                        kind, L, a = st[0], st[1], st[2:]
                        key = (kind, L.name) + a
                        if kind == "xb":
                            g, = a
                            x_ready(pool, index(L), g)
                            pool.tensor_tensor(xb[:, g, :], x[:, g, :], row(L.row), ALU.add
                                               ).then_inc(s["xb_done"], 1)
                        elif kind == "ql" and key in turn.mask_pool:
                            g, mt = a
                            if L.quant:
                                operand(pool, ("q", L.name, g, mt), L)
                                src, dst = qsb[:, g, 0, mt, :], qmb[:, g, 0, mt]
                            else:
                                drained(pool, ("q", L.name, g, mt))
                                src, dst = qs[:, g, 1, mt, :], qm[:, g, 1, mt]
                            pool.tensor_tensor(dst, src.unsqueeze(1).to_broadcast([128, 8, T]),
                                               head_masks.unsqueeze(2).to_broadcast([128, 8, T]), ALU.mult
                                               ).then_inc(s["q_pool"], 1)
                        elif kind in ("lna", "cln", "pna"):
                            ln, slot = turn.lnorm[key], norm_slot(key)
                            pool.wait_ge(s["stat_done"], ln + 1)
                            pool.tensor_scalar(nrm[:, slot, 0:1], mv[:, slot, 1:2], EPS, None, ALU.add
                                               ).then_inc(s["ln_half"], 1)
                            pool.wait_ge(s["ln_half"], ln + 1)
                            pool.tensor_tensor(nrm[:, slot, 1:2], nrm[:, slot, 0:1], neghalf[0:T, :], ALU.pow
                                               ).then_inc(s["rstd_done"], 1)
                        elif kind in KEYS and L.quant:
                            buf, dst, _ = quant_buffer(key)
                            pool.wait_ge(s["clipped"], turn.quant[key] + 1)
                            pool.tensor_scalar(dst, buf, MAGIC, None, ALU.subtract).then_inc(s["int_done"], 1)
                        elif kind == "qk" and (L.quant or L.wide):
                            g, n = a
                            j, nh = gpos(L, g, n), len(heads(L, n))
                            scale = dmul[0:T, 2 * (L.quant - 1):2 * (L.quant - 1) + 1] if L.quant else HD2 ** -0.5
                            pool.wait_ge(s["neg_max"], turn.rescaled[L.name, g, n] + 1)
                            pool.tensor_scalar(negs[:, j % 4, 0:nh], negm[:, j % 4, 0:nh], scale, None,
                                               ALU.mult).then_inc(s["neg_scaled"], 1)
                        elif kind == "sp":
                            g, n = a
                            j = gpos(L, g, n)
                            w_ = len(heads(L, n)) * (M if L.cross else T)
                            if not L.quant:
                                if L.cross:
                                    pool.wait_ge(s["hi_act"], turn.high_act[L.name, g, n] + 1)
                                else:
                                    pool.wait_ge(s["hi_dve"], turn.high_dve[L.name, g, n] + 1)
                                pool.tensor_tensor(Ps[:, j % RP, w_:2 * w_], P[:, j % RP, 0:w_], Ps[:, j % RP, 0:w_],
                                                   ALU.subtract).then_inc(s["split_lo"], 1)

                @block.vector
                def _(dve):
                    chain = [0]

                    def link(ins):
                        chain[0] += 1
                        ins.then_inc(s["dve_chain"], 1)
                        dve.wait_ge(s["dve_chain"], chain[0])

                    def statistics(src, key):
                        slot = norm_slot(key)
                        link(dve.bn_stats(stats[:, slot, :], src))
                        dve.bn_aggr(mv[:, slot, :], stats[:, slot, :]).then_inc(s["stat_done"], 1)

                    def refine(key):
                        ln, slot = turn.lnorm[key], norm_slot(key)
                        v = mv[:, slot, 1:2]
                        n = nrm[:, slot, :]
                        dve.wait_ge(s["rstd_done"], ln + 1)
                        link(dve.tensor_scalar(n[:, 2:3], v, EPS, n[:, 1:2], ALU.add, ALU.mult))
                        link(dve.tensor_scalar(n[:, 2:3], n[:, 2:3], n[:, 1:2], -0.5, ALU.mult, ALU.mult))
                        link(dve.tensor_scalar(n[:, 3:4], n[:, 2:3], 1.5, n[:, 1:2], ALU.add, ALU.mult))

                    def normalize(dst, src, key):
                        slot = norm_slot(key)
                        return dve.tensor_scalar(dst, src, mv[:, slot, 0:1], nrm[:, slot, 3:4],
                                                 ALU.subtract, ALU.mult)

                    for st in turn.steps:
                        kind, L, a = st[0], st[1], st[2:]
                        key = (kind, L.name) + a
                        i = index(L)
                        if kind in PSUM_STEPS:
                            bank = mp[turn.psum[key] % NM]
                        if kind == "ql" and L.quant:
                            g, mt = a
                            if key in turn.mask_dve:
                                operand(dve, ("q", L.name, g, mt), L)
                                for h8 in range(8):
                                    last = dve.tensor_scalar(qmb[:, g, 0, mt, h8, :], qsb[:, g, 0, mt, :],
                                                             head_mask[h8], None, ALU.mult)
                                last.then_inc(s["q_dve"], 1)
                        elif kind == "lna":
                            g, = a
                            x_ready(dve, i, g)
                            statistics(x[:, g, :], key)
                        elif kind == "lnb":
                            g, = a
                            norm = ("lna", L.name, g)
                            refine(norm)
                            normalize(xn[:, g, :], x[:, g, :], norm).then_inc(s["xn_done"], 1)
                        elif kind == "cln":
                            g, = a
                            dve.wait_ge(s["ctx_in"], 16 * G * 2)
                            statistics(ctok[:, g, :], key)
                        elif kind == "cnb":
                            g, = a
                            norm = ("cln", L.name, g)
                            refine(norm)
                            normalize(ctok[:, g, :], ctok[:, g, :], norm).then_inc(s["xn_done"], 1)
                        elif kind == "pna":
                            g, = a
                            if L.kind == "norm":
                                x_ready(dve, i, g)
                            else:
                                drained(dve, ("wo", L.name, g))
                            statistics(x[:, g, :], key)
                        elif kind == "pnb":
                            g, = a
                            norm = ("pna", L.name, g)
                            refine(norm)
                            link(normalize(x[:, g, :], x[:, g, :], norm))
                            link(dve.tensor_tensor(x[:, g, :], x[:, g, :], row(L.post[0]), ALU.mult))
                            dve.tensor_tensor(x[:, g, :], x[:, g, :], row(L.post[1]), ALU.add
                                              ).then_inc(s["x_done"], 1)
                        elif kind in ("trx", "ctr"):
                            g, = a
                            filled(dve, key)
                            dst = hT if kind == "trx" else cnT
                            if L.pre:
                                for kt in range(KT):
                                    last = dve.tensor_scalar(dst[:, kt, g * T:(g + 1) * T], bank[:, kt * T:(kt + 1) * T],
                                                             col(L.pre[0], kt), col(L.pre[1], kt), ALU.mult, ALU.add)
                            else:
                                last = dve.tensor_copy(dst[:, :, g * T:(g + 1) * T],
                                                       bank[:, 0:KT * T].rearrange("p (k n) -> p k n", k=KT))
                            last.then_inc(drain_mark(key), 1)
                        elif kind in KEYS and L.quant:
                            buf, _, _ = quant_buffer(key)
                            drained(dve, key)
                            dve.tensor_scalar(buf, buf, MAGIC - 128.0, MAGIC + 127.0, ALU.max, ALU.min
                                              ).then_inc(s["clipped"], 1)
                        elif kind in KEYS:
                            src, hi, lo, bias = kv_split(key, L)
                            dve.wait_ge(s["kv_hi"], turn.split[key] + 1)
                            if bias is None:
                                ins = dve.tensor_tensor(lo, src, hi, ALU.subtract)
                            else:
                                ins = dve.scalar_tensor_tensor(lo, src, bias, hi, ALU.add, ALU.subtract)
                            ins.then_inc(drain_mark(key), 1)
                        elif kind == "ql":
                            g, mt = a
                            drained(dve, ("q", L.name, g, mt))
                            for h8 in range(8):
                                last = dve.tensor_scalar(qm[:, g, 0, mt, h8, :], qs[:, g, 0, mt, :], head_mask[h8],
                                                         None, ALU.mult)
                            last.then_inc(s["q_dve"], 1)
                        elif kind == "qk":
                            g, n = a
                            j = gpos(L, g, n)
                            nh = len(heads(L, n))
                            kk = M if L.cross else T
                            dve.wait_ge(s["s_full"], j + 1)
                            ins = dve.tensor_reduce(negm[:, j % 4, 0:nh],
                                                    Sb[j % NS][0:T, 0:nh * kk].rearrange("p (h k) -> p h k", h=nh),
                                                    AX.X, ALU.max, negate=True)
                            ins.then_inc(s["neg_max" if L.quant or L.wide else "max_done"], 1)
                        elif kind == "sp" and not L.quant:
                            if not L.cross:
                                g, n = a
                                j = gpos(L, g, n)
                                w_ = len(heads(L, n)) * T
                                dve.wait_ge(s["exp_done"], j + 1)
                                if j >= RP:
                                    dve.wait_ge(s["tp_done"], j - RP + 1)
                                dve.tensor_copy(Ps[:, j % RP, 0:w_], P[:, j % RP, 0:w_]).then_inc(s["hi_dve"], 1)
                        elif kind == "sp":
                            g, n = a
                            j = gpos(L, g, n)
                            nh = len(heads(L, n))
                            kk = M if L.cross else T
                            dw = dinv[0:T, 4 * L.quant - 1:4 * L.quant]
                            dve.wait_ge(s["exp_done"], j + 1)
                            if L.cross:
                                link(dve.reciprocal(rinv[:, j % 4, 0:1], sums[:, g, n:n + 1]))
                            else:
                                link(dve.reciprocal(rinv[:, j % 4, 0:4].rearrange("p (a b) -> p a b", a=2),
                                                    sums[:, g, :].rearrange("p (a c) -> p a c", a=2)[:, :, 2 * n:2 * n + 2]))
                            ins = dve.tensor_scalar(rq[:, j % 4, 0:nh], rinv[:, j % 4, 0:nh], dw, None, ALU.mult)
                            if L.cross:
                                ins.then_inc(s["rq_done"], 1)
                            else:
                                link(ins)
                            if not L.cross:
                                for hi, h in enumerate(heads(L, n)):
                                    cs = slice(hi * kk, (hi + 1) * kk)
                                    last = dve.tensor_scalar(P[:, j % RP, cs], P[:, j % RP, cs], rq[:, j % 4, hi:hi + 1],
                                                             MAGIC, ALU.mult, ALU.add)
                                last.then_inc(s["scaled_dve"], 1)
                        elif kind == "sr":
                            g, n = a
                            j = gpos(L, g, n)
                            w_ = len(heads(L, n)) * (M if L.cross else T)
                            if L.cross:
                                dve.wait_ge(s["scaled"], turn.scaled[L.name, g, n] + 1)
                            else:
                                dve.wait_ge(s["scaled_dve"], turn.whole[L.name, g, n] + 1)
                            if j >= RP:
                                dve.wait_ge(s["tp_done"], j - RP + 1)
                            dve.tensor_scalar(Psb[:, j % RP, 0:w_], P[:, j % RP, 0:w_], MAGIC, 255.0,
                                              ALU.subtract, ALU.min).then_inc(s["split_int"], 1)
                        elif kind == "tp":
                            g, n = a
                            j = gpos(L, g, n)
                            kk, nch = shapes(L)
                            w_ = nch * len(heads(L, n)) * T * (1 if L.quant else 2)
                            dve.wait_ge(s["tp_done"], j + 1)
                            if j >= 2:
                                dve.wait_ge(s["av_done"], j - 1)
                            dve.tensor_copy(PT[0:kk, j % 2, 0:w_], Tb[j % NT][0:kk, 0:w_]).then_inc(s["pt_done"], 1)
                        elif kind == "fin":
                            g, half = a
                            ou = turn.obank[L.name, g, half]
                            last_group = (half + 1) * len(L.groups) // (2 if L.wide else 1) - 1
                            if ou >= 2:
                                prev = [k for k, v in turn.obank.items() if v == ou - 2][0]
                                dve.wait_ge(s["mp_full"], turn.psum[("tro",) + prev] + 1)
                            if L.quant:
                                dve.wait_ge(s["av_done"], gpos(L, g, last_group) + 1)
                                qi = 2 * (L.quant - 1) + 1
                                dve.tensor_scalar(Osb[:, ou % 2, 0:D], Ob[0:T, 0:D], dmul[0:T, qi:qi + 1], None,
                                                  ALU.mult).then_inc(s["fin_done"], 1)
                            else:
                                nh, hd = (8, HD2) if L.wide else (H, HD)
                                hs = slice(half * nh, half * nh + nh)
                                dve.wait_ge(s["exp_done"], gpos(L, g, last_group) + 1)
                                link(dve.reciprocal(rsum[:, g % 2, hs], sums[:, g, hs]))
                                dve.wait_ge(s["av_done"], gpos(L, g, last_group) + 1)
                                osb = Osb[:, ou % 2, 0:nh * hd].rearrange("p (h d) -> p h d", h=nh)
                                if L.wide:
                                    src = Ob[0:T, 0:nh * hd].rearrange("p (h d) -> p h d", h=nh)
                                else:
                                    src = osb
                                    link(dve.tensor_reduce(osb, Ob[0:T, 0:2 * nh * hd].rearrange(
                                        "p (h l d) -> p h d l", h=nh, l=2), AX.X, ALU.add))
                                dve.tensor_tensor(osb, src, rsum[:, g % 2, hs].unsqueeze(2).to_broadcast([T, nh, hd]),
                                                  ALU.mult).then_inc(s["fin_done"], 1)
                        elif kind == "tro":
                            g, half = a
                            nk = 4 if L.wide else KT
                            filled(dve, key)
                            dst = OT[:, g % 2, half * nk:(half + 1) * nk, :]
                            src = bank[:, 0:nk * T].rearrange("p (k n) -> p k n", k=nk)
                            if "bv" in L.w:
                                c0 = COLS[L.w["bv"][0]][0] + L.w["bv"][1] + half * nk
                                ins = dve.tensor_tensor(dst, src, cols[:, c0:c0 + nk].unsqueeze(2).to_broadcast([128, nk, T]),
                                                        ALU.add)
                            else:
                                ins = dve.tensor_copy(dst, src)
                            ins.then_inc(drain_mark(key), 1)
                        elif kind in ("wo", "f2"):
                            g, = a
                            filled(dve, key)
                            dve.wait_ge(s["xb_done"], turn.at["xb", L.name, g] + 1)
                            dve.tensor_tensor(x[:, g, :], bank[0:T, 0:D], xb[:, g, :], ALU.add
                                              ).then_inc(drain_mark(key), 1)
                        elif kind == "fa" and L.kind == "geglu":
                            g, m = a
                            filled(dve, key)
                            drained(dve, ("fg", L.name, g, m))
                            dve.scalar_tensor_tensor(hf[g][:, m, :], bank[:, 0:PT2], col(L.w["b1"][0], m), gl[:, m % MRUN, :],
                                                     ALU.add, ALU.mult).then_inc(drain_mark(key), 1)
                        elif kind == "rt1":
                            g, = a
                            r = rt[:, g, :]
                            filled(dve, key)
                            dve.tensor_tensor(lg[:, g, :], bank[0:T, 0:E], rb_row[:], ALU.add
                                              ).then_inc(drain_mark(key), 1)
                            drained(dve, key)
                            dve.tensor_reduce(r[:, 0:1], lg[:, g, :], AX.X, ALU.max, negate=True).then_inc(s["rt_sum"], 1)
                            dve.wait_ge(s["rt_exp"], g + 1)
                            link(dve.reciprocal(r[:, 2:3], r[:, 1:2]))
                            link(dve.tensor_scalar(pr[:, g, :], ex[:, g, :], r[:, 2:3], None, ALU.mult))
                            link(dve.max(top[:, g, :], pr[:, g, :]))
                            link(dve.max_index(topi[:, g, :], top[:, g, :], pr[:, g, :]))
                            dve.tensor_tensor(r[:, 3:4], top[:, g, 1:2], top[:, g, 0:1], ALU.subtract).then_inc(s["rt_gap"], 1)
                            dve.tensor_copy(topf[:, g, :], topi[:, g, :])
                            dve.wait_ge(s["rt_w"], g + 1)
                            link(dve.tensor_scalar(r[:, 5:6], r[:, 4:5], 1.0, None, ALU.add))
                            link(dve.reciprocal(r[:, 6:7], r[:, 5:6]))
                            link(dve.tensor_tensor(r[:, 7:8], r[:, 6:7], r[:, 4:5], ALU.mult))
                            dve.tensor_scalar(c1[:, g, :], iota[:], topf[:, g, 0:1], r[:, 6:7], ALU.is_equal, ALU.mult)
                            link(dve.tensor_scalar(c2[:, g, :], iota[:], topf[:, g, 1:2], r[:, 7:8], ALU.is_equal, ALU.mult))
                            dve.tensor_tensor(comb[:, g, :], c1[:, g, :], c2[:, g, :], ALU.add).then_inc(s["comb_done"], 1)
                        elif kind == "rt3":
                            g, = a
                            filled(dve, key)
                            dve.tensor_tensor(acc[:, g, :], bank[0:T, 0:D], x[:, g, :], ALU.add
                                              ).then_inc(drain_mark(key), 1)

            with nc.Block() as block:
                @block.sync
                def _(sp):
                    for v in s.values():
                        sp.sem_clear(v)


SCALE = 256.0


def experts_pass(nc, t, env, next_weights, scratch, w_in):
    hT_d, acc_d, comb_d = env["hT_d"], env["acc_d"], env["comb_d"]
    HALF = B * T // 2
    BH = B // 2
    NW1, NW2 = KT * FF, FT * D
    RH = 4
    with ExitStack() as ctx:
        def sb(name, shape, dt=F32):
            return ctx.enter_context(nc.sbuf_tensor("b_" + name, shape, dt))

        def sem(name):
            return ctx.enter_context(nc.semaphore("b_" + name))

        h_in = scratch["L3_xattn_fc_w"][:].rearrange("p k n -> p (k n)")[:, 0:KT * B * T]
        stage = [expert_stage(scratch, slot) for slot in range(2)]
        h = sb("h", [128, 2, KT * B * T], F16)
        acc = sb("acc", [T, B, D])
        comb = sb("comb", [T, B, E])
        ce = sb("ce", [T, 2, B])
        w1 = sb("w1", [128, 2, 2, NW1], F16)
        w2 = sb("w2", [128, 2, 2, NW2], F16)
        b1_in = sb("b1_in", [128, E, FT])
        b1 = sb("b1", [128, 2, FT])
        hid = sb("hid", [128, RH, HALF])
        hs = sb("hid_split", [128, 2, 2, FT, HALF + 128 - T], F16)
        hp = [ctx.enter_context(nc.psum_tensor(f"b_hidden{i}", [128, 512], F32)) for i in range(4)]
        yp = [ctx.enter_context(nc.psum_tensor(f"b_out{i}", [128, 512], F32)) for i in range(4)]
        in_once, pad_done = sem("in_once"), sem("pad_done")
        turn_sems = {n: sem(n) for n in ["w_hi", "w_lo", "h_full", "h_free", "hid_hi", "hid_lo", "y_full", "y_free",
                                         "ce_done"]}
        w_hi, w_lo, h_full, h_free, hid_hi, hid_lo, y_full, y_free, ce_done = turn_sems.values()
        stored = sem("stored")
        h_hi, h_done = sem("in_hi"), sem("in_lo")
        first_hi, first_lo = sem("first_hi"), sem("first_lo")
        TERMS = [(0, 0), (0, 1), (1, 0)]

        def split_high(act, slot, loaded, hi):
            act.wait_ge(w_in[slot], loaded)
            for i, w in enumerate((w1, w2)):
                act.activation(w[:, slot, 0, :], stage[slot][i], ACT.Copy, scale=SCALE).then_inc(hi, 1)

        def split_low(dve, slot, hi, before, lo):
            for i, w in enumerate((w1, w2)):
                dve.wait_ge(hi, before + i + 1)
                dve.scalar_tensor_tensor(w[:, slot, 1, :], stage[slot][i], SCALE, w[:, slot, 0, :],
                                         ALU.mult, ALU.subtract).then_inc(lo, 1)

        with nc.Block() as block:
            @block.sync
            def _(sp):
                sp.dma_start(h_in.rearrange("p (k n) -> p k n", k=KT), hT_d).then_inc(in_once, 16)
                sp.dma_start(acc[:], acc_d.rearrange("b p n -> p b n")).then_inc(in_once, 16)
                sp.dma_start(comb[:], comb_d.rearrange("b p n -> p b n")).then_inc(in_once, 16)
                sp.dma_start(b1_in[:], t["e_b1T"].rearrange("e p n -> p e n")).then_inc(in_once, 16)
                load_weights(sp, t, next_weights)
                sp.wait_ge(in_once, 64)

            @block.vector
            def _(dve):
                dve.memset(hs[:].rearrange("p s l m n -> p (s l m) n")[:, :, HALF:], 0.0).then_inc(pad_done, 1)
                dve.wait_ge(in_once, 64)
                dve.wait_ge(h_hi, 1)
                dve.scalar_tensor_tensor(h[:, 1, :], h_in, SCALE, h[:, 0, :], ALU.mult, ALU.subtract
                                         ).then_inc(h_done, 1)
                dve.wait_ge(h_done, 1)
                split_low(dve, 0, first_hi, 0, first_lo)

            @block.scalar
            def _(act):
                act.wait_ge(in_once, 64)
                act.activation(h[:, 0, :], h_in, ACT.Copy, scale=SCALE).then_inc(h_hi, 1)
                split_high(act, 0, 32 * TURNS, first_hi)

        units = [(slot, half) for slot in range(2) for half in range(2)]
        with nc.Fori(0, E // 2) as pair:
            with nc.Block() as block:
                @block.sync
                def _(sp):
                    load_expert(sp, t, scratch, 0, (pair * 2 + 2) % E, w_in[0])
                    sp.wait_ge(w_lo, 2)
                    load_expert(sp, t, scratch, 1, (pair * 2 + 3) % E, w_in[1])

                @block.tensor
                def _(pe):
                    def hidden(n):
                        slot, half = units[n]
                        if slot == 1:
                            pe.wait_ge(w_lo, 1)
                        for m in range(FT):
                            u = n * FT + m
                            if u >= 4:
                                pe.wait_ge(h_free, u - 3)
                            for kt in range(KT):
                                for ti, (lw, lh) in enumerate(TERMS):
                                    last = pe.matmul(hp[u % 4][:, 0:HALF],
                                                     w1[:, slot, lw, kt * FF + m * 128:kt * FF + (m + 1) * 128],
                                                     h[:, lh, kt * B * T + half * HALF:kt * B * T + (half + 1) * HALF],
                                                     start=kt == 0 and ti == 0, stop=kt == KT - 1 and ti == 2)
                            last.then_inc(h_full, 1)

                    def output(n):
                        slot, half = units[n]
                        if slot == 1:
                            pe.wait_ge(w_lo, 2)
                        pe.wait_ge(hid_lo, (n + 1) * FT)
                        for b in range(BH):
                            u = n * BH + b
                            if u >= 4:
                                pe.wait_ge(y_free, u - 3)
                            for m in range(FT):
                                for ti, (lh, lw) in enumerate(TERMS):
                                    last = pe.matmul(yp[u % 4][:, 0:D], hs[:, n % 2, lh, m, b * T:b * T + 128],
                                                     w2[:, slot, lw, m * D:(m + 1) * D],
                                                     start=m == 0 and ti == 0, stop=m == FT - 1 and ti == 2)
                            last.then_inc(y_full, 1)

                    hidden(0)
                    for n in range(1, len(units)):
                        hidden(n)
                        output(n - 1)
                    output(len(units) - 1)

                @block.scalar
                def _(act):
                    act.wait_ge(ce_done, 4)
                    for n, (slot, half) in enumerate(units):
                        for m in range(FT):
                            u = n * FT + m
                            act.wait_ge(h_full, u + 1)
                            if u >= RH:
                                act.wait_ge(hid_lo, u - RH + 1)
                            act.activation(hid[:, u % RH, :], hp[u % 4][:, 0:HALF], ACT.Gelu,
                                           bias=b1[:, slot, m:m + 1], scale=SCALE ** -2).then_inc(h_free, 1)
                        if n == 0:
                            split_high(act, 1, 32 * (pair + TURNS), w_hi)
                        elif n == 3:
                            act.wait_ge(y_full, 2 * BH)
                            split_high(act, 0, 32 * (pair + TURNS + 1), w_hi)

                @block.vector
                def _(dve):
                    def weigh(n, b):
                        slot, half = units[n]
                        u = n * BH + b
                        tile = half * BH + b
                        dve.wait_ge(y_full, u + 1)
                        if n >= 2:
                            dve.wait_ge(y_free, (n - 2) * BH + b + 1)
                        dve.scalar_tensor_tensor(acc[:, tile, :], yp[u % 4][0:T, 0:D], ce[:, slot, tile:tile + 1],
                                                 acc[:, tile, :], ALU.mult, ALU.add).then_inc(y_free, 1)

                    for slot in range(2):
                        dve.tensor_copy(b1[:, slot, :], b1_in[:, bass.ds(pair * 2 + slot, 1), :].rearrange("p o n -> p (o n)")
                                        ).then_inc(ce_done, 1)
                        dve.tensor_scalar(ce[:, slot, :], comb[:, :, bass.ds(pair * 2 + slot, 1)].rearrange("p b o -> p (b o)"),
                                          SCALE ** -1, None, ALU.mult).then_inc(ce_done, 1)
                    dve.wait_ge(ce_done, 4)
                    for n, (slot, half) in enumerate(units):
                        for m in range(FT):
                            u = n * FT + m
                            dve.wait_ge(h_free, u + 1)
                            if n >= 2 and m == 0:
                                dve.wait_ge(y_full, (n - 1) * BH)
                            dve.tensor_copy(hs[:, n % 2, 0, m, 0:HALF], hid[:, u % RH, :]).then_inc(hid_hi, 1)
                            dve.wait_ge(hid_hi, u + 1)
                            dve.tensor_tensor(hs[:, n % 2, 1, m, 0:HALF], hid[:, u % RH, :], hs[:, n % 2, 0, m, 0:HALF],
                                              ALU.subtract).then_inc(hid_lo, 1)
                            if n >= 2 and m % 2 == 1:
                                weigh(n - 2, m // 2)
                        if n == 0:
                            split_low(dve, 1, w_hi, 0, w_lo)
                    for b in range(BH):
                        weigh(len(units) - 2, b)
                    split_low(dve, 0, w_hi, 2, w_lo)
                    for b in range(BH):
                        weigh(len(units) - 1, b)
            with nc.Block() as block:
                @block.sync
                def _(sp):
                    for v in turn_sems.values():
                        sp.sem_clear(v)

        with nc.Block() as block:
            @block.sync
            def _(sp):
                for w in w_in:
                    sp.wait_ge(w, 32 * (E // 2 + TURNS))
                sp.dma_start(acc_d.rearrange("b p n -> p b n"), acc[:]).then_inc(stored, 16)
                sp.wait_ge(stored, 16)


_NAMES = ["x", "ctx_1024", "L0_xattn_e_w1", "L0_xattn_e_w2", "L0_xattn_e_b2", "L0_xattn_router_b"]


def kernel(**inputs):
    import numpy as _np
    import concourse.bacc as _bacc
    from concourse.bass_utils import run_bass_kernel_spmd as _run

    given = {n: _np.asarray(a) for n, a in inputs.items()}
    arrays = {n: given[n] for n in _NAMES}
    arrays["ctxT"] = given["ctx_1024"].transpose(0, 2, 1)
    arrays["e_b1T"] = given["L0_xattn_e_b1"].reshape(E, FT, 128).transpose(0, 2, 1)
    for name, (_, _, turned) in WEIGHTS.items():
        arrays[name] = given[name].T if turned else given[name]
    bf16 = mybir.dt.np(BF16)
    arrays["ident"] = _np.eye(128, dtype=_np.float32)
    arrays["ident16"] = _np.eye(128).astype(bf16)
    arrays["identh"] = _np.eye(128, dtype=_np.float16)
    arrays["causal16"] = _np.tile(_np.where(_np.tri(T) > 0, 0.0, -1e30), (1, 4)).astype(bf16)
    arrays["iota"] = _np.tile(_np.arange(E, dtype=_np.float32), (T, 1))
    masks = (_np.arange(128)[:, None] // HD == _np.arange(8)).astype(_np.float32)
    parts = []
    for name, (_, n) in COLS.items():
        if name == "head_masks":
            parts.append(masks)
        elif name == "head_masks_scaled":
            parts.append((masks * HD ** -0.5).astype(_np.float32))
        elif n == 1:
            parts.append(_np.broadcast_to(given[name].reshape(1, 1), (128, 1)))
        else:
            parts.append(given[name].reshape(n, 128).T)
    arrays["cols"] = _np.concatenate(parts, axis=1)
    arrays["rows"] = _np.stack([given[name] for name in ROWS])

    nc = _bacc.Bacc("TRN2", target_bir_lowering=False, num_devices=1)
    feed, aps = {}, {}
    for name, a in arrays.items():
        a = _np.ascontiguousarray(a)
        feed[f"in_{name}_dram"] = a
        aps[name] = nc.dram_tensor(f"in_{name}_dram", a.shape, mybir.dt.from_np(a.dtype), kind="ExternalInput").ap()
    out = nc.dram_tensor("out_dram", (B, T, D), F32, kind="ExternalOutput").ap()
    network(nc, aps, out)
    return _run(nc, [feed], core_ids=[0]).results[0]["out_dram"]
```
